# Optimizing a Trainium2 kernel written in Bass

```python
import numpy as np
import jax
import jax.numpy as jnp

def _softmax(x, axis=-1):
    return jax.nn.softmax(x, axis=axis)

def _gelu(x):
    return jax.nn.gelu(x, approximate=True)

def _silu(x):
    return jax.nn.silu(x)

def _sigmoid(x):
    return jax.nn.sigmoid(x)

def _layernorm(x, axis=-1, eps=1e-05):
    m = jnp.mean(x, axis=axis, keepdims=True)
    v = jnp.var(x, axis=axis, keepdims=True)
    return (x - m) / jnp.sqrt(v + eps)

def _scatter_add(tgt, idx, src, axis=0):
    return tgt.at[idx].add(src)

def _segment_sum(src, seg, n):
    return jax.ops.segment_sum(src, seg, n)
kernel_name = 'mk_seq_preln_d1_jaxref_r4_5c19c4'

def setup_inputs(seed: int=0):
    np.random.seed(seed)
    _w = jnp.asarray

    def _L0_attn_setup():
        import jax, jax.numpy as jnp
        import numpy as np
        EPS = 1e-06
        CAP = 15.0
        NH = 8

        def soft_cap(x, cap=CAP):
            return cap * jnp.tanh(x / cap)

        def _mlstm_scan(q, k, v, i_pre, f_pre):
            B, S, nh, DQ = q.shape
            DV = v.shape[-1]
            scale = DQ ** (-0.5)

            def step(carry, xs):
                C, n, m = carry
                q_t, k_t, v_t, i_t, f_t = xs
                f_log = jax.nn.log_sigmoid(f_t)
                m_new = jnp.maximum(f_log + m, i_t)
                F = jnp.exp(f_log + m - m_new)
                I = jnp.exp(i_t - m_new)
                C_new = F[..., None, None] * C + (I[..., None] * k_t)[..., :, None] * v_t[..., None, :]
                n_new = F[..., None] * n + I[..., None] * k_t
                qs = q_t * scale
                h_num = jnp.einsum('bhd,bhdv->bhv', qs, C_new)
                qn = jnp.einsum('bhd,bhd->bh', qs, n_new)
                denom = jnp.maximum(jnp.abs(qn), jnp.exp(-m_new)) + EPS
                h = h_num / denom[..., None]
                return ((C_new, n_new, m_new), h)
            C0 = jnp.zeros((B, nh, DQ, DV), q.dtype)
            n0 = jnp.zeros((B, nh, DQ), q.dtype)
            m0 = jnp.zeros((B, nh), q.dtype)
            to_s = lambda a: jnp.moveaxis(a, 1, 0)
            (Cf, nf, mf), hs = jax.lax.scan(step, (C0, n0, m0), (to_s(q), to_s(k), to_s(v), to_s(i_pre), to_s(f_pre)))
            return (jnp.moveaxis(hs, 0, 1), (Cf, nf, mf))

        def _multihead_norm(h, gamma):
            h32 = h.astype(jnp.float32)
            mu = jnp.mean(h32, axis=-1, keepdims=True)
            var = jnp.mean((h32 - mu) ** 2, axis=-1, keepdims=True)
            hn = (h32 - mu) * jax.lax.rsqrt(var + EPS)
            return (hn * gamma).astype(h.dtype)

        def _reference_tuple_inner(x, Wq, Wk, Wv, Wog, Wig, big, Wfg, bfg, gamma, Wout):
            B, S, D = x.shape
            q = x @ Wq.T
            k = x @ Wk.T
            v = x @ Wv.T
            o_preact = x @ Wog.T
            i_pre = soft_cap(x @ Wig.T + big)
            f_pre = soft_cap(x @ Wfg.T + bfg)
            q = q.reshape(B, S, NH, -1)
            k = k.reshape(B, S, NH, -1)
            v = v.reshape(B, S, NH, -1)
            h, state = _mlstm_scan(q, k, v, i_pre, f_pre)
            h_norm = _multihead_norm(h, gamma).reshape(B, S, -1)
            h_out = jax.nn.sigmoid(o_preact) * h_norm
            y = h_out @ Wout.T
            return (y, *state)
        key = jax.random.key(seed)
        ks = jax.random.split(key, 12)
        B, S, D = (2, 512, 512)
        QK, V = (D // 2, D)
        DHV = V // NH
        s = lambda fan_in: 1.0 / np.sqrt(fan_in)
        return {'x': jax.random.normal(ks[0], (B, S, D), jnp.float32), 'Wq': jax.random.normal(ks[1], (QK, D), jnp.float32) * s(D), 'Wk': jax.random.normal(ks[2], (QK, D), jnp.float32) * s(D), 'Wv': jax.random.normal(ks[3], (V, D), jnp.float32) * s(D), 'Wog': jax.random.normal(ks[4], (V, D), jnp.float32) * s(D), 'Wig': jax.random.normal(ks[5], (NH, D), jnp.float32) * s(D), 'big': jax.random.normal(ks[6], (NH,), jnp.float32) * 0.1, 'Wfg': jax.random.normal(ks[7], (NH, D), jnp.float32) * s(D), 'bfg': jax.random.normal(ks[8], (NH,), jnp.float32) * 0.1 + 3.0, 'gamma': jnp.ones((NH, DHV), jnp.float32), 'Wout': jax.random.normal(ks[9], (D, V), jnp.float32) * s(V)}
    _L0_attn_in = _L0_attn_setup()

    def _L0_ffn_setup():
        import jax, jax.numpy as jnp
        import numpy as np
        D_MODEL = 512
        D_FF = 2048

        def absmean_quant(w):
            scale = jnp.mean(jnp.abs(w))
            mask = (jnp.abs(w) >= scale * 0.7).astype(w.dtype)
            return jnp.sign(w) * mask
        key = jax.random.key(seed)
        k_x, k_w1, k_w2 = jax.random.split(key, 3)
        x = jax.random.normal(k_x, (4, 1024, D_MODEL), dtype=jnp.float32)
        w1 = jax.random.normal(k_w1, (D_FF, D_MODEL), dtype=jnp.float32)
        b1 = jnp.zeros((D_FF,), dtype=jnp.float32)
        w2 = jax.random.normal(k_w2, (D_MODEL, D_FF), dtype=jnp.float32)
        b2 = jnp.zeros((D_MODEL,), dtype=jnp.float32)
        return {'x': x, 'w1': w1, 'b1': b1, 'w2': w2, 'b2': b2}
    _L0_ffn_in = _L0_ffn_setup()
    _d = {'L0_attn_x': _L0_attn_in['x'], 'L0_attn_Wq': _L0_attn_in['Wq'], 'L0_attn_Wk': _L0_attn_in['Wk'], 'L0_attn_Wv': _L0_attn_in['Wv'], 'L0_attn_Wog': _L0_attn_in['Wog'], 'L0_attn_Wig': _L0_attn_in['Wig'], 'L0_attn_big': _L0_attn_in['big'], 'L0_attn_Wfg': _L0_attn_in['Wfg'], 'L0_attn_bfg': _L0_attn_in['bfg'], 'L0_attn_gamma': _L0_attn_in['gamma'], 'L0_attn_Wout': _L0_attn_in['Wout'], 'L0_ffn_w1': _L0_ffn_in['w1'], 'L0_ffn_b1': _L0_ffn_in['b1'], 'L0_ffn_w2': _L0_ffn_in['w2'], 'L0_ffn_b2': _L0_ffn_in['b2']}
    _x0 = _d['L0_attn_x']
    _d['L0_attn_x'] = jax.random.normal(jax.random.fold_in(jax.random.key(seed), 1), (16, 512, 512), dtype=_x0.dtype)
    del _x0
    return _d

def reference(L0_attn_x, L0_attn_Wq, L0_attn_Wk, L0_attn_Wv, L0_attn_Wog, L0_attn_Wig, L0_attn_big, L0_attn_Wfg, L0_attn_bfg, L0_attn_gamma, L0_attn_Wout, L0_ffn_w1, L0_ffn_b1, L0_ffn_w2, L0_ffn_b2):

    def _L0_attn_ref(x, Wq, Wk, Wv, Wog, Wig, big, Wfg, bfg, gamma, Wout):
        import jax, jax.numpy as jnp
        import numpy as np
        EPS = 1e-06
        CAP = 15.0
        NH = 8

        def soft_cap(x, cap=CAP):
            return cap * jnp.tanh(x / cap)

        def _mlstm_scan(q, k, v, i_pre, f_pre):
            B, S, nh, DQ = q.shape
            DV = v.shape[-1]
            scale = DQ ** (-0.5)

            def step(carry, xs):
                C, n, m = carry
                q_t, k_t, v_t, i_t, f_t = xs
                f_log = jax.nn.log_sigmoid(f_t)
                m_new = jnp.maximum(f_log + m, i_t)
                F = jnp.exp(f_log + m - m_new)
                I = jnp.exp(i_t - m_new)
                C_new = F[..., None, None] * C + (I[..., None] * k_t)[..., :, None] * v_t[..., None, :]
                n_new = F[..., None] * n + I[..., None] * k_t
                qs = q_t * scale
                h_num = jnp.einsum('bhd,bhdv->bhv', qs, C_new)
                qn = jnp.einsum('bhd,bhd->bh', qs, n_new)
                denom = jnp.maximum(jnp.abs(qn), jnp.exp(-m_new)) + EPS
                h = h_num / denom[..., None]
                return ((C_new, n_new, m_new), h)
            C0 = jnp.zeros((B, nh, DQ, DV), q.dtype)
            n0 = jnp.zeros((B, nh, DQ), q.dtype)
            m0 = jnp.zeros((B, nh), q.dtype)
            to_s = lambda a: jnp.moveaxis(a, 1, 0)
            (Cf, nf, mf), hs = jax.lax.scan(step, (C0, n0, m0), (to_s(q), to_s(k), to_s(v), to_s(i_pre), to_s(f_pre)))
            return (jnp.moveaxis(hs, 0, 1), (Cf, nf, mf))

        def _multihead_norm(h, gamma):
            h32 = h.astype(jnp.float32)
            mu = jnp.mean(h32, axis=-1, keepdims=True)
            var = jnp.mean((h32 - mu) ** 2, axis=-1, keepdims=True)
            hn = (h32 - mu) * jax.lax.rsqrt(var + EPS)
            return (hn * gamma).astype(h.dtype)

        def _reference_tuple_inner(x, Wq, Wk, Wv, Wog, Wig, big, Wfg, bfg, gamma, Wout):
            B, S, D = x.shape
            q = x @ Wq.T
            k = x @ Wk.T
            v = x @ Wv.T
            o_preact = x @ Wog.T
            i_pre = soft_cap(x @ Wig.T + big)
            f_pre = soft_cap(x @ Wfg.T + bfg)
            q = q.reshape(B, S, NH, -1)
            k = k.reshape(B, S, NH, -1)
            v = v.reshape(B, S, NH, -1)
            h, state = _mlstm_scan(q, k, v, i_pre, f_pre)
            h_norm = _multihead_norm(h, gamma).reshape(B, S, -1)
            h_out = jax.nn.sigmoid(o_preact) * h_norm
            y = h_out @ Wout.T
            return (y, *state)
        return _reference_tuple_inner(x, Wq, Wk, Wv, Wog, Wig, big, Wfg, bfg, gamma, Wout)[0]

    def _L0_ffn_ref(x, w1, b1, w2, b2):
        import jax, jax.numpy as jnp
        import numpy as np
        D_MODEL = 512
        D_FF = 2048

        def absmean_quant(w):
            scale = jnp.mean(jnp.abs(w))
            mask = (jnp.abs(w) >= scale * 0.7).astype(w.dtype)
            return jnp.sign(w) * mask
        w1_q = absmean_quant(w1)
        w2_q = absmean_quant(w2)
        h = jnp.einsum('bsd,fd->bsf', x, w1_q) + b1
        h = jax.nn.gelu(h, approximate=False)
        out = jnp.einsum('bsf,df->bsd', h, w2_q) + b2
        return out
    x = L0_attn_x
    x = x + _L0_attn_ref(_layernorm(x, axis=-1), L0_attn_Wq, L0_attn_Wk, L0_attn_Wv, L0_attn_Wog, L0_attn_Wig, L0_attn_big, L0_attn_Wfg, L0_attn_bfg, L0_attn_gamma, L0_attn_Wout)
    x = x + _L0_ffn_ref(_layernorm(x, axis=-1), L0_ffn_w1, L0_ffn_b1, L0_ffn_w2, L0_ffn_b2)
    return x

_drawn_inputs = setup_inputs


def setup_inputs(seed=0):
    import zlib

    import numpy as np

    out = dict(_drawn_inputs(seed))
    spreads = {'L0_attn_gamma': (1.0, 0.2), 'L0_ffn_b1': (0.0, 0.8), 'L0_ffn_b2': (0.0, 2.0)}
    factors = {'L0_attn_big': 64.0}
    for name, (base, spread) in spreads.items():
        noise = np.random.default_rng([zlib.crc32(name.encode()), seed]).standard_normal(out[name].shape)
        drawn = base * np.exp(spread * noise) if base else spread * noise
        out[name] = jnp.asarray(drawn.astype(out[name].dtype))
    for name, factor in factors.items():
        out[name] = (out[name] * factor).astype(out[name].dtype)
    return out
```

```python
from contextlib import ExitStack

import concourse.bass as bass
from concourse import mybir

F32 = mybir.dt.float32
F16 = mybir.dt.float16
I32 = mybir.dt.int32
ALU = mybir.AluOpType
ACT = mybir.ActivationFunctionType
AX = mybir.AxisListType
RMAX = bass.bass_isa.ReduceOp.max
RADD = bass.bass_isa.ReduceOp.add

P = 128
CAP = 15.0
MLSTM_EPS = 1e-6
LN_EPS = 1e-5
MASKED = -30000.0
X_SCALE = 2.0 ** 11
H_SCALE = 2.0 ** 12
TOP = 2.0 ** 14
HI, LO = 0, 1


def at(b, per, k):
    return b * per + k


class Chain:

    def __init__(self, b, per):
        self.b, self.per, self.n = b, per, 0

    def next(self):
        self.n += 1
        assert self.n <= self.per, self.n
        return at(self.b, self.per, self.n)


DVE_L, DVE_A = 3, 6 + 4 * 5 + 4 + 2
POOL_A = 4


def block_program(nc, x, Wq, Wk, Wv, Wog, Wig, big, Wfg, bfg, gamma, Wout, w1, b1, w2, b2, out):
    B, S, D = x.shape
    QK, DV_ALL = Wq.shape[0], Wv.shape[0]
    NH, DHV = gamma.shape
    DQ = QK // NH
    FF = w1.shape[0]
    T = S // P
    KD = D // P
    NF = FF // P
    HG = NH * DQ // P
    H4 = NH // HG
    VA = DHV + 1
    GATE_F = 32
    GROWS = GATE_F + NH
    EM, GS = 32, 64
    STACK = GS + NH
    LATE = S - P
    C_QK, C_V, C_O, C_OUT = 0, D, 2 * D, 3 * D
    W_QK, W_V, W_O, W_OUT, W_GATE, W_GELU = range(6)
    assert (T, KD, HG, QK, DV_ALL) == (4, 4, 2, 256, D)

    U_T1, U_GATE, U_V, U_O, U_Q, U_K, U_KTOK = 0, 4, 5, 9, 13, 15, 17
    U_HT, U_Y = (20, 21, 23, 25), (22, 24, 26, 27)
    PA_USES = 28
    U_T2, U_F1, U_F2 = 0, KD, KD + NF
    PF_USES = KD + NF + T
    U_GT, U_U, U_H = 0, 1, T
    PH_USES = 2 * T

    gate_r = nc.dram_tensor("gate_r", (B, NH, S), F32, kind="Internal").ap()
    gate_w = nc.dram_tensor("gate_w", (B, NH, LATE), F32, kind="Internal").ap()

    with ExitStack() as ctx:
        def sb(name, shape, dt=F32):
            return ctx.enter_context(nc.sbuf_tensor(name, shape, dt))

        def pb(name):
            return ctx.enter_context(nc.psum_tensor(name, [P, 2, 512], F32))

        def sem(name):
            return ctx.enter_context(nc.semaphore(name))

        wT = sb("wT", [P, 2, KD, 4 * D], F16)
        wgT = sb("wgT", [P, 2, KD, GROWS], F16)
        w1T = sb("w1T", [P, KD, FF], F16)
        w2T = sb("w2T", [P, NF, D], F16)
        b1c = sb("b1c", [P, NF])
        b2r = sb("b2r", [P, D])
        gate_bias = sb("gate_bias", [GROWS, 1])
        ident = sb("ident", [P, P])
        ident16 = sb("ident16", [P, P], F16)
        causal = sb("causal", [P, P])
        own_head = sb("own_head", [P, H4 * VA])
        restart = sb("restart", [NH, S])
        half = sb("half", [P, NH])
        amax = sb("amax", [P, 6])
        pow2 = sb("pow2", [P, 6])
        wscale = sb("wscale", [P, 6])
        winv = sb("winv", [P, 6])
        evac = sb("evac", [P, 6])
        asum = sb("asum", [P, 16])
        thr = sb("thr", [P, 4])
        xin = sb("xin", [P, T, D])
        xres = sb("xres", [P, T, D])
        x1b = sb("x1b", [P, T, D])
        xT = sb("xT", [P, 2, KD, S], F16)
        x2T = sb("x2T", [P, 2, KD, S], F16)
        qT = sb("qT", [P, HG, S])
        kT = sb("kT", [P, HG, S])
        qw = sb("qw", [P, HG, LATE])
        fcol = sb("fcol", [P, HG, T - 1])
        vaug = sb("vaug", [P, T, NH, VA])
        sigT = sb("sigT", [P, KD, S])
        dec = sb("dec", [P, NH, S])
        ktok = sb("ktok", [P, T - 1, QK])
        cst = sb("cst", [P, T - 1, HG, H4 * VA])
        g32 = sb("g32", [P, 2, S])
        gT = sb("gT", [P, 2, NF, S], F16)
        stack = sb("stack", [STACK, S])
        gtok = sb("gtok", [P, T, STACK])
        th = sb("th", [GROWS, S])
        ge = sb("ge", [NH, S])
        st1, st2 = sb("st1", [P, T, 6]), sb("st2", [P, T, 6])
        mean1, dif1, dev1, ve1, rstd1 = (sb(n + "1", [P, T]) for n in ("mean", "dif", "dev", "ve", "rstd"))
        mean2, dif2, dev2, ve2, rstd2 = (sb(n + "2", [P, T]) for n in ("mean", "dif", "dev", "ve", "rstd"))
        den, hsum, hvar, hinv = (sb(n, [P, NH]) for n in ("den", "hsum", "hvar", "hinv"))
        gu, gl = g32[0:NH, 0, :], g32[0:NH, 1, :]
        gi, gf = kT[0:NH, 0, :], kT[0:NH, 1, :]
        cent = [kT[:, i, :] for i in range(2)]
        hog = [qT[:, i, :] for i in range(2)]
        square = ktok[:, 0:2, :]
        rows = gT[:, :, :, :].bitcast(F32).rearrange("p a n s -> p (a n s)").rearrange("p (n s) -> p n s", s=D)

        pa, pf, ps, ph = pb("pa"), pb("pf"), pb("ps"), pb("ph")

        s_wload = [sem(f"s_wload{g}") for g in range(5)]
        s_small = sem("s_small")
        s_w12 = [sem("s_w1load"), sem("s_w2load")]
        s_const = sem("s_const")
        s_ident = sem("s_ident")
        s_pchain = sem("s_pchain")
        s_dchain = sem("s_dchain")
        s_amax = sem("s_amax")
        s_allmax = sem("s_allmax")
        s_scales = sem("s_scales")
        s_whi = sem("s_whi")
        s_wfill = sem("s_wfill")
        s_wfree = [sem("s_wfree0"), sem("s_wfree1")]
        s_asum = sem("s_asum")
        s_allsum = sem("s_allsum")
        s_low = sem("s_low")
        s_tern = sem("s_tern")
        s_ufill = sem("s_ufill")
        x_loaded, res_loaded = sem("x_loaded"), sem("res_loaded")
        r_stored, w_stored = sem("r_stored"), sem("w_stored")
        r_loaded = [sem(f"r_loaded{g}") for g in range(HG)]
        w_loaded = sem("w_loaded")
        out_stored = [sem(f"out_stored{t}") for t in range(T)]
        pa_fill, pf_fill, ps_fill, ph_fill = sem("pa_fill"), sem("pf_fill"), sem("ps_fill"), sem("ph_fill")
        pa_free = [sem("pa_free0"), sem("pa_free1")]
        pf_free = [sem("pf_free0"), sem("pf_free1")]
        ps_free = [sem("ps_free0"), sem("ps_free1")]
        ph_free = sem("ph_free")
        dve_l, dve_a, dve_f = sem("dve_l"), sem("dve_a"), sem("dve_f")
        pool_a = sem("pool_a")
        var1, var2 = sem("var1"), sem("var2")
        rstd1_ok, rstd2_ok = sem("rstd1_ok"), sem("rstd2_ok")
        xn_ok, xn2_ok = sem("xn_ok"), sem("xn2_ok")
        x_hi, x2_hi = sem("x_hi"), sem("x2_hi")
        gate_dve, gate_act = sem("gate_dve"), sem("gate_act")
        r_ok = sem("r_ok")
        masked = sem("masked")
        d_ok = sem("d_ok")
        qw_ok, fcol_ok = sem("qw_ok"), sem("fcol_ok")
        c_ok = sem("c_ok")
        sq_ok = sem("sq_ok")
        hvar_ok = sem("hvar_ok")
        hn_ok = sem("hn_ok")
        ho_hi, ho_lo = sem("ho_hi"), sem("ho_lo")
        x1b_ok = sem("x1b_ok")
        gs_ok = sem("gs_ok")

        PF = PF_USES // 2
        PF_SETUP = 16

        def pa_done(b, use):
            return at(b, PA_USES // 2, use // 2 + 1)

        def pf_done(fb, use):
            return at(fb, PF, PF_SETUP + use // 2 + 1)

        def tok(t):
            return slice(t * P, (t + 1) * P)

        def per_head(ap, n):
            return ap.rearrange("p (a h) -> p a h", h=H4).unsqueeze(3).to_broadcast([P, HG, H4, n])

        def heads(j):
            return ph[:, :, 0:H4 * VA].rearrange("p a (h v) -> p a h v", v=VA)[:, :, :, 0:DHV]

        def by_head(ap):
            return ap.rearrange("p (a h v) -> p a h v", a=HG, h=H4)

        block = ctx.enter_context(nc.Block())

        @block.sync
        def _(sp):
            for g, parts in enumerate(((Wq, Wk), (Wv,), (Wog,), (Wout,))):
                n = 4 * g
                for w in parts:
                    k = w.shape[0] // P
                    sp.dma_start(rows[:, n:n + k, :], w.rearrange("(n p) d -> p n d", p=P)).then_inc(s_wload[g], 16)
                    n += k
                if g == 0:
                    sp.dma_start(xin[:, :, :], x[0].rearrange("(t p) d -> p t d", p=P)).then_inc(x_loaded, 16)
                    sp.wait_ge(s_const, 1)
                    sp.dma_start(th[0:NH, :], Wig).then_inc(s_wload[4], 16)
                    sp.dma_start(th[GATE_F:GROWS, :], Wfg).then_inc(s_wload[4], 16)
                    sp.dma_start(gate_bias[0:NH, :], big.unsqueeze(1)).then_inc(s_small, 16)
                    sp.dma_start(gate_bias[GATE_F:GROWS, :], bfg.unsqueeze(1)).then_inc(s_small, 16)
                    sp.dma_start(g32[:, 0, :], gamma.rearrange("h v -> (h v)").partition_broadcast(P)).then_inc(s_small, 16)
                    sp.dma_start(b2r[:, :], b2.partition_broadcast(P)).then_inc(s_small, 16)
                    sp.dma_start(b1c[:, :], b1.rearrange("(n p) -> p n", p=P),
                                 allow_slow_non_contiguous=True).then_inc(s_small, 16)

            def stage_a(b):
                if isinstance(b, int) and b == 0:
                    pass
                else:
                    sp.wait_ge(pf_fill, at(b - 1, PF_USES, U_T2 + KD))
                sp.dma_start(xres[:, :, :], x[b].rearrange("(t p) d -> p t d", p=P)).then_inc(res_loaded, 16)

            def gate_rows(b):
                sp.wait_ge(r_ok, at(b, 1, 1))
                sp.dma_start(gate_r[b], th[0:NH, :]).then_inc(r_stored, 16)
                sp.wait_ge(gate_act, at(b, 5, 4))
                sp.dma_start(gate_w[b], ge[:, 0:LATE]).then_inc(w_stored, 16)
                if not (isinstance(b, int) and b == 0):
                    sp.wait_ge(ph_fill, at(b, PH_USES, 0))
                sp.wait_ge(r_stored, at(b, 16, 16))
                for g in range(HG):
                    sp.dma_start(dec[:, g * H4:(g + 1) * H4, :],
                                 gate_r[b, g * H4:(g + 1) * H4, :].rearrange("h s -> (h s)").partition_broadcast(P)
                                 .rearrange("p (h s) -> p h s", s=S)).then_inc(r_loaded[g], 16)
                sp.wait_ge(w_stored, at(b, 16, 16))
                for h in range(H4):
                    for g in range(HG):
                        sp.dma_start(qw[h * DQ:(h + 1) * DQ, g, :],
                                     gate_w[b, g * H4 + h, :].partition_broadcast(DQ)).then_inc(w_loaded, 16)

            def next_x(b):
                sp.wait_ge(pa_fill, at(b, PA_USES, U_T1 + KD))
                sp.dma_start(xin[:, :, :], x[b + 1].rearrange("(t p) d -> p t d", p=P)).then_inc(x_loaded, 16)

            def store(fb):
                for t in range(T):
                    use = U_F2 + t
                    sp.wait_ge(pf_free[use % 2], pf_done(fb, use))
                    sp.dma_start(out[fb, tok(t), :], x1b[:, t, :]).then_inc(out_stored[t], 16)

            stage_a(0)
            gate_rows(0)
            wv = [w1.rearrange("(n p) d -> p n d", p=P), w2.rearrange("(n p) (c d) -> p n c d", p=P, d=D)]
            sp.wait_ge(s_wfree[0], 9)
            sp.wait_ge(s_wfree[1], 8)
            for n in range(4):
                sp.dma_start(rows[:, 4 * n:4 * n + 4, :], wv[0][:, 4 * n:4 * n + 4, :]).then_inc(s_w12[0], 16)
            next_x(0)
            sp.wait_ge(s_tern, 16)
            for n in range(4):
                sp.dma_start(rows[:, 4 * n:4 * n + 4, :], wv[1][:, n, :, :]).then_inc(s_w12[1], 16)
            with sp.Fori(1, B - 1) as b:
                next_x(b)
                gate_rows(b)
                stage_a(b)
                store(b - 1)
            gate_rows(B - 1)
            stage_a(B - 1)
            store(B - 2)
            store(B - 1)
            for t in range(T):
                sp.wait_ge(out_stored[t], 16 * B)

        @block.gpsimd
        def _(pool):
            nc.gpsimd.memset(gate_bias[:, :], 0.0)
            nc.gpsimd.memset(th[:, :], 0.0).then_inc(s_const, 1)
            nc.gpsimd.memset(ident[:, :], 0.0)
            nc.gpsimd.memset(causal[:, :], 0.0)
            nc.gpsimd.memset(own_head[:, :], 1.0)
            nc.gpsimd.memset(restart[:, :], 1.0)
            nc.gpsimd.memset(stack[:, :], 0.0)
            nc.gpsimd.memset(amax[:, :], 0.0)
            nc.gpsimd.memset(half[:, :], -0.5)
            nc.gpsimd.memset(vaug[:, :, :, DHV:VA], 1.0).then_inc(s_pchain, 1)
            pool.wait_ge(s_pchain, 1)
            nc.gpsimd.affine_select(out=ident[:, :], in_=ident[:, :], compare_op=ALU.not_equal, fill=1.0,
                                    base=0, pattern=[[-1, P]], channel_multiplier=1)
            nc.gpsimd.affine_select(out=causal[:, :], in_=causal[:, :], compare_op=ALU.is_ge, fill=MASKED,
                                    base=0, pattern=[[1, P]], channel_multiplier=-1)
            nc.gpsimd.affine_select(out=restart[:, :], in_=restart[:, :], compare_op=ALU.not_equal, fill=0.0,
                                    base=0, pattern=[[0, T], [1, P]], channel_multiplier=0)
            nc.gpsimd.affine_select(out=own_head[:, :], in_=own_head[:, :], compare_op=ALU.is_ge, fill=0.0,
                                    base=0, pattern=[[-DQ, H4], [0, VA]], channel_multiplier=1).then_inc(s_pchain, 1)
            pool.wait_ge(s_pchain, 2)
            nc.gpsimd.affine_select(out=own_head[:, :], in_=own_head[:, :], compare_op=ALU.is_ge, fill=0.0,
                                    base=DQ - 1, pattern=[[DQ, H4], [0, VA]], channel_multiplier=-1)
            nc.gpsimd.tensor_copy(ident16[:, :], ident[:, :]).then_inc(s_ident, 1)
            pool.wait_ge(s_amax, 1)
            nc.gpsimd.partition_all_reduce(pow2[:, :], amax[:, :], P, RMAX).then_inc(s_allmax, 1)

            def layer_norm(b):
                pool.wait_ge(var1, at(b, 1, 1))
                nc.gpsimd.tensor_tensor(rstd1[:, :], ve1[:, :], half[:, 0:T], ALU.pow).then_inc(rstd1_ok, 1)

            def decay(b):
                for n in range(NH // 2):
                    if n % 2 == 0:
                        pool.wait_ge(r_loaded[n // 2], at(b, 16, 16))
                    rows_of = dec[:, 2 * n:2 * n + 2, :].rearrange("p h (t s) -> p (h t) s", s=P)
                    nc.gpsimd.tensor_tensor(rows_of, rows_of,
                                            causal[:, :].unsqueeze(1).to_broadcast([P, 2 * T, P]),
                                            ALU.add).then_inc(masked, 1)
                pool.wait_ge(fcol_ok, at(b, 1, 1))
                pool.wait_ge(pa_free[(U_Q + 1) % 2], pa_done(b, U_Q + 1))
                pool.wait_ge(pa_free[U_Q % 2], pa_done(b, U_Q))
                nc.gpsimd.tensor_tensor(qw[:, :, :], qw[:, :, :], qT[:, :, P:S], ALU.mult).then_inc(qw_ok, 1)

            def head_norm(b, j):
                pool.wait_ge(hvar_ok, at(b, T, j + 1))
                nc.gpsimd.tensor_tensor(hinv[:, :], hvar[:, :], half[:, :], ALU.pow).then_inc(pool_a, 1)
                pool.wait_ge(pool_a, at(b, POOL_A, j + 1))
                hc = by_head(cent[j % 2])
                nc.gpsimd.tensor_tensor(hc, hc, per_head(hinv[:, :], DHV), ALU.mult).then_inc(hn_ok, 1)

            def gated_lo(b, j):
                pool.wait_ge(ho_hi, at(b, T, j + 1))
                nc.gpsimd.tensor_tensor(xT[:, LO, :, tok(j)], hog[j % 2].rearrange("p (k s) -> p k s", s=P),
                                        xT[:, HI, :, tok(j)], ALU.subtract).then_inc(ho_lo, 1)

            def residual_bias(b, t):
                use = U_Y[t]
                pool.wait_ge(pa_free[use % 2], pa_done(b, use))
                if not (isinstance(b, int) and b == 0):
                    pool.wait_ge(out_stored[t], at(b, 16, 0))
                nc.gpsimd.tensor_tensor(x1b[:, t, :], xres[:, t, :], b2r[:, :], ALU.add).then_inc(x1b_ok, 1)

            def layer_norm2(b):
                pool.wait_ge(var2, at(b, 1, 1))
                nc.gpsimd.tensor_tensor(rstd2[:, :], ve2[:, :], half[:, 0:T], ALU.pow).then_inc(rstd2_ok, 1)

            def sequence(b, ahead):
                decay(b)
                if ahead:
                    layer_norm(b + 1)
                head_norm(b, 0)
                head_norm(b, 1)
                gated_lo(b, 0)
                head_norm(b, 2)
                gated_lo(b, 1)
                head_norm(b, 3)
                residual_bias(b, 0)
                gated_lo(b, 2)
                residual_bias(b, 1)
                gated_lo(b, 3)
                residual_bias(b, 2)
                residual_bias(b, 3)
                layer_norm2(b)

            pool.wait_ge(s_small, 80)
            layer_norm(0)
            sequence(0, True)
            for n in range(2):
                pool.wait_ge(s_asum, n + 1)
                nc.gpsimd.partition_all_reduce(thr[:, 1:2], thr[:, 0:1], P, RADD).then_inc(s_allsum, 1)
            with pool.Fori(1, B - 1) as b:
                sequence(b, True)
            sequence(B - 1, False)

        @block.scalar
        def _(act):
            act.wait_ge(s_scales, 1)
            for n in range(17):
                g, k = divmod(n, KD)
                act.wait_ge(s_wfill, n + 1)
                if g < 4:
                    nc.scalar.activation(wT[:, HI, k, g * D:(g + 1) * D], pa[:, n % 2, :], ACT.Copy,
                                         scale=wscale[:, g:g + 1]).then_inc(s_whi, 1)
                else:
                    nc.scalar.activation(wgT[:, HI, :, :], pa[:, n % 2, 0:KD * GROWS].rearrange("p (k r) -> p k r", r=GROWS),
                                         ACT.Copy, scale=wscale[:, W_GATE:W_GATE + 1]).then_inc(s_whi, 1)

            def ternary_out(w):
                with act.Fori(0, 8) as i:
                    for p in range(2):
                        u = i * 2 + p
                        act.wait_ge(s_ufill, i * 2 + (16 * w + p + 1))
                        src = pf[:, p, 0:D // 2].bitcast(F16).rearrange("p (k c) -> p k c", c=P)
                        if w == 0:
                            dst = w1T[:, :, bass.ds(u * P, P)]
                        else:
                            dst = w2T[:, bass.ds((i * 2 + p) % 4 * 4, 4), bass.ds((i * 2 + p) // 4 * P, P)]
                        nc.scalar.activation(dst, src, ACT.Copy).then_inc(pf_free[p], 1)

            def split_hi(b):
                for k in range(KD):
                    act.wait_ge(pa_fill, at(b, PA_USES, U_T1 + k + 1))
                    nc.scalar.activation(xT[:, HI, k, :], pa[:, (U_T1 + k) % 2, :], ACT.Copy,
                                         scale=X_SCALE).then_inc(x_hi, 1)

            def gates(b):
                act.wait_ge(pa_fill, at(b, PA_USES, U_GATE + 1))
                nc.scalar.activation(th[:, :], pa[0:GROWS, U_GATE % 2, :], ACT.Tanh, bias=gate_bias[:, 0:1],
                                     scale=evac[0:GROWS, W_GATE:W_GATE + 1]).then_inc(pa_free[U_GATE % 2], 1)
                act.wait_ge(gate_dve, at(b, 4, 1))
                nc.scalar.activation(ge[:, :], ge[:, :], ACT.Exp).then_inc(gate_act, 1)
                act.wait_ge(gate_dve, at(b, 4, 2))
                nc.scalar.activation(gl, gu, ACT.Ln).then_inc(gate_act, 1)
                act.wait_ge(gate_dve, at(b, 4, 3))
                nc.scalar.activation(stack[EM:EM + NH, :], gu, ACT.Exp, scale=-1.0).then_inc(gate_act, 1)
                act.wait_ge(gate_dve, at(b, 4, 4))
                nc.scalar.activation(ge[:, 0:LATE], ge[:, 0:LATE], ACT.Exp).then_inc(gate_act, 1)
                nc.scalar.activation(stack[GS:GS + NH, 0:LATE], gf[:, 0:LATE], ACT.Exp).then_inc(gate_act, 1)

            def output_gate(b):
                for n in range(KD):
                    use = U_O + n
                    act.wait_ge(pa_fill, at(b, PA_USES, use + 1))
                    nc.scalar.activation(sigT[:, n, :], pa[:, use % 2, :], ACT.Sigmoid,
                                         scale=evac[:, W_O:W_O + 1]).then_inc(pa_free[use % 2], 1)

            def gate_columns(b):
                act.wait_ge(ph_fill, at(b, PH_USES, U_GT + 1))
                nc.scalar.activation(gtok[:, :, :], ph[:, 0, 0:T * STACK].rearrange("p (t g) -> p t g", g=STACK),
                                     ACT.Copy).then_inc(ph_free, 1)

            def queries_keys(b):
                for n in range(2 * HG):
                    use = U_Q + n
                    act.wait_ge(pa_fill, at(b, PA_USES, use + 1))
                    if n < HG:
                        nc.scalar.activation(qT[:, n, :], pa[:, use % 2, :], ACT.Copy,
                                             scale=evac[:, W_GELU:W_GELU + 1]).then_inc(pa_free[use % 2], 1)
                    else:
                        nc.scalar.activation(kT[:, n - HG, :], pa[:, use % 2, :], ACT.Copy,
                                             scale=evac[:, W_QK:W_QK + 1]).then_inc(pa_free[use % 2], 1)

            def decay(b):
                act.wait_ge(ph_free, at(b, PH_USES, U_GT + 1))
                for h in range(NH):
                    if h % 2 == 0:
                        act.wait_ge(masked, at(b, NH // 2, h // 2 + 1))
                    for j in range(T):
                        last = nc.scalar.activation(dec[:, h, tok(j)], dec[:, h, tok(j)], ACT.Exp,
                                                    bias=gtok[:, j, h:h + 1])
                    last.then_inc(d_ok, 1)

            def split2_hi(fb):
                for k in range(KD):
                    act.wait_ge(pf_fill, at(fb, PF_USES, U_T2 + k + 1))
                    nc.scalar.activation(x2T[:, HI, k, :], pf[:, (U_T2 + k) % 2, :], ACT.Copy,
                                         scale=X_SCALE).then_inc(x2_hi, 1)

            def gelu(fb, f):
                use = U_F1 + f
                act.wait_ge(pf_fill, at(fb, PF_USES, use + 1))
                if f >= 2:
                    act.wait_ge(gs_ok, at(fb, NF, f - 1))
                if f == 0:
                    act.wait_ge(gate_act, at(fb, 5, 5))
                nc.scalar.activation(g32[:, f % 2, :], pf[:, use % 2, :], ACT.Gelu, bias=b1c[:, f:f + 1],
                                     scale=1.0 / X_SCALE).then_inc(pf_free[use % 2], 1)

            def squares(b, j):
                act.wait_ge(ph_free, at(b, PH_USES, U_H + j + 1))
                nc.scalar.activation(square, cent[j % 2].rearrange("p (a s) -> p a s", a=2), ACT.Square).then_inc(sq_ok, 1)

            def gated_hi(b, j):
                use = U_HT[j]
                act.wait_ge(pa_free[use % 2], pa_done(b, use))
                nc.scalar.activation(xT[:, HI, :, tok(j)], hog[j % 2].rearrange("p (k s) -> p k s", s=P),
                                     ACT.Copy).then_inc(ho_hi, 1)

            def sequence(b, fb):
                split_hi(b)
                gates(b)
                output_gate(b)
                gate_columns(b)
                if fb is not None:
                    split2_hi(fb)
                queries_keys(b)
                decay(b)
                if fb is not None:
                    for f in range(NF):
                        gelu(fb, f)
                squares(b, 0)
                squares(b, 1)
                gated_hi(b, 0)
                squares(b, 2)
                gated_hi(b, 1)
                squares(b, 3)
                gated_hi(b, 2)
                gated_hi(b, 3)

            sequence(0, None)
            ternary_out(0)
            ternary_out(1)
            with act.Fori(1, B - 1) as b:
                sequence(b, b - 1)
            sequence(B - 1, B - 2)
            split2_hi(B - 1)
            act.wait_ge(gs_ok, at(B - 1, NF, 0))
            for f in range(NF):
                gelu(B - 1, f)

        @block.vector
        def _(dve):
            for g in (W_QK, W_V, W_O, W_OUT):
                dve.wait_ge(s_wload[g], 32 if g == W_QK else 16)
                if g == W_OUT:
                    dve.wait_ge(s_small, 80)
                    dve.wait_ge(s_const, 1)
                    wo = rows[:, 4 * g:4 * g + 4, :]
                    nc.vector.tensor_tensor(wo, wo, g32[:, 0, :].unsqueeze(1).to_broadcast([P, 4, D]),
                                            ALU.mult).then_inc(s_dchain, 1)
                    dve.wait_ge(s_dchain, 1)
                if g == W_QK:
                    dve.wait_ge(s_ident, 1)
                nc.vector.tensor_reduce(amax[:, g:g + 1], rows[:, 4 * g:4 * g + 4, :], AX.XY, ALU.max,
                                        apply_absolute_value=True)
            dve.wait_ge(s_wload[4], 32)
            nc.vector.tensor_reduce(amax[0:GROWS, W_GATE:W_GATE + 1], th[:, :], AX.X, ALU.max, apply_absolute_value=True)
            nc.vector.tensor_scalar(gate_bias[:, :], gate_bias[:, :], 1.0 / CAP, None, ALU.mult)
            nc.vector.tensor_reduce(amax[:, W_GELU:W_GELU + 1], b1c[:, :], AX.X, ALU.max,
                                    apply_absolute_value=True).then_inc(s_amax, 1)
            dve.wait_ge(s_allmax, 1)
            nc.vector.tensor_scalar(pow2[:, W_GELU:W_GELU + 1], pow2[:, W_GELU:W_GELU + 1], float(D), None,
                                    ALU.add).then_inc(s_dchain, 1)
            dve.wait_ge(s_dchain, 2)
            bits = pow2[:, :].bitcast(I32)
            nc.vector.tensor_scalar(bits, bits, 0x7F800000, None, ALU.bitwise_and).then_inc(s_dchain, 1)
            dve.wait_ge(s_dchain, 3)
            nc.vector.tensor_scalar(pow2[:, :], pow2[:, :], 2.0 ** -100, 1.0 / TOP, ALU.max, ALU.mult).then_inc(s_dchain, 1)
            dve.wait_ge(s_dchain, 4)
            nc.vector.reciprocal(wscale[:, :], pow2[:, :])
            nc.vector.tensor_copy(winv[:, :], pow2[:, :])
            for g, c in ((W_QK, 1.0 / X_SCALE), (W_V, 1.0 / X_SCALE), (W_O, 1.0 / X_SCALE), (W_OUT, 1.0 / H_SCALE),
                         (W_GATE, 1.0 / (X_SCALE * CAP))):
                nc.vector.tensor_scalar(evac[:, g:g + 1], pow2[:, g:g + 1], c, None, ALU.mult)
            nc.vector.tensor_scalar(evac[:, W_GELU:W_GELU + 1], pow2[:, W_QK:W_QK + 1], DQ ** -0.5 / X_SCALE, None,
                                    ALU.mult).then_inc(s_scales, 1)
            dve.wait_ge(s_scales, 1)
            for n in range(17):
                g, k = divmod(n, KD)
                dve.wait_ge(s_whi, n + 1)
                if g < 4:
                    hi, lo = (wT[:, part, k, g * D:(g + 1) * D] for part in (HI, LO))
                    src = pa[:, n % 2, :]
                else:
                    hi, lo = (wgT[:, part, :, :] for part in (HI, LO))
                    src = pa[:, n % 2, 0:KD * GROWS].rearrange("p (k r) -> p k r", r=GROWS)
                nc.vector.scalar_tensor_tensor(lo, src, wscale[:, g:g + 1], hi, ALU.mult,
                                               ALU.subtract).then_inc(s_wfree[n % 2], 1)

            def ternary(w):
                dve.wait_ge(s_w12[w], 64)
                base = 4 + 3 * w
                nc.vector.tensor_reduce(asum[:, :], rows, AX.X, ALU.add, apply_absolute_value=True).then_inc(s_dchain, 1)
                dve.wait_ge(s_dchain, base + 1)
                nc.vector.tensor_reduce(thr[:, 0:1], asum[:, :], AX.X, ALU.add).then_inc(s_asum, 1)
                dve.wait_ge(s_allsum, w + 1)
                nc.vector.tensor_scalar(thr[:, 2:3], thr[:, 1:2], 1.0 / (FF * D), 0.7, ALU.mult, ALU.mult).then_inc(s_dchain, 1)
                dve.wait_ge(s_dchain, base + 2)
                nc.vector.tensor_scalar(thr[:, 3:4], thr[:, 2:3], -1.0, None, ALU.mult).then_inc(s_dchain, 1)
                dve.wait_ge(s_dchain, base + 3)
                with dve.Fori(0, 8) as i:
                    for p in range(2):
                        u = i * 2 + p
                        unit = rows[:, bass.ds(u, 1), :].rearrange("p a d -> p (a d)")
                        tern, low = x2T[:, HI, p, :], x2T[:, LO, p, :]
                        nc.vector.tensor_scalar(low, unit, thr[:, 3:4], None, ALU.is_le).then_inc(s_low, 1)
                        dve.wait_ge(s_low, i * 2 + (16 * w + p + 1))
                        nc.vector.scalar_tensor_tensor(tern, unit, thr[:, 2:3], low, ALU.is_ge,
                                                       ALU.subtract).then_inc(s_tern, 1)
                    dve.wait_ge(s_ufill, i * 2 + (16 * w + 2))

            def mean_var(st, mean, dif, dev, order, ch):
                nc.vector.tensor_tensor(mean[:, :], st[:, :, 1], st[:, :, 4], ALU.add)
                nc.vector.tensor_tensor(dif[:, :], st[:, :, 1], st[:, :, 4], ALU.subtract)
                nc.vector.tensor_tensor(dev[:, :], st[:, :, 2], st[:, :, 5], ALU.add).then_inc(order, 1)
                dve.wait_ge(order, ch.next())
                nc.vector.tensor_scalar(mean[:, :], mean[:, :], 0.5, None, ALU.mult)
                nc.vector.scalar_tensor_tensor(dif[:, :], dif[:, :], 0.25, dif[:, :], ALU.mult, ALU.mult)
                nc.vector.tensor_scalar(dev[:, :], dev[:, :], 1.0 / D, LN_EPS, ALU.mult, ALU.add).then_inc(order, 1)
                dve.wait_ge(order, ch.next())

            def norm_stats(b):
                ch = Chain(b, DVE_L)
                dve.wait_ge(x_loaded, at(b, 16, 16))
                for t in range(T):
                    last = nc.vector.bn_stats(st1[:, t, :], xin[:, t, :])
                last.then_inc(dve_l, 1)
                dve.wait_ge(dve_l, ch.next())
                mean_var(st1, mean1, dif1, dev1, dve_l, ch)
                nc.vector.tensor_tensor(ve1[:, :], dif1[:, :], dev1[:, :], ALU.add).then_inc(var1, 1)

            def norm_apply(b):
                dve.wait_ge(rstd1_ok, at(b, 1, 1))
                for t in range(T):
                    nc.vector.tensor_scalar(xin[:, t, :], xin[:, t, :], mean1[:, t:t + 1], rstd1[:, t:t + 1],
                                            ALU.subtract, ALU.mult).then_inc(xn_ok, 1)

            def split_lo(b):
                for k in range(KD):
                    use = U_T1 + k
                    dve.wait_ge(x_hi, at(b, KD, k + 1))
                    nc.vector.scalar_tensor_tensor(xT[:, LO, k, :], pa[:, use % 2, :], X_SCALE, xT[:, HI, k, :],
                                                   ALU.mult, ALU.subtract).then_inc(pa_free[use % 2], 1)

            def gate_decay(b, ch, between):
                dve.wait_ge(pa_free[U_GATE % 2], pa_done(b, U_GATE))
                nc.vector.tensor_scalar(ge[:, :], th[GATE_F:GROWS, :], CAP, None, ALU.mult).then_inc(dve_a, 1)
                dve.wait_ge(dve_a, ch.next())
                nc.vector.scalar_tensor_tensor(ge[:, :], ge[:, :], -1.0, ge[:, :], ALU.mult, ALU.min).then_inc(gate_dve, 1)
                nc.vector.tensor_scalar(gi, th[0:NH, :], CAP, None, ALU.mult)
                nc.vector.tensor_scalar(gf, th[GATE_F:GROWS, :], CAP, 0.0, ALU.mult, ALU.min)
                between[0]()
                dve.wait_ge(gate_act, at(b, 5, 1))
                nc.vector.tensor_scalar(gu, ge[:, :], 1.0, None, ALU.add).then_inc(gate_dve, 1)
                dve.wait_ge(gate_dve, at(b, 4, 2))
                nc.vector.scalar_tensor_tensor(ge[:, :], gu, 1.0, ge[:, :], ALU.subtract, ALU.subtract).then_inc(dve_a, 1)
                dve.wait_ge(dve_a, ch.next())
                nc.vector.tensor_tensor(gf, gf, ge[:, :], ALU.add).then_inc(dve_a, 1)
                dve.wait_ge(dve_a, ch.next())
                dve.wait_ge(gate_act, at(b, 5, 2))
                nc.vector.tensor_tensor(gf, gf, gl, ALU.subtract).then_inc(dve_a, 1)
                dve.wait_ge(dve_a, ch.next())
                nc.vector.tensor_tensor_scan(gu, gf, gi, 0.0, ALU.add, ALU.max).then_inc(gate_dve, 1)
                nc.vector.tensor_tensor_scan(gl, restart[:, :], gf, 0.0, ALU.mult, ALU.add).then_inc(dve_a, 1)
                dve.wait_ge(dve_a, ch.next())
                nc.vector.tensor_tensor(th[0:NH, :], gl, gu, ALU.subtract).then_inc(r_ok, 1)
                nc.vector.tensor_tensor(stack[0:NH, :], gi, gl, ALU.subtract).then_inc(dve_a, 1)
                dve.wait_ge(dve_a, ch.next())
                dve.wait_ge(r_ok, at(b, 1, 1))
                chunks = (NH, T - 1, P)
                nc.vector.tensor_tensor(ge[:, 0:LATE].rearrange("h (c s) -> h c s", s=P),
                                        th[0:NH, P:S].rearrange("h (c s) -> h c s", s=P),
                                        gu[:, P - 1:LATE:P].unsqueeze(2).to_broadcast(list(chunks)), ALU.add)
                nc.vector.tensor_tensor(gf[:, 0:LATE].rearrange("h (c s) -> h c s", s=P),
                                        stack[0:NH, 0:LATE].rearrange("h (c s) -> h c s", s=P),
                                        th[0:NH, P - 1:LATE:P].unsqueeze(2).to_broadcast(list(chunks)),
                                        ALU.add).then_inc(gate_dve, 1)
                between[1]()

            def values(b):
                for t in range(T):
                    use = U_V + t
                    dve.wait_ge(pa_fill, at(b, PA_USES, use + 1))
                    nc.vector.tensor_scalar(vaug[:, t, :, 0:DHV], pa[:, use % 2, :].rearrange("p (h v) -> p h v", v=DHV),
                                            evac[:, W_V:W_V + 1], None, ALU.mult).then_inc(pa_free[use % 2], 1)

            def keys(b):
                dve.wait_ge(ph_free, at(b, PH_USES, U_GT + 1))
                for j in range(T - 1):
                    use = U_KTOK + j
                    dve.wait_ge(pa_fill, at(b, PA_USES, use + 1))
                    nc.vector.tensor_tensor(ktok[:, j, :].rearrange("p (h d) -> p h d", d=DQ),
                                            pa[:, use % 2, 0:QK].rearrange("p (h d) -> p h d", d=DQ),
                                            gtok[:, j, GS:GS + NH].unsqueeze(2).to_broadcast([P, NH, DQ]),
                                            ALU.mult).then_inc(pa_free[use % 2], 1)

            def chunk_decay(b):
                dve.wait_ge(w_loaded, at(b, 16 * NH, 16 * NH))
                nc.vector.tensor_copy(fcol[:, :, :], qw[:, :, P - 1::P]).then_inc(fcol_ok, 1)

            def state(b, j):
                dve.wait_ge(ph_fill, at(b, PH_USES, U_U + j + 1))
                nc.vector.tensor_tensor(cst[:, j, :, :], ph[:, :, 0:H4 * VA],
                                        own_head[:, :].unsqueeze(1).to_broadcast([P, HG, H4 * VA]),
                                        ALU.mult).then_inc(ph_free, 1)
                dve.wait_ge(ph_free, at(b, PH_USES, U_U + j + 1))
                if j == 1:
                    dve.wait_ge(fcol_ok, at(b, 1, 1))
                if j == 2:
                    dve.wait_ge(c_ok, at(b, T - 2, 1))
                if j >= 1:
                    for g in range(HG):
                        last = nc.vector.scalar_tensor_tensor(cst[:, j, g, :], cst[:, j - 1, g, :], fcol[:, g, j - 1:j],
                                                              cst[:, j, g, :], ALU.mult, ALU.add)
                    last.then_inc(c_ok, 1)

            def weigh(b, h):
                dve.wait_ge(ps_fill, at(b, NH, h + 1))
                dve.wait_ge(d_ok, at(b, NH, h + 1))
                nc.vector.tensor_tensor(dec[:, h, :], ps[:, h % 2, :], dec[:, h, :], ALU.mult).then_inc(ps_free[h % 2], 1)

            def head_stats(b, j, ch):
                if not (isinstance(b, int) and b == 0 and j == 0):
                    dve.wait_ge(hvar_ok, at(b, T, j))
                dve.wait_ge(ph_fill, at(b, PH_USES, U_H + j + 1))
                norm = ph[:, :, 0:H4 * VA].rearrange("p a (h v) -> p a h v", v=VA)[:, :, :, DHV]
                den_of = den[:, :].rearrange("p (a h) -> p a h", h=H4)
                nc.vector.tensor_tensor(den_of, norm, gtok[:, j, EM:EM + NH].rearrange("p (a h) -> p a h", h=H4), ALU.max)
                nc.vector.tensor_reduce(hsum[:, :].rearrange("p (a h) -> p a h", h=H4), heads(j), AX.X,
                                        ALU.add).then_inc(dve_a, 1)
                dve.wait_ge(dve_a, ch.next())
                nc.vector.scalar_tensor_tensor(den_of, norm, -1.0, den_of, ALU.mult, ALU.max)
                nc.vector.tensor_scalar(hsum[:, :], hsum[:, :], 1.0 / DHV, None, ALU.mult).then_inc(dve_a, 1)
                dve.wait_ge(dve_a, ch.next())
                nc.vector.tensor_scalar(den[:, :], den[:, :], MLSTM_EPS, None, ALU.add).then_inc(dve_a, 1)
                dve.wait_ge(dve_a, ch.next())
                nc.vector.tensor_tensor(by_head(cent[j % 2]), heads(j), per_head(hsum[:, :], DHV),
                                        ALU.subtract).then_inc(ph_free, 1)
                nc.vector.scalar_tensor_tensor(den[:, :], den[:, :], MLSTM_EPS, den[:, :], ALU.mult, ALU.mult).then_inc(dve_a, 1)
                dve.wait_ge(dve_a, ch.next())
                dve.wait_ge(sq_ok, at(b, T, j + 1))
                nc.vector.tensor_reduce(hsum[:, :], square.rearrange("p a (h v) -> p (a h) v", v=DHV), AX.X,
                                        ALU.add).then_inc(dve_a, 1)
                dve.wait_ge(dve_a, ch.next())
                if not (isinstance(b, int) and b == 0 and j == 0):
                    dve.wait_ge(hn_ok, at(b, T, j))
                nc.vector.scalar_tensor_tensor(hvar[:, :], hsum[:, :], 1.0 / DHV, den[:, :], ALU.mult,
                                               ALU.add).then_inc(hvar_ok, 1)

            def gated(b, j):
                use = U_HT[j]
                dve.wait_ge(pa_fill, at(b, PA_USES, use + 1))
                if j == 0:
                    dve.wait_ge(pa_free[(U_O + 2) % 2], pa_done(b, U_O + 2))
                    dve.wait_ge(pa_free[(U_O + 3) % 2], pa_done(b, U_O + 3))
                    dve.wait_ge(qw_ok, at(b, 1, 1))
                if j >= 2:
                    dve.wait_ge(ho_lo, at(b, T, j - 1))
                nc.vector.scalar_tensor_tensor(hog[j % 2].rearrange("p (k s) -> p k s", s=P),
                                               pa[:, use % 2, :].rearrange("p (k s) -> p k s", s=P), H_SCALE,
                                               sigT[:, :, tok(j)], ALU.mult, ALU.mult).then_inc(pa_free[use % 2], 1)

            def residual(b, t, ch):
                use = U_Y[t]
                dve.wait_ge(pa_fill, at(b, PA_USES, use + 1))
                if t == 0:
                    dve.wait_ge(res_loaded, at(b, 16, 16))
                nc.vector.scalar_tensor_tensor(xres[:, t, :], pa[:, use % 2, :], evac[:, W_OUT:W_OUT + 1], xres[:, t, :],
                                               ALU.mult, ALU.add).then_inc(pa_free[use % 2], 1)
                dve.wait_ge(pa_free[use % 2], pa_done(b, use))
                nc.vector.bn_stats(st2[:, t, :], xres[:, t, :]).then_inc(dve_a, 1)
                dve.wait_ge(dve_a, ch.next())
                if t == T - 1:
                    mean_var(st2, mean2, dif2, dev2, dve_a, ch)
                    nc.vector.tensor_tensor(ve2[:, :], dif2[:, :], dev2[:, :], ALU.add).then_inc(var2, 1)

            def norm2_apply(fb, tiles):
                dve.wait_ge(rstd2_ok, at(fb, 1, 1))
                for t in tiles:
                    dve.wait_ge(x1b_ok, at(fb, T, t + 1))
                    nc.vector.tensor_scalar(xres[:, t, :], xres[:, t, :], mean2[:, t:t + 1], rstd2[:, t:t + 1],
                                            ALU.subtract, ALU.mult).then_inc(xn2_ok, 1)

            def split2_lo(fb):
                for k in range(KD):
                    use = U_T2 + k
                    dve.wait_ge(x2_hi, at(fb, KD, k + 1))
                    nc.vector.scalar_tensor_tensor(x2T[:, LO, k, :], pf[:, use % 2, :], X_SCALE, x2T[:, HI, k, :],
                                                   ALU.mult, ALU.subtract).then_inc(pf_free[use % 2], 1)

            def gelu_split(fb, f, ch):
                use = U_F1 + f
                dve.wait_ge(pf_free[use % 2], pf_done(fb, use))
                nc.vector.tensor_scalar(gT[:, HI, f, :], g32[:, f % 2, :], wscale[:, W_GELU:W_GELU + 1], None,
                                        ALU.mult).then_inc(dve_f, 1)
                dve.wait_ge(dve_f, ch.next())
                nc.vector.scalar_tensor_tensor(gT[:, LO, f, :], g32[:, f % 2, :], wscale[:, W_GELU:W_GELU + 1],
                                               gT[:, HI, f, :], ALU.mult, ALU.subtract).then_inc(gs_ok, 1)

            def result(fb, t):
                use = U_F2 + t
                dve.wait_ge(pf_fill, at(fb, PF_USES, use + 1))
                dve.wait_ge(x1b_ok, at(fb, T, t + 1))
                nc.vector.scalar_tensor_tensor(x1b[:, t, :], pf[:, use % 2, :], winv[:, W_GELU:W_GELU + 1], x1b[:, t, :],
                                               ALU.mult, ALU.add).then_inc(pf_free[use % 2], 1)

            def sequence(b, fb, ahead):
                ca = Chain(b, DVE_A)
                cf = Chain(fb, NF)
                run_f = fb is not None
                split_lo(b)
                gate_decay(b, ca, [lambda: norm2_apply(fb, (0, 1)) if run_f else None,
                                   lambda: norm2_apply(fb, (2, 3)) if run_f else None])
                values(b)
                if run_f:
                    split2_lo(fb)
                keys(b)
                chunk_decay(b)

                def hidden(*fs):
                    if run_f:
                        for f in fs:
                            gelu_split(fb, f, cf)

                hidden(0, 1, 2, 3)
                for j in range(T - 1):
                    state(b, j)
                    hidden(4 + j)
                if ahead:
                    norm_stats(b + 1)
                hidden(7)
                weigh(b, 0)
                weigh(b, 1)
                hidden(8)
                if ahead:
                    norm_apply(b + 1)
                for h in range(2, NH):
                    weigh(b, h)
                    hidden(7 + h)
                hidden(15)

                def done(t):
                    if run_f:
                        result(fb, t)

                done(0)
                head_stats(b, 0, ca)
                head_stats(b, 1, ca)
                gated(b, 0)
                done(1)
                head_stats(b, 2, ca)
                gated(b, 1)
                head_stats(b, 3, ca)
                done(2)
                residual(b, 0, ca)
                gated(b, 2)
                residual(b, 1, ca)
                gated(b, 3)
                done(3)
                residual(b, 2, ca)
                residual(b, 3, ca)
                assert ca.n == DVE_A, ca.n

            norm_stats(0)
            norm_apply(0)
            sequence(0, None, True)
            ternary(0)
            ternary(1)
            with dve.Fori(1, B - 1) as b:
                sequence(b, b - 1, True)
            sequence(B - 1, B - 2, False)
            cf = Chain(B - 1, NF)
            norm2_apply(B - 1, range(T))
            split2_lo(B - 1)
            for f in range(NF):
                gelu_split(B - 1, f, cf)
            for t in range(T):
                result(B - 1, t)

        @block.tensor
        def _(pe):
            PARTS = ((HI, HI), (HI, LO), (LO, HI))

            pe.wait_ge(s_ident, 1)
            pe.wait_ge(s_amax, 1)
            for n in range(17):
                g, k = divmod(n, KD)
                if n >= 2:
                    pe.wait_ge(s_wfree[n % 2], n // 2)
                for i in range(4):
                    if g < 4:
                        last = nc.tensor.transpose(pa[:, n % 2, tok(i)], rows[:, 4 * g + i, tok(k)], ident[:, :])
                    else:
                        last = nc.tensor.transpose(pa[:, n % 2, i * GROWS:(i + 1) * GROWS], th[:, tok(i)],
                                                   ident[0:GROWS, 0:GROWS])
                last.then_inc(s_wfill, 1)

            def ternary_transpose(w):
                with pe.Fori(0, 8) as i:
                    for p in range(2):
                        pe.wait_ge(s_tern, i * 2 + (16 * w + p + 1))
                        bank = pf[:, p, 0:D // 2].bitcast(F16)
                        for k in range(KD):
                            last = nc.tensor.transpose(bank[:, tok(k)], x2T[:, HI, p, tok(k)], ident16[:, :])
                        last.then_inc(s_ufill, 1)
                    for p in range(2):
                        pe.wait_ge(pf_free[p], i + (8 * w + 1))

            def take_pa(b, use):
                if not (isinstance(b, int) and b == 0 and use < 2):
                    pe.wait_ge(pa_free[use % 2], at(b, PA_USES // 2, use // 2))
                return pa[:, use % 2, :]

            def take_pf(fb, use):
                pe.wait_ge(pf_free[use % 2], at(fb, PF, PF_SETUP + use // 2))
                return pf[:, use % 2, :]

            def take_ph(b, use):
                if not (isinstance(b, int) and b == 0 and use == 0):
                    pe.wait_ge(ph_free, at(b, PH_USES, use))

            def transposes(b):
                for k in range(KD):
                    bank = take_pa(b, U_T1 + k)
                    for t in range(T):
                        if k == 0:
                            pe.wait_ge(xn_ok, at(b, T, t + 1))
                        last = nc.tensor.transpose(bank[:, tok(t)], xin[:, t, tok(k)], ident[:, :])
                    last.then_inc(pa_fill, 1)

            def gates(b):
                bank = take_pa(b, U_GATE)
                for k in range(KD):
                    pe.wait_ge(pa_free[(U_T1 + k) % 2], pa_done(b, U_T1 + k))
                    for n, (ws, xs) in enumerate(PARTS):
                        last = nc.tensor.matmul(bank[0:GROWS, :], wgT[:, ws, k, :], xT[:, xs, k, :],
                                                start=(k == 0 and n == 0), stop=(k == KD - 1 and n == 2))
                last.then_inc(pa_fill, 1)

            def features(b, use, col):
                bank = take_pa(b, use)
                for k in range(KD):
                    for n, (ws, xs) in enumerate(PARTS):
                        last = nc.tensor.matmul(bank, wT[:, ws, k, col:col + P], xT[:, xs, k, :],
                                                start=(k == 0 and n == 0), stop=(k == KD - 1 and n == 2))
                last.then_inc(pa_fill, 1)

            def tokens(b, use, t, col):
                bank = take_pa(b, use)
                for k in range(KD):
                    for n, (xs, ws) in enumerate(PARTS):
                        last = nc.tensor.matmul(bank, xT[:, xs, k, tok(t)], wT[:, ws, k, col:col + D],
                                                start=(k == 0 and n == 0), stop=(k == KD - 1 and n == 2))
                last.then_inc(pa_fill, 1)

            def gate_columns(b):
                take_ph(b, U_GT)
                pe.wait_ge(gate_act, at(b, 5, 5))
                for t in range(T):
                    last = nc.tensor.transpose(ph[:, 0, t * STACK:(t + 1) * STACK], stack[:, tok(t)],
                                               ident[0:STACK, 0:STACK])
                last.then_inc(ph_fill, 1)

            def key_tokens(b):
                for n in range(HG):
                    pe.wait_ge(pa_free[(U_K + n) % 2], pa_done(b, U_K + n))
                for j in range(T - 1):
                    bank = take_pa(b, U_KTOK + j)
                    for g in range(HG):
                        last = nc.tensor.transpose(bank[:, tok(g)], kT[:, g, tok(j)], ident[:, :])
                    last.then_inc(pa_fill, 1)

            def outer(b, j):
                take_ph(b, U_U + j)
                pe.wait_ge(pa_free[(U_KTOK + j) % 2], pa_done(b, U_KTOK + j))
                if j == 0:
                    for t in (T - 2, T - 1):
                        pe.wait_ge(pa_free[(U_V + t) % 2], pa_done(b, U_V + t))
                for g in range(HG):
                    last = nc.tensor.matmul(ph[:, g, 0:H4 * VA], ktok[:, j, tok(g)],
                                            vaug[:, j, g * H4:(g + 1) * H4, :], start=True, stop=True)
                last.then_inc(ph_fill, 1)

            def scores(b, h):
                if not (isinstance(b, int) and b == 0 and h < 2):
                    pe.wait_ge(ps_free[h % 2], at(b, NH // 2, h // 2))
                g, row = h // H4, h % H4 * DQ
                for j in range(T):
                    last = nc.tensor.matmul(ps[:, h % 2, tok(j)], kT[row:row + DQ, g, tok(j)], qT[row:row + DQ, g, tok(j)],
                                            start=True, stop=True)
                last.then_inc(ps_fill, 1)

            def chunk(b, j):
                take_ph(b, U_H + j)
                if j == 0:
                    for n in range(2):
                        pe.wait_ge(ps_free[n], at(b, NH // 2, NH // 2))
                if j == 1:
                    pe.wait_ge(qw_ok, at(b, 1, 1))
                    pe.wait_ge(ph_free, at(b, PH_USES, U_U + 1))
                if j >= 2:
                    pe.wait_ge(c_ok, at(b, T - 2, j - 1))
                for g in range(HG):
                    if j > 0:
                        nc.tensor.matmul(ph[:, g, 0:H4 * VA], qw[:, g, tok(j - 1)], cst[:, j - 1, g, :],
                                         start=True, stop=False, skip_group_check=True)
                    for i in range(H4):
                        h = g * H4 + i
                        last = nc.tensor.matmul(ph[:, g, i * VA:(i + 1) * VA], dec[:, h, tok(j)], vaug[:, j, h, :],
                                                start=(j == 0 and i == 0), stop=(i == H4 - 1), skip_group_check=True)
                last.then_inc(ph_fill, 1)

            def head_transposes(b, j):
                bank = take_pa(b, U_HT[j])
                pe.wait_ge(hn_ok, at(b, T, j + 1))
                for k in range(KD):
                    last = nc.tensor.transpose(bank[:, tok(k)], cent[j % 2][:, tok(k)], ident[:, :])
                last.then_inc(pa_fill, 1)

            def project(b, t):
                pe.wait_ge(ho_lo, at(b, T, t + 1))
                tokens(b, U_Y[t], t, C_OUT)

            def transposes2(fb):
                for k in range(KD):
                    bank = take_pf(fb, U_T2 + k)
                    for t in range(T):
                        if k == 0:
                            pe.wait_ge(xn2_ok, at(fb, T, t + 1))
                        last = nc.tensor.transpose(bank[:, tok(t)], xres[:, t, tok(k)], ident[:, :])
                    last.then_inc(pf_fill, 1)

            def up(fb, f):
                bank = take_pf(fb, U_F1 + f)
                for k in range(KD):
                    if f == 0:
                        pe.wait_ge(pf_free[(U_T2 + k) % 2], pf_done(fb, U_T2 + k))
                    for part in (HI, LO):
                        last = nc.tensor.matmul(bank, w1T[:, k, tok(f)], x2T[:, part, k, :],
                                                start=(k == 0 and part == HI), stop=(k == KD - 1 and part == LO))
                last.then_inc(pf_fill, 1)

            def down(fb, t, fs):
                bank = take_pf(fb, U_F2 + t) if fs[0] == 0 else pf[:, (U_F2 + t) % 2, :]
                for f in fs:
                    if t == 0 and (f % 4 == 0 or f >= NF - 4):
                        pe.wait_ge(gs_ok, at(fb, NF, max(f + 1, min(f + 4, NF - 4))))
                    for part in (HI, LO):
                        last = nc.tensor.matmul(bank, gT[:, part, f, tok(t)], w2T[:, f, :],
                                                start=(f == 0 and part == HI), stop=(f == NF - 1 and part == LO))
                if fs[-1] == NF - 1:
                    last.then_inc(pf_fill, 1)

            FIRST, SECOND, ALL = range(NF // 2), range(NF // 2, NF), range(NF)

            def sequence(b, fb):
                def hidden(*fs):
                    if fb is not None:
                        for f in fs:
                            up(fb, f)

                def model(t, fs):
                    if fb is not None:
                        down(fb, t, fs)

                transposes(b)
                gates(b)
                for t in range(T):
                    tokens(b, U_V + t, t, C_V)
                for n in range(KD):
                    features(b, U_O + n, C_O + n * P)
                gate_columns(b)
                if fb is not None:
                    transposes2(fb)
                for n in range(2 * HG):
                    features(b, U_Q + n, C_QK + n * P)
                key_tokens(b)
                hidden(0, 1, 2, 3)
                for j in range(T - 1):
                    outer(b, j)
                    hidden(4 + j)
                hidden(7)
                scores(b, 0)
                scores(b, 1)
                hidden(8)
                for h in range(2, NH):
                    scores(b, h)
                    hidden(7 + h)
                hidden(15)
                model(0, ALL)
                chunk(b, 0)
                model(1, FIRST)
                chunk(b, 1)
                model(1, SECOND)
                head_transposes(b, 0)
                chunk(b, 2)
                model(2, FIRST)
                head_transposes(b, 1)
                chunk(b, 3)
                model(2, SECOND)
                project(b, 0)
                head_transposes(b, 2)
                model(3, FIRST)
                project(b, 1)
                head_transposes(b, 3)
                model(3, SECOND)
                project(b, 2)
                project(b, 3)

            pe.wait_ge(s_wfree[0], 9)
            pe.wait_ge(s_wfree[1], 8)
            sequence(0, None)
            ternary_transpose(0)
            ternary_transpose(1)
            with pe.Fori(1, B - 1) as b:
                sequence(b, b - 1)
            sequence(B - 1, B - 2)
            transposes2(B - 1)
            for f in range(NF):
                up(B - 1, f)
            for t in range(T):
                down(B - 1, t, ALL)


_INS = ["x", "Wq", "Wk", "Wv", "Wog", "Wig", "big", "Wfg", "bfg", "gamma", "Wout"]
_FFN = ["w1", "b1", "w2", "b2"]


def kernel(**inputs):
    import numpy as np
    import concourse.bacc as bacc
    from concourse.bass_utils import run_bass_kernel_spmd

    nc = bacc.Bacc("TRN2", target_bir_lowering=False, num_devices=1)
    arrays, args = {}, []
    for name in [f"L0_attn_{n}" for n in _INS] + [f"L0_ffn_{n}" for n in _FFN]:
        a = np.ascontiguousarray(inputs[name])
        arrays[name] = a
        args.append(nc.dram_tensor(name, a.shape, mybir.dt.from_np(a.dtype), kind="ExternalInput").ap())
    shape = inputs["L0_attn_x"].shape
    out = nc.dram_tensor("out", shape, F32, kind="ExternalOutput").ap()
    block_program(nc, *args, out)
    return run_bass_kernel_spmd(nc, [arrays], core_ids=[0]).results[0]["out"]
```

```python
from contextlib import ExitStack

import concourse.bass as bass
from concourse import mybir

F32 = mybir.dt.float32
F16 = mybir.dt.float16
I32 = mybir.dt.int32
ALU = mybir.AluOpType
ACT = mybir.ActivationFunctionType
AX = mybir.AxisListType
RMAX = bass.bass_isa.ReduceOp.max
RADD = bass.bass_isa.ReduceOp.add

P = 128
CAP = 15.0
MLSTM_EPS = 1e-6
LN_EPS = 1e-5
MASKED = -30000.0
X_SCALE = 2.0 ** 11
H_SCALE = 2.0 ** 12
TOP = 2.0 ** 14
HI, LO = 0, 1


def at(b, per, k):
    return b * per + k


class Chain:

    def __init__(self, b, per):
        self.b, self.per, self.n = b, per, 0

    def next(self):
        self.n += 1
        assert self.n <= self.per, self.n
        return at(self.b, self.per, self.n)


DVE_L, DVE_A = 3, 6 + 4 + 4 * 5 + 4 + 2
POOL_A = 4


def block_program(nc, x, Wq, Wk, Wv, Wog, Wig, big, Wfg, bfg, gamma, Wout, w1, b1, w2, b2, out):
    B, S, D = x.shape
    QK, DV_ALL = Wq.shape[0], Wv.shape[0]
    NH, DHV = gamma.shape
    DQ = QK // NH
    FF = w1.shape[0]
    T = S // P
    KD = D // P
    NF = FF // P
    HG = NH * DQ // P
    H4 = NH // HG
    VA = DHV + 1
    GATE_F = 32
    GROWS = GATE_F + NH
    ROW_C, ROW_EM, ROW_G = range(3)
    STACK = 2 * 32 + NH
    UNITS = FF * D // (P * D)
    LATE = S - P
    C_QK, C_V, C_O, C_OUT = 0, D, 2 * D, 3 * D
    W_QK, W_V, W_O, W_OUT, W_GATE, W_GELU = range(6)
    assert (T, KD, HG, QK, DV_ALL) == (4, 4, 2, 256, D)

    HEADS = [g * H4 + h for h in range(H4) for g in range(HG)]
    U_GATE, U_V, U_K, U_Q, U_O, U_KLAST = 0, 1, 5, 7, 9, 13
    U_HT, U_Y, U_X = (14, 15, 16, 20), (17, 21, 24, 25), (18, 19, 22, 23)
    PA_USES = 26
    PS_USES = (1 + NH // 2, NH // 2)
    U_T2, U_F1, U_F2 = 0, KD, KD + NF
    PF_USES = KD + NF + T
    U_GT, U_U, U_H = 0, 1, T
    PH_USES = 2 * T

    gate_r = nc.dram_tensor("gate_r", (B, NH, S), F32, kind="Internal").ap()
    gate_w = nc.dram_tensor("gate_w", (B, NH, LATE), F32, kind="Internal").ap()

    with ExitStack() as ctx:
        def sb(name, shape, dt=F32):
            return ctx.enter_context(nc.sbuf_tensor(name, shape, dt))

        def pb(name):
            return ctx.enter_context(nc.psum_tensor(name, [P, 2, 512], F32))

        def sem(name):
            return ctx.enter_context(nc.semaphore(name))

        wT = sb("wT", [P, 2, KD, 4 * D], F16)
        wgT = sb("wgT", [P, 2, KD, GROWS], F16)
        w1T = sb("w1T", [P, KD, FF], F16)
        w2T = sb("w2T", [P, NF, D], F16)
        b1c = sb("b1c", [P, NF])
        b2r = sb("b2r", [P, D])
        gate_bias = sb("gate_bias", [GROWS, 1])
        ident = sb("ident", [P, P])
        ident16 = sb("ident16", [P, P], F16)
        causal = sb("causal", [P, P])
        own_head = sb("own_head", [P, H4])
        one = sb("one", [P, 1])
        half = sb("half", [P, NH])
        amax = sb("amax", [P, 6])
        pow2 = sb("pow2", [P, 6])
        wscale = sb("wscale", [P, 6])
        winv = sb("winv", [P, 6])
        split_scale = sb("split_scale", [P, 2])
        evac = sb("evac", [P, 6])
        asum = sb("asum", [P, UNITS // 2])
        thr = sb("thr", [P, 4])
        xin = sb("xin", [P, T, D])
        xres = sb("xres", [P, T, D])
        x1b = sb("x1b", [P, T, D])
        xT = sb("xT", [P, 2, KD, S], F16)
        hoT = sb("hoT", [P, 2, KD, S], F16)
        x2T = sb("x2T", [P, 2, KD, S], F16)
        qT = sb("qT", [P, HG, S])
        kT = sb("kT", [P, HG, S])
        qw = sb("qw", [P, HG, LATE])
        fcol = sb("fcol", [P, HG, T - 1])
        vaug = sb("vaug", [P, T, NH, VA])
        sigT = sb("sigT", [P, KD, S])
        dec = sb("dec", [P, NH, S])
        ktok = sb("ktok", [P, T - 1, QK])
        cst = sb("cst", [P, T - 1, HG, H4 * VA])
        g32 = sb("g32", [P, 2, S])
        gT = sb("gT", [P, 2, NF, S], F16)
        stack = sb("stack", [STACK, S])
        gtok = sb("gtok", [P, T, 3, NH])
        st1, st2 = sb("st1", [P, T, 6]), sb("st2", [P, T, 6])
        mean1, dif1, dev1, ve1, rstd1 = (sb(n + "1", [P, T]) for n in ("mean", "dif", "dev", "ve", "rstd"))
        mean2, dif2, dev2, ve2, rstd2 = (sb(n + "2", [P, T]) for n in ("mean", "dif", "dev", "ve", "rstd"))
        den, hsum, hvar, hinv = (sb(n, [P, NH]) for n in ("den", "hsum", "hvar", "hinv"))
        gu, gl = g32[0:NH, 0, :], g32[0:NH, 1, :]
        gi, gf = kT[0:NH, 0, :], kT[0:NH, 1, :]
        th, ge = qT[0:GROWS, 0, :], qT[0:NH, 1, :]
        cent = [kT[:, i, :] for i in range(2)]
        hog = [qT[:, i, :] for i in range(2)]
        square = ktok[:, 0:2, :]
        kq_parts = (cst[:, :, :, :].rearrange("p a g n -> p (a g n)")[:, 0:HG * S].bitcast(F16)
                    .rearrange("p (a g s) -> p a g s", a=2, g=HG))
        kst = hoT[:, :, :, :].rearrange("p a k s -> p (a k) s")

        def qst(b):
            return xres[:, :, :].bitcast(F16).rearrange("p t (a s) -> p (t a) s", s=S) if isinstance(b, int) and b == 0 \
                else gT[:, HI, NF - NH:NF, :]

        rows = gT[:, :, :, :].bitcast(F32).rearrange("p a n s -> p (a n s)").rearrange("p (n s) -> p n s", s=D)

        pa, pf, ps, ph = pb("pa"), pb("pf"), pb("ps"), pb("ph")

        s_wload = [sem(f"s_wload{g}") for g in range(5)]
        s_small = sem("s_small")
        s_w12 = [[sem(f"s_w{w}load{n}") for n in range(4)] for w in (1, 2)]
        s_const = sem("s_const")
        s_ident = sem("s_ident")
        s_pchain = sem("s_pchain")
        s_dchain = sem("s_dchain")
        s_amax = sem("s_amax")
        s_allmax = sem("s_allmax")
        s_scales = sem("s_scales")
        s_whi = sem("s_whi")
        s_wfill = sem("s_wfill")
        s_wfree = [sem(f"s_wfree{n}") for n in range(4)]
        s_abs = sem("s_abs")
        s_asum = sem("s_asum")
        s_allsum = sem("s_allsum")
        s_thr = sem("s_thr")
        s_low = [sem("s_low_pool"), sem("s_low_dve")]
        s_tern = sem("s_tern")
        s_ufill = sem("s_ufill")
        x_loaded, res_loaded = sem("x_loaded"), sem("res_loaded")
        r_stored, w_stored = sem("r_stored"), sem("w_stored")
        r_loaded = [sem(f"r_loaded{g}") for g in range(HG)]
        w_loaded = sem("w_loaded")
        out_stored = [sem(f"out_stored{t}") for t in range(T)]
        pa_fill, pf_fill, ps_fill, ph_fill = sem("pa_fill"), sem("pf_fill"), sem("ps_fill"), sem("ph_fill")
        pa_free = [sem("pa_free0"), sem("pa_free1")]
        pf_free = [sem("pf_free0"), sem("pf_free1")]
        ps_free = [sem("ps_free0"), sem("ps_free1")]
        ph_free = sem("ph_free")
        dve_l, dve_a = sem("dve_l"), sem("dve_a")
        pool_a = sem("pool_a")
        var1, var2 = sem("var1"), sem("var2")
        rstd1_ok, rstd2_ok = sem("rstd1_ok"), sem("rstd2_ok")
        xn_ok, xn2_ok = sem("xn_ok"), sem("xn2_ok")
        x_hi, x2_hi = sem("x_hi"), sem("x2_hi")
        gate_dve, gate_act = sem("gate_dve"), sem("gate_act")
        r_ok = sem("r_ok")
        masked = sem("masked")
        d_ok = sem("d_ok")
        qw_ok, fcol_ok = sem("qw_ok"), sem("fcol_ok")
        k_ok, kq_ok = sem("k_ok"), sem("kq_ok")
        c_ok = sem("c_ok")
        sq_ok = sem("sq_ok")
        hvar_ok = sem("hvar_ok")
        hn_ok = sem("hn_ok")
        ho_hi, ho_lo = sem("ho_hi"), sem("ho_lo")
        x1b_ok = sem("x1b_ok")
        g_hi, gs_ok = sem("g_hi"), sem("gs_ok")
        sig_ok = sem("sig_ok")

        def skipped(b, use):
            return sum(u < use for u in U_X) if isinstance(b, int) and b == B - 1 else 0

        def pa_filled(b, use):
            return at(b, PA_USES, KD + use + 1 - skipped(b, use))

        def pa_taken(b, use):
            return at(b, PA_USES // 2, (KD + use - skipped(b, use)) // 2)

        def pa_done(b, use):
            return at(b, PA_USES // 2, (KD + use - skipped(b, use)) // 2 + 1)

        def x_use(b, k):
            return (b - 1, U_X[k]) if not (isinstance(b, int) and b == 0) else (-1, k + PA_USES - KD)

        def ps_done(b, n):
            return at(b, PS_USES[n % 2], PS_USES[n % 2] - NH // 2 + n // 2 + 1)

        PF = PF_USES // 2
        PF_SETUP = UNITS // 2

        def pf_done(fb, use):
            return at(fb, PF, PF_SETUP + use // 2 + 1)

        def tok(t):
            return slice(t * P, (t + 1) * P)

        def per_head(ap, n):
            return ap.rearrange("p (a h) -> p a h", h=H4).unsqueeze(3).to_broadcast([P, HG, H4, n])

        def heads(j):
            return ph[:, :, 0:H4 * VA].rearrange("p a (h v) -> p a h v", v=VA)[:, :, :, 0:DHV]

        def by_head(ap):
            return ap.rearrange("p (a h v) -> p a h v", a=HG, h=H4)

        wbank = [pa[:, 0, :], pa[:, 1, :], ps[:, 0, :], ps[:, 1, :]]
        W_BANKS = 4 * KD + 1
        W_READ = [(W_BANKS - n + 3) // 4 for n in range(4)]

        def tern(u):
            return x2T[:, HI, u % 4, :]

        def low(u):
            return x2T[:, LO, u % 4, :]

        def pair_bank(q):
            return pf[:, q % 2, :].bitcast(F16).rearrange("p (u k c) -> p u k c", u=2, c=P)

        block = ctx.enter_context(nc.Block())

        @block.sync
        def _(sp):
            sp.dma_start(xin[:, :, :], x[0].rearrange("(t p) d -> p t d", p=P)).then_inc(x_loaded, 16)
            for g, parts in enumerate(((Wq, Wk), (Wv,), (Wog,), (Wout,))):
                n = 4 * g
                for w in parts:
                    k = w.shape[0] // P
                    sp.dma_start(rows[:, n:n + k, :], w.rearrange("(n p) d -> p n d", p=P)).then_inc(s_wload[g], 16)
                    n += k
                if g == 0:
                    sp.wait_ge(s_const, 1)
                    sp.dma_start(th[0:NH, :], Wig).then_inc(s_wload[4], 16)
                    sp.dma_start(th[GATE_F:GROWS, :], Wfg).then_inc(s_wload[4], 16)
                    sp.dma_start(gate_bias[0:NH, :], big.unsqueeze(1)).then_inc(s_small, 16)
                    sp.dma_start(gate_bias[GATE_F:GROWS, :], bfg.unsqueeze(1)).then_inc(s_small, 16)
                    sp.dma_start(g32[:, 0, :], gamma.rearrange("h v -> (h v)").partition_broadcast(P)).then_inc(s_small, 16)
                    sp.dma_start(b2r[:, :], b2.partition_broadcast(P)).then_inc(s_small, 16)
                    sp.dma_start(b1c[:, :], b1.rearrange("(n p) -> p n", p=P),
                                 allow_slow_non_contiguous=True).then_inc(s_small, 16)

            def stage_a(b):
                if isinstance(b, int) and b == 0:
                    sp.wait_ge(ps_fill, sum(PS_USES))
                else:
                    sp.wait_ge(pf_fill, at(b - 1, PF_USES, U_T2 + KD))
                sp.dma_start(xres[:, :, :], x[b].rearrange("(t p) d -> p t d", p=P)).then_inc(res_loaded, 16)

            def gate_rows(b):
                sp.wait_ge(r_ok, at(b, 1, 1))
                sp.dma_start(gate_r[b], th[0:NH, :]).then_inc(r_stored, 16)
                sp.wait_ge(gate_act, at(b, 5, 4))
                sp.dma_start(gate_w[b], ge[:, 0:LATE]).then_inc(w_stored, 16)
                if not (isinstance(b, int) and b == 0):
                    sp.wait_ge(ph_fill, at(b, PH_USES, 0))
                sp.wait_ge(r_stored, at(b, 16, 16))
                for g in range(HG):
                    sp.dma_start(dec[:, g * H4:(g + 1) * H4, :],
                                 gate_r[b, g * H4:(g + 1) * H4, :].rearrange("h s -> (h s)").partition_broadcast(P)
                                 .rearrange("p (h s) -> p h s", s=S)).then_inc(r_loaded[g], 16)
                sp.wait_ge(w_stored, at(b, 16, 16))
                for h in range(H4):
                    for g in range(HG):
                        sp.dma_start(qw[h * DQ:(h + 1) * DQ, g, :],
                                     gate_w[b, g * H4 + h, :].partition_broadcast(DQ)).then_inc(w_loaded, 16)

            def next_x(b):
                sp.wait_ge(pa_fill, pa_filled(*x_use(b, KD - 1)))
                sp.dma_start(xin[:, :, :], x[b + 1].rearrange("(t p) d -> p t d", p=P)).then_inc(x_loaded, 16)

            def store(fb):
                for t in range(T):
                    use = U_F2 + t
                    sp.wait_ge(pf_free[use % 2], pf_done(fb, use))
                    sp.dma_start(out[fb, tok(t), :], x1b[:, t, :]).then_inc(out_stored[t], 16)

            next_x(0)
            gate_rows(0)
            for n in range(4):
                sp.wait_ge(s_tern, 4 * (n + 1))
                sp.dma_start(rows[:, 4 * n:4 * n + 4, :],
                             w2.rearrange("(n p) (c d) -> p n c d", p=P, d=D)[:, n, :, :]).then_inc(s_w12[1][n], 16)
            stage_a(0)
            with sp.Fori(1, B - 1) as b:
                next_x(b)
                gate_rows(b)
                stage_a(b)
                store(b - 1)
            gate_rows(B - 1)
            stage_a(B - 1)
            store(B - 2)
            store(B - 1)
            for t in range(T):
                sp.wait_ge(out_stored[t], 16 * B)

        @block.gpsimd
        def _(pool):
            nc.gpsimd.memset(gate_bias[:, :], 0.0)
            nc.gpsimd.memset(th, 0.0).then_inc(s_const, 1)
            nc.gpsimd.memset(ident[:, :], 0.0)
            nc.gpsimd.memset(causal[:, :], 0.0)
            nc.gpsimd.memset(own_head[:, :], 1.0)
            nc.gpsimd.memset(one[:, :], 1.0)
            nc.gpsimd.memset(stack[:, :], 0.0)
            nc.gpsimd.memset(amax[:, :], 0.0)
            nc.gpsimd.memset(half[:, :], -0.5)
            nc.gpsimd.memset(vaug[:, :, :, DHV:VA], 1.0).then_inc(s_pchain, 1)
            pool.wait_ge(s_pchain, 1)
            nc.gpsimd.affine_select(out=ident[:, :], in_=ident[:, :], compare_op=ALU.not_equal, fill=1.0,
                                    base=0, pattern=[[-1, P]], channel_multiplier=1)
            nc.gpsimd.affine_select(out=causal[:, :], in_=causal[:, :], compare_op=ALU.is_ge, fill=MASKED,
                                    base=0, pattern=[[1, P]], channel_multiplier=-1)
            nc.gpsimd.affine_select(out=own_head[:, :], in_=own_head[:, :], compare_op=ALU.is_ge, fill=0.0,
                                    base=0, pattern=[[-DQ, H4]], channel_multiplier=1).then_inc(s_pchain, 1)
            pool.wait_ge(s_pchain, 2)
            nc.gpsimd.affine_select(out=own_head[:, :], in_=own_head[:, :], compare_op=ALU.is_ge, fill=0.0,
                                    base=DQ - 1, pattern=[[DQ, H4]], channel_multiplier=-1)
            nc.gpsimd.tensor_copy(ident16[:, :], ident[:, :]).then_inc(s_ident, 1)

            def w_sum(n):
                pool.wait_ge(s_asum, n + 1)
                nc.gpsimd.partition_all_reduce(thr[:, 1:2], thr[:, 0:1], P, RADD).then_inc(s_allsum, 1)

            def layer_norm(b):
                pool.wait_ge(var1, at(b, 1, 1))
                nc.gpsimd.tensor_tensor(rstd1[:, :], ve1[:, :], half[:, 0:T], ALU.pow).then_inc(rstd1_ok, 1)

            def ternary_low():
                for u in range(0, UNITS, 2):
                    if u == 0:
                        pool.wait_ge(s_thr, 1)
                    if u >= 4:
                        pool.wait_ge(s_tern, u - 3)
                    nc.gpsimd.tensor_scalar(low(u), rows[:, u, :], thr[:, 3:4], None, ALU.is_le).then_inc(s_low[0], 1)

            def decay(b):
                for n in range(NH // 2):
                    if n % 2 == 0:
                        pool.wait_ge(r_loaded[n // 2], at(b, 16, 16))
                    rows_of = dec[:, 2 * n:2 * n + 2, :].rearrange("p h (t s) -> p (h t) s", s=P)
                    nc.gpsimd.tensor_tensor(rows_of, rows_of,
                                            causal[:, :].unsqueeze(1).to_broadcast([P, 2 * T, P]),
                                            ALU.add).then_inc(masked, 1)

            def weigh_queries(b):
                pool.wait_ge(fcol_ok, at(b, 1, 1))
                pool.wait_ge(pa_free[(U_Q + 1) % 2], pa_done(b, U_Q + 1))
                pool.wait_ge(pa_free[U_Q % 2], pa_done(b, U_Q))
                nc.gpsimd.tensor_tensor(qw[:, :, :], qw[:, :, :], qT[:, :, P:S], ALU.mult).then_inc(qw_ok, 1)

            def head_norm(b, j):
                pool.wait_ge(hvar_ok, at(b, T, j + 1))
                nc.gpsimd.tensor_tensor(hinv[:, :], hvar[:, :], half[:, :], ALU.pow).then_inc(pool_a, 1)
                pool.wait_ge(pool_a, at(b, POOL_A, j + 1))
                hc = by_head(cent[j % 2])
                nc.gpsimd.tensor_tensor(hc, hc, per_head(hinv[:, :], DHV), ALU.mult).then_inc(hn_ok, 1)

            def gated_lo(b, j):
                pool.wait_ge(ho_hi, at(b, T, j + 1))
                nc.gpsimd.tensor_tensor(hoT[:, LO, :, tok(j)], hog[j % 2].rearrange("p (k s) -> p k s", s=P),
                                        hoT[:, HI, :, tok(j)], ALU.subtract).then_inc(ho_lo, 1)

            def residual_bias(b, t):
                use = U_Y[t]
                pool.wait_ge(pa_free[use % 2], pa_done(b, use))
                if not (isinstance(b, int) and b == 0):
                    pool.wait_ge(out_stored[t], at(b, 16, 0))
                nc.gpsimd.tensor_tensor(x1b[:, t, :], xres[:, t, :], b2r[:, :], ALU.add).then_inc(x1b_ok, 1)

            def layer_norm2(b):
                pool.wait_ge(var2, at(b, 1, 1))
                nc.gpsimd.tensor_tensor(rstd2[:, :], ve2[:, :], half[:, 0:T], ALU.pow).then_inc(rstd2_ok, 1)

            layer_norm(0)
            pool.wait_ge(s_amax, 1)
            nc.gpsimd.partition_all_reduce(pow2[:, :], amax[:, :], P, RMAX).then_inc(s_allmax, 1)

            def sequence(b, ahead):
                if ahead:
                    layer_norm(b + 1)
                first = isinstance(b, int) and b == 0
                decay(b)
                if first:
                    w_sum(0)
                    ternary_low()
                weigh_queries(b)
                head_norm(b, 0)
                if first:
                    w_sum(1)
                head_norm(b, 1)
                gated_lo(b, 0)
                head_norm(b, 2)
                gated_lo(b, 1)
                head_norm(b, 3)
                residual_bias(b, 0)
                gated_lo(b, 2)
                residual_bias(b, 1)
                gated_lo(b, 3)
                residual_bias(b, 2)
                residual_bias(b, 3)
                layer_norm2(b)

            sequence(0, True)
            with pool.Fori(1, B - 1) as b:
                sequence(b, True)
            sequence(B - 1, False)

        @block.scalar
        def _(act):
            def weights_hi():
                act.wait_ge(s_scales, 1)
                for n in range(W_BANKS):
                    g, k = divmod(n, KD)
                    act.wait_ge(s_wfill, n + 1)
                    if g < 4:
                        nc.scalar.activation(wT[:, HI, k, g * D:(g + 1) * D], wbank[n % 4], ACT.Copy,
                                             scale=wscale[:, g:g + 1]).then_inc(s_whi, 1)
                    else:
                        nc.scalar.activation(wgT[:, HI, :, :], wbank[n % 4][:, 0:KD * GROWS].rearrange("p (k r) -> p k r", r=GROWS),
                                             ACT.Copy, scale=wscale[:, W_GATE:W_GATE + 1]).then_inc(s_whi, 1)

            def load_w1():
                for n in range(4):
                    act.wait_ge(s_wfree[n], W_READ[n])
                for n in range(4):
                    act.dma_start(rows[:, 4 * n:4 * n + 4, :],
                                  w1.rearrange("(n p) d -> p n d", p=P)[:, 4 * n:4 * n + 4, :]).then_inc(s_w12[0][n], 16)

            def absolute_sums(w, *ns):
                for n in ns:
                    if n % 2 == 0:
                        act.wait_ge(s_w12[w][n // 2], 16)
                    if w == 0 and n == 0:
                        act.wait_ge(gate_act, 5)
                    else:
                        act.wait_ge(s_abs, UNITS // 2 * w + n)
                    if w == 1 and n == 0:
                        act.wait_ge(s_asum, 1)
                    nc.scalar.activation(g32[:, :, :], rows[:, 2 * n:2 * n + 2, :], ACT.Abs,
                                         accum_out=asum[:, n:n + 1]).then_inc(s_abs, 1)

            def ternary_out(w, pairs):
                for q in pairs:
                    act.wait_ge(s_ufill, UNITS // 2 * w + q + 1)
                    if w == 0:
                        dst = w1T[:, :, 2 * q * P:(2 * q + 2) * P].rearrange("p k (u c) -> p u k c", c=P)
                        src = pair_bank(q)
                    else:
                        dst = w2T[:, 8 * (q % 2):8 * (q % 2) + 8, q // 2 * P:(q // 2 + 1) * P]
                        src = pair_bank(q).rearrange("p u k c -> p (u k) c")
                    nc.scalar.activation(dst, src, ACT.Copy).then_inc(pf_free[q % 2], 1)

            def split_hi(b, ks):
                for k in ks:
                    when, use = x_use(b, k)
                    act.wait_ge(pa_fill, pa_filled(when, use))
                    nc.scalar.activation(xT[:, HI, k, :], pa[:, use % 2, :], ACT.Copy,
                                         scale=X_SCALE).then_inc(x_hi, 1)

            def gates(b):
                act.wait_ge(pa_fill, pa_filled(b, U_GATE))
                nc.scalar.activation(th, pa[0:GROWS, U_GATE % 2, :], ACT.Tanh, bias=gate_bias[:, 0:1],
                                     scale=evac[0:GROWS, W_GATE:W_GATE + 1]).then_inc(pa_free[U_GATE % 2], 1)
                act.wait_ge(gate_dve, at(b, 4, 1))
                nc.scalar.activation(ge, ge, ACT.Exp).then_inc(gate_act, 1)
                value(b, 0)
                act.wait_ge(gate_dve, at(b, 4, 2))
                nc.scalar.activation(gl, gu, ACT.Ln).then_inc(gate_act, 1)
                value(b, 1)
                value(b, 2)
                act.wait_ge(gate_dve, at(b, 4, 3))
                nc.scalar.activation(stack[32:32 + NH, :], gu, ACT.Exp, scale=-1.0).then_inc(gate_act, 1)
                act.wait_ge(gate_dve, at(b, 4, 4))
                nc.scalar.activation(ge[:, 0:LATE], ge[:, 0:LATE], ACT.Exp).then_inc(gate_act, 1)
                nc.scalar.activation(stack[64:64 + NH, 0:LATE], gf[:, 0:LATE], ACT.Exp).then_inc(gate_act, 1)
                value(b, 3)

            def value(b, t):
                use = U_V + t
                act.wait_ge(pa_fill, pa_filled(b, use))
                nc.scalar.activation(vaug[:, t, :, 0:DHV], pa[:, use % 2, :].rearrange("p (h v) -> p h v", v=DHV),
                                     ACT.Copy, scale=evac[:, W_V:W_V + 1]).then_inc(pa_free[use % 2], 1)

            def output_gate(b, *ns):
                for n in ns:
                    use = U_O + n
                    act.wait_ge(pa_fill, pa_filled(b, use))
                    nc.scalar.activation(sigT[:, n, :], pa[:, use % 2, :], ACT.Copy,
                                         scale=evac[:, W_O:W_O + 1]).then_inc(pa_free[use % 2], 1)

            def sigmoids(b):
                for n in (U_O + 2, U_O + 3):
                    act.wait_ge(pa_free[n % 2], pa_done(b, n))
                nc.scalar.activation(sigT[:, :, :], sigT[:, :, :], ACT.Sigmoid).then_inc(sig_ok, 1)

            def gate_columns(b):
                act.wait_ge(ph_fill, at(b, PH_USES, U_GT + 1))
                nc.scalar.activation(gtok[:, :, :, :], ph[:, 0, :].rearrange("p (t a h) -> p t a h", t=T, h=32)[:, :, 0:3, 0:NH],
                                     ACT.Copy).then_inc(ph_free, 1)

            def keys(b, *ns):
                for n in ns:
                    use = U_K + n
                    act.wait_ge(pa_fill, pa_filled(b, use))
                    nc.scalar.activation(kT[:, n, :], pa[:, use % 2, :], ACT.Copy,
                                         scale=evac[:, W_QK:W_QK + 1]).then_inc(pa_free[use % 2], 1)

            def queries(b, *ns):
                if 0 in ns:
                    act.wait_ge(r_stored, at(b, 16, 16))
                    act.wait_ge(w_stored, at(b, 16, 16))
                for n in ns:
                    use = U_Q + n
                    act.wait_ge(pa_fill, pa_filled(b, use))
                    nc.scalar.activation(qT[:, n, :], pa[:, use % 2, :], ACT.Copy,
                                         scale=evac[:, W_GELU:W_GELU + 1]).then_inc(pa_free[use % 2], 1)

            def decay(b, first):
                act.wait_ge(masked, at(b, NH // 2, first // 2 + 1))
                if first == 0:
                    act.wait_ge(ph_free, at(b, PH_USES, U_GT + 1))
                for h in (first, first + 1):
                    for j in range(T):
                        last = nc.scalar.activation(dec[:, h, tok(j)], dec[:, h, tok(j)], ACT.Exp,
                                                    bias=gtok[:, j, ROW_C, h:h + 1])
                    last.then_inc(d_ok, 1)

            def split2_hi(fb, ks):
                for k in ks:
                    act.wait_ge(pf_fill, at(fb, PF_USES, U_T2 + k + 1))
                    nc.scalar.activation(x2T[:, HI, k, :], pf[:, (U_T2 + k) % 2, :], ACT.Copy,
                                         scale=X_SCALE).then_inc(x2_hi, 1)

            def gelu(fb, f):
                use = U_F1 + f
                act.wait_ge(pf_fill, at(fb, PF_USES, use + 1))
                if f >= 2:
                    act.wait_ge(gs_ok, at(fb, NF, f - 1))
                if f == 0:
                    act.wait_ge(gate_act, at(fb, 5, 5))
                nc.scalar.activation(g32[:, f % 2, :], pf[:, use % 2, :], ACT.Gelu, bias=b1c[:, f:f + 1],
                                     scale=1.0 / X_SCALE).then_inc(pf_free[use % 2], 1)
                act.wait_ge(pf_free[use % 2], pf_done(fb, use))
                nc.scalar.activation(gT[:, HI, f, :], g32[:, f % 2, :], ACT.Copy,
                                     scale=wscale[:, W_GELU:W_GELU + 1]).then_inc(g_hi, 1)

            def squares(b, j):
                act.wait_ge(ph_free, at(b, PH_USES, U_H + j + 1))
                nc.scalar.activation(square, cent[j % 2].rearrange("p (a s) -> p a s", a=2), ACT.Square).then_inc(sq_ok, 1)

            def gated_hi(b, j):
                use = U_HT[j]
                act.wait_ge(pa_free[use % 2], pa_done(b, use))
                nc.scalar.activation(hoT[:, HI, :, tok(j)], hog[j % 2].rearrange("p (k s) -> p k s", s=P),
                                     ACT.Copy).then_inc(ho_hi, 1)

            def sequence(b, fb, ahead):
                gates(b)
                run_f = fb is not None
                if run_f:
                    keys(b, 0, 1)
                    gate_columns(b)
                    queries(b, 0, 1)
                else:
                    absolute_sums(0, 0)
                    keys(b, 0)
                    absolute_sums(0, 1, 2)
                    keys(b, 1)
                    gate_columns(b)
                    absolute_sums(0, 3, 4)
                    queries(b, 0)
                    absolute_sums(0, 5)
                    queries(b, 1)
                    absolute_sums(0, 6, 7)
                decay(b, 0)
                output_gate(b, 0)
                decay(b, 2)
                output_gate(b, 1)
                if run_f:
                    split2_hi(fb, (0, 1))
                decay(b, 4)
                output_gate(b, 2)
                if run_f:
                    split2_hi(fb, (2, 3))
                decay(b, 6)
                output_gate(b, 3)
                if run_f:
                    for f in range(NF):
                        gelu(fb, f)
                else:
                    ternary_out(0, range(0, 5))
                    for n in range(3):
                        absolute_sums(1, n)
                        ternary_out(0, (5 + n,))
                    absolute_sums(1, 3, 4, 5, 6, 7)

                def ternary2(*pairs):
                    if not run_f:
                        ternary_out(1, pairs)

                sigmoids(b)
                squares(b, 0)
                squares(b, 1)
                ternary2(0)
                gated_hi(b, 0)
                squares(b, 2)
                ternary2(1, 2)
                gated_hi(b, 1)
                squares(b, 3)
                ternary2(3)
                gated_hi(b, 2)
                ternary2(4, 5)
                if ahead:
                    split_hi(b + 1, (0, 1))
                gated_hi(b, 3)
                ternary2(6)
                if ahead:
                    split_hi(b + 1, (2, 3))
                ternary2(7)

            split_hi(0, range(KD))
            weights_hi()
            load_w1()
            sequence(0, None, True)
            with act.Fori(1, B - 1) as b:
                sequence(b, b - 1, True)
            sequence(B - 1, B - 2, False)
            split2_hi(B - 1, range(KD))
            act.wait_ge(gs_ok, at(B - 1, NF, 0))
            for f in range(NF):
                gelu(B - 1, f)

        @block.vector
        def _(dve):
            def largest(g):
                dve.wait_ge(s_wload[g], 32 if g == W_QK else 16)
                if g == W_OUT:
                    dve.wait_ge(s_small, 80)
                    wo = rows[:, 4 * g:4 * g + 4, :]
                    nc.vector.tensor_tensor(wo, wo, g32[:, 0, :].unsqueeze(1).to_broadcast([P, 4, D]),
                                            ALU.mult).then_inc(s_dchain, 1)
                    dve.wait_ge(s_dchain, 1)
                if g == W_QK:
                    dve.wait_ge(s_ident, 1)
                nc.vector.tensor_reduce(amax[:, g:g + 1], rows[:, 4 * g:4 * g + 4, :], AX.XY, ALU.max,
                                        apply_absolute_value=True)

            def scales():
                dve.wait_ge(s_wload[4], 32)
                nc.vector.tensor_reduce(amax[0:GROWS, W_GATE:W_GATE + 1], th, AX.X, ALU.max, apply_absolute_value=True)
                nc.vector.tensor_scalar(gate_bias[:, :], gate_bias[:, :], 1.0 / CAP, None, ALU.mult)
                nc.vector.tensor_reduce(amax[:, W_GELU:W_GELU + 1], b1c[:, :], AX.X, ALU.max,
                                        apply_absolute_value=True).then_inc(s_amax, 1)
                dve.wait_ge(s_allmax, 1)
                nc.vector.tensor_scalar(pow2[:, W_GELU:W_GELU + 1], pow2[:, W_GELU:W_GELU + 1], float(D), None,
                                        ALU.add).then_inc(s_dchain, 1)
                dve.wait_ge(s_dchain, 2)
                bits = pow2[:, :].bitcast(I32)
                nc.vector.tensor_scalar(bits, bits, 0x7F800000, None, ALU.bitwise_and).then_inc(s_dchain, 1)
                dve.wait_ge(s_dchain, 3)
                nc.vector.tensor_scalar(pow2[:, :], pow2[:, :], 2.0 ** -100, 1.0 / TOP, ALU.max, ALU.mult).then_inc(s_dchain, 1)
                dve.wait_ge(s_dchain, 4)
                nc.vector.reciprocal(wscale[:, :], pow2[:, :])
                nc.vector.tensor_copy(winv[:, :], pow2[:, :])
                nc.vector.tensor_scalar(split_scale[:, 1:2], pow2[:, W_QK:W_QK + 1], 2.0 ** 9, pow2[:, W_QK:W_QK + 1],
                                        ALU.mult, ALU.mult)
                for g, c in ((W_QK, 1.0 / X_SCALE), (W_V, 1.0 / X_SCALE), (W_O, 1.0 / X_SCALE), (W_OUT, 1.0 / H_SCALE),
                             (W_GATE, 1.0 / (X_SCALE * CAP))):
                    nc.vector.tensor_scalar(evac[:, g:g + 1], pow2[:, g:g + 1], c, None, ALU.mult)
                nc.vector.tensor_scalar(evac[:, W_GELU:W_GELU + 1], pow2[:, W_QK:W_QK + 1], DQ ** -0.5 / X_SCALE, None,
                                        ALU.mult).then_inc(s_scales, 1)
                dve.wait_ge(s_scales, 1)
                nc.vector.tensor_scalar(split_scale[:, 0:1], wscale[:, W_QK:W_QK + 1], 2.0 ** -9, None, ALU.mult)
                nc.vector.tensor_scalar(split_scale[:, 1:2], split_scale[:, 1:2], 2.0 ** 9, None,
                                        ALU.mult).then_inc(s_dchain, 1)

            def weights_lo():
                for n in range(W_BANKS):
                    g, k = divmod(n, KD)
                    dve.wait_ge(s_whi, n + 1)
                    if g < 4:
                        hi, lo = (wT[:, part, k, g * D:(g + 1) * D] for part in (HI, LO))
                        src = wbank[n % 4]
                    else:
                        hi, lo = (wgT[:, part, :, :] for part in (HI, LO))
                        src = wbank[n % 4][:, 0:KD * GROWS].rearrange("p (k r) -> p k r", r=GROWS)
                    nc.vector.scalar_tensor_tensor(lo, src, wscale[:, g:g + 1], hi, ALU.mult,
                                                   ALU.subtract).then_inc(s_wfree[n % 4], 1)

            def threshold(w):
                dve.wait_ge(s_abs, UNITS // 2 * (w + 1))
                nc.vector.tensor_reduce(thr[:, 0:1], asum[:, :], AX.X, ALU.add).then_inc(s_asum, 1)
                dve.wait_ge(s_allsum, w + 1)
                nc.vector.tensor_scalar(thr[:, 2:3], thr[:, 1:2], 1.0 / (FF * D), 0.7, ALU.mult, ALU.mult).then_inc(s_dchain, 1)
                dve.wait_ge(s_dchain, 6 + w)
                nc.vector.tensor_scalar(thr[:, 3:4], thr[:, 2:3], -1.0, None, ALU.mult).then_inc(s_thr, 1)
                dve.wait_ge(s_thr, w + 1)

            def ternary(w, units):
                for u in units:
                    by_pool = w == 0 and u % 2 == 0
                    if not by_pool:
                        if u >= 4 or w > 0:
                            dve.wait_ge(s_tern, UNITS * w + u - 3)
                        nc.vector.tensor_scalar(low(u), rows[:, u, :], thr[:, 3:4], None, ALU.is_le).then_inc(s_low[1], 1)
                    dve.wait_ge(s_low[0 if by_pool else 1], u // 2 + 1 if w == 0 else UNITS // 2 + u + 1)
                    if UNITS * w + u >= 4:
                        dve.wait_ge(s_ufill, (UNITS * w + u) // 2 - 1)
                    nc.vector.scalar_tensor_tensor(tern(u), rows[:, u, :], thr[:, 2:3], low(u), ALU.is_ge,
                                                   ALU.subtract).then_inc(s_tern, 1)

            def mean_var(st, mean, dif, dev, order, ch):
                nc.vector.tensor_tensor(mean[:, :], st[:, :, 1], st[:, :, 4], ALU.add)
                nc.vector.tensor_tensor(dif[:, :], st[:, :, 1], st[:, :, 4], ALU.subtract)
                nc.vector.tensor_tensor(dev[:, :], st[:, :, 2], st[:, :, 5], ALU.add).then_inc(order, 1)
                dve.wait_ge(order, ch.next())
                nc.vector.tensor_scalar(mean[:, :], mean[:, :], 0.5, None, ALU.mult)
                nc.vector.scalar_tensor_tensor(dif[:, :], dif[:, :], 0.25, dif[:, :], ALU.mult, ALU.mult)
                nc.vector.tensor_scalar(dev[:, :], dev[:, :], 1.0 / D, LN_EPS, ALU.mult, ALU.add).then_inc(order, 1)
                dve.wait_ge(order, ch.next())

            def norm_stats(b):
                ch = Chain(b, DVE_L)
                dve.wait_ge(x_loaded, at(b, 16, 16))
                for t in range(T):
                    last = nc.vector.bn_stats(st1[:, t, :], xin[:, t, :])
                last.then_inc(dve_l, 1)
                dve.wait_ge(dve_l, ch.next())
                mean_var(st1, mean1, dif1, dev1, dve_l, ch)
                nc.vector.tensor_tensor(ve1[:, :], dif1[:, :], dev1[:, :], ALU.add).then_inc(var1, 1)

            def norm_apply(b):
                dve.wait_ge(rstd1_ok, at(b, 1, 1))
                for t in range(T):
                    nc.vector.tensor_scalar(xin[:, t, :], xin[:, t, :], mean1[:, t:t + 1], rstd1[:, t:t + 1],
                                            ALU.subtract, ALU.mult).then_inc(xn_ok, 1)

            def split_lo(b, ks):
                for k in ks:
                    when, use = x_use(b, k)
                    dve.wait_ge(x_hi, at(b, KD, k + 1))
                    nc.vector.scalar_tensor_tensor(xT[:, LO, k, :], pa[:, use % 2, :], X_SCALE, xT[:, HI, k, :],
                                                   ALU.mult, ALU.subtract).then_inc(pa_free[use % 2], 1)

            def gate_decay(b, ch, between):
                dve.wait_ge(pa_free[U_GATE % 2], pa_done(b, U_GATE))
                nc.vector.tensor_scalar(ge, th[GATE_F:GROWS, :], CAP, None, ALU.mult).then_inc(dve_a, 1)
                dve.wait_ge(dve_a, ch.next())
                nc.vector.scalar_tensor_tensor(ge, ge, -1.0, ge, ALU.mult, ALU.min).then_inc(gate_dve, 1)
                nc.vector.tensor_scalar(gi, th[0:NH, :], CAP, None, ALU.mult)
                nc.vector.tensor_scalar(gf, th[GATE_F:GROWS, :], CAP, 0.0, ALU.mult, ALU.min)
                between[0]()
                dve.wait_ge(gate_act, at(b, 5, 1))
                nc.vector.tensor_scalar(gu, ge, 1.0, None, ALU.add).then_inc(gate_dve, 1)
                dve.wait_ge(gate_dve, at(b, 4, 2))
                nc.vector.scalar_tensor_tensor(ge, gu, 1.0, ge, ALU.subtract, ALU.subtract).then_inc(dve_a, 1)
                dve.wait_ge(dve_a, ch.next())
                nc.vector.tensor_tensor(gf, gf, ge, ALU.add).then_inc(dve_a, 1)
                dve.wait_ge(dve_a, ch.next())
                dve.wait_ge(gate_act, at(b, 5, 2))
                nc.vector.tensor_tensor(gf, gf, gl, ALU.subtract).then_inc(dve_a, 1)
                dve.wait_ge(dve_a, ch.next())
                nc.vector.tensor_tensor_scan(gu, gf, gi, 0.0, ALU.add, ALU.max).then_inc(gate_dve, 1)
                for j in range(T):
                    last = nc.vector.tensor_tensor_scan(gl[:, tok(j)], one[0:NH, :].to_broadcast([NH, P]), gf[:, tok(j)], 0.0,
                                                        ALU.mult, ALU.add)
                last.then_inc(dve_a, 1)
                dve.wait_ge(dve_a, ch.next())
                nc.vector.tensor_tensor(th[0:NH, :], gl, gu, ALU.subtract).then_inc(r_ok, 1)
                nc.vector.tensor_tensor(stack[0:NH, :], gi, gl, ALU.subtract).then_inc(dve_a, 1)
                dve.wait_ge(dve_a, ch.next())
                dve.wait_ge(r_ok, at(b, 1, 1))
                chunks = (NH, T - 1, P)
                nc.vector.tensor_tensor(ge[:, 0:LATE].rearrange("h (c s) -> h c s", s=P),
                                        th[0:NH, P:S].rearrange("h (c s) -> h c s", s=P),
                                        gu[:, P - 1:LATE:P].unsqueeze(2).to_broadcast(list(chunks)), ALU.add)
                nc.vector.tensor_tensor(gf[:, 0:LATE].rearrange("h (c s) -> h c s", s=P),
                                        stack[0:NH, 0:LATE].rearrange("h (c s) -> h c s", s=P),
                                        th[0:NH, P - 1:LATE:P].unsqueeze(2).to_broadcast(list(chunks)),
                                        ALU.add).then_inc(gate_dve, 1)
                between[1]()

            def split_parts(b, ch, use, whole):
                for n in range(HG):
                    dve.wait_ge(pa_free[(use + n) % 2], pa_done(b, use + n))
                nc.vector.tensor_scalar(kq_parts[:, HI, :, :], whole, split_scale[:, 0:1], None, ALU.mult).then_inc(dve_a, 1)
                dve.wait_ge(dve_a, ch.next())
                nc.vector.scalar_tensor_tensor(kq_parts[:, LO, :, :], whole, split_scale[:, 0:1], kq_parts[:, HI, :, :],
                                               ALU.mult, ALU.subtract).then_inc(dve_a, 1)
                dve.wait_ge(dve_a, ch.next())

            def stack_heads(stacked, order, h, done):
                for r, part in enumerate(order):
                    last = nc.vector.tensor_copy(stacked[r * DQ:(r + 1) * DQ, h::H4, :],
                                                 kq_parts[h * DQ:(h + 1) * DQ, part, :, :])
                last.then_inc(done, 1)

            def weigh_keys(b, chunks, src, free):
                n = len(chunks)
                nc.vector.tensor_tensor(ktok[:, chunks[0]:chunks[0] + n, :].rearrange("p c (h d) -> p c h d", d=DQ),
                                        src.rearrange("p (c h d) -> p c h d", c=n, d=DQ),
                                        gtok[:, chunks[0]:chunks[0] + n, ROW_G, :].unsqueeze(3).to_broadcast([P, n, NH, DQ]),
                                        ALU.mult).then_inc(free, 1)

            def keys_first(b):
                dve.wait_ge(ph_free, at(b, PH_USES, U_GT + 1))
                dve.wait_ge(ps_fill, at(b, sum(PS_USES), 1))
                weigh_keys(b, (0, 1), ps[:, 0, :], ps_free[0])

            def keys_last(b):
                dve.wait_ge(pa_fill, pa_filled(b, U_KLAST))
                weigh_keys(b, (2,), pa[:, U_KLAST % 2, 0:QK], pa_free[U_KLAST % 2])

            def chunk_decay(b):
                dve.wait_ge(w_loaded, at(b, 16 * NH, 16 * NH))
                nc.vector.tensor_copy(fcol[:, :, :], qw[:, :, P - 1::P]).then_inc(fcol_ok, 1)

            def state(b, j):
                dve.wait_ge(ph_fill, at(b, PH_USES, U_U + j + 1))
                nc.vector.tensor_tensor(cst[:, j, :, :].rearrange("p a (h v) -> p a h v", v=VA),
                                        ph[:, :, 0:H4 * VA].rearrange("p a (h v) -> p a h v", v=VA),
                                        own_head[:, :].unsqueeze(1).unsqueeze(3).to_broadcast([P, HG, H4, VA]),
                                        ALU.mult).then_inc(ph_free, 1)
                dve.wait_ge(ph_free, at(b, PH_USES, U_U + j + 1))
                if j == 1:
                    dve.wait_ge(fcol_ok, at(b, 1, 1))
                if j == 2:
                    dve.wait_ge(c_ok, at(b, T - 2, 1))
                if j >= 1:
                    for g in range(HG):
                        last = nc.vector.scalar_tensor_tensor(cst[:, j, g, :], cst[:, j - 1, g, :], fcol[:, g, j - 1:j],
                                                              cst[:, j, g, :], ALU.mult, ALU.add)
                    last.then_inc(c_ok, 1)

            def weigh(b, n):
                h = HEADS[n]
                dve.wait_ge(ps_fill, at(b, sum(PS_USES), n + 2))
                dve.wait_ge(d_ok, at(b, NH, h + 1))
                nc.vector.scalar_tensor_tensor(dec[:, h, :], ps[:, n % 2, :], split_scale[:, 1:2], dec[:, h, :],
                                               ALU.mult, ALU.mult).then_inc(ps_free[n % 2], 1)

            def head_stats(b, j, ch):
                if not (isinstance(b, int) and b == 0 and j == 0):
                    dve.wait_ge(hvar_ok, at(b, T, j))
                dve.wait_ge(ph_fill, at(b, PH_USES, U_H + j + 1))
                norm = ph[:, :, 0:H4 * VA].rearrange("p a (h v) -> p a h v", v=VA)[:, :, :, DHV]
                den_of = den[:, :].rearrange("p (a h) -> p a h", h=H4)
                nc.vector.tensor_tensor(den_of, norm, gtok[:, j, ROW_EM, :].rearrange("p (a h) -> p a h", h=H4), ALU.max)
                nc.vector.tensor_reduce(hsum[:, :].rearrange("p (a h) -> p a h", h=H4), heads(j), AX.X,
                                        ALU.add).then_inc(dve_a, 1)
                dve.wait_ge(dve_a, ch.next())
                nc.vector.scalar_tensor_tensor(den_of, norm, -1.0, den_of, ALU.mult, ALU.max)
                nc.vector.tensor_scalar(hsum[:, :], hsum[:, :], 1.0 / DHV, None, ALU.mult).then_inc(dve_a, 1)
                dve.wait_ge(dve_a, ch.next())
                nc.vector.tensor_scalar(den[:, :], den[:, :], MLSTM_EPS, None, ALU.add).then_inc(dve_a, 1)
                dve.wait_ge(dve_a, ch.next())
                nc.vector.tensor_tensor(by_head(cent[j % 2]), heads(j), per_head(hsum[:, :], DHV),
                                        ALU.subtract).then_inc(ph_free, 1)
                nc.vector.scalar_tensor_tensor(den[:, :], den[:, :], MLSTM_EPS, den[:, :], ALU.mult, ALU.mult).then_inc(dve_a, 1)
                dve.wait_ge(dve_a, ch.next())
                dve.wait_ge(sq_ok, at(b, T, j + 1))
                nc.vector.tensor_reduce(hsum[:, :], square.rearrange("p a (h v) -> p (a h) v", v=DHV), AX.X,
                                        ALU.add).then_inc(dve_a, 1)
                dve.wait_ge(dve_a, ch.next())
                if not (isinstance(b, int) and b == 0 and j == 0):
                    dve.wait_ge(hn_ok, at(b, T, j))
                nc.vector.scalar_tensor_tensor(hvar[:, :], hsum[:, :], 1.0 / DHV, den[:, :], ALU.mult,
                                               ALU.add).then_inc(hvar_ok, 1)

            def gated(b, j):
                use = U_HT[j]
                dve.wait_ge(pa_fill, pa_filled(b, use))
                if j == 0:
                    dve.wait_ge(sig_ok, at(b, 1, 1))
                    dve.wait_ge(qw_ok, at(b, 1, 1))
                if j >= 2:
                    dve.wait_ge(ho_lo, at(b, T, j - 1))
                nc.vector.scalar_tensor_tensor(hog[j % 2].rearrange("p (k s) -> p k s", s=P),
                                               pa[:, use % 2, :].rearrange("p (k s) -> p k s", s=P), H_SCALE,
                                               sigT[:, :, tok(j)], ALU.mult, ALU.mult).then_inc(pa_free[use % 2], 1)

            def residual(b, t, ch):
                use = U_Y[t]
                dve.wait_ge(pa_fill, pa_filled(b, use))
                if t == 0:
                    dve.wait_ge(res_loaded, at(b, 16, 16))
                nc.vector.scalar_tensor_tensor(xres[:, t, :], pa[:, use % 2, :], evac[:, W_OUT:W_OUT + 1], xres[:, t, :],
                                               ALU.mult, ALU.add).then_inc(pa_free[use % 2], 1)
                dve.wait_ge(pa_free[use % 2], pa_done(b, use))
                nc.vector.bn_stats(st2[:, t, :], xres[:, t, :]).then_inc(dve_a, 1)
                dve.wait_ge(dve_a, ch.next())
                if t == T - 1:
                    mean_var(st2, mean2, dif2, dev2, dve_a, ch)
                    nc.vector.tensor_tensor(ve2[:, :], dif2[:, :], dev2[:, :], ALU.add).then_inc(var2, 1)

            def norm2_apply(fb, tiles):
                dve.wait_ge(rstd2_ok, at(fb, 1, 1))
                for t in tiles:
                    dve.wait_ge(x1b_ok, at(fb, T, t + 1))
                    nc.vector.tensor_scalar(xres[:, t, :], xres[:, t, :], mean2[:, t:t + 1], rstd2[:, t:t + 1],
                                            ALU.subtract, ALU.mult).then_inc(xn2_ok, 1)

            def split2_lo(fb, ks):
                for k in ks:
                    use = U_T2 + k
                    dve.wait_ge(x2_hi, at(fb, KD, k + 1))
                    nc.vector.scalar_tensor_tensor(x2T[:, LO, k, :], pf[:, use % 2, :], X_SCALE, x2T[:, HI, k, :],
                                                   ALU.mult, ALU.subtract).then_inc(pf_free[use % 2], 1)

            def gelu_lo(fb, f):
                dve.wait_ge(g_hi, at(fb, NF, f + 1))
                nc.vector.scalar_tensor_tensor(gT[:, LO, f, :], g32[:, f % 2, :], wscale[:, W_GELU:W_GELU + 1],
                                               gT[:, HI, f, :], ALU.mult, ALU.subtract).then_inc(gs_ok, 1)

            def result(fb, t):
                use = U_F2 + t
                dve.wait_ge(pf_fill, at(fb, PF_USES, use + 1))
                dve.wait_ge(x1b_ok, at(fb, T, t + 1))
                nc.vector.scalar_tensor_tensor(x1b[:, t, :], pf[:, use % 2, :], winv[:, W_GELU:W_GELU + 1], x1b[:, t, :],
                                               ALU.mult, ALU.add).then_inc(pf_free[use % 2], 1)

            def sequence(b, fb, ahead):
                ca = Chain(b, DVE_A)
                run_f = fb is not None
                gate_decay(b, ca, [lambda: norm2_apply(fb, (0, 1)) if run_f else None,
                                   lambda: norm2_apply(fb, (2, 3)) if run_f else None])
                if ahead:
                    norm_stats(b + 1)
                    norm_apply(b + 1)
                split_parts(b, ca, U_K, kT[:, :, :])
                for h in range(H4):
                    stack_heads(kst, (HI, HI, LO, LO), h, k_ok)
                    if h == 1:
                        keys_first(b)
                        chunk_decay(b)
                dve.wait_ge(k_ok, at(b, H4, H4))
                split_parts(b, ca, U_Q, qT[:, :, :])
                for h in range(H4):
                    if run_f and h % 2 == 0:
                        split2_lo(fb, (h, h + 1))
                    stack_heads(qst(b), (HI, LO, HI, LO), h, kq_ok)
                keys_last(b)
                dve.wait_ge(kq_ok, at(b, H4, H4))
                if not run_f:
                    threshold(0)

                def hidden(*fs):
                    if run_f:
                        for f in fs:
                            gelu_lo(fb, f)

                hidden(0, 1)
                for n in range(NH):
                    if not run_f:
                        ternary(0, (2 * n, 2 * n + 1))
                    weigh(b, n)
                    hidden(2 + n)
                    if n == 3:
                        state(b, 0)
                state(b, 1)
                hidden(10, 11, 12)
                state(b, 2)
                hidden(13, 14, 15)

                def done(t):
                    if run_f:
                        result(fb, t)

                def ternary2(*units):
                    if not run_f:
                        ternary(1, units)

                done(0)
                head_stats(b, 0, ca)
                if not run_f:
                    threshold(1)
                ternary2(0, 1, 2)
                head_stats(b, 1, ca)
                gated(b, 0)
                ternary2(3, 4, 5)
                done(1)
                head_stats(b, 2, ca)
                gated(b, 1)
                ternary2(6, 7, 8)
                head_stats(b, 3, ca)
                done(2)
                gated(b, 2)
                ternary2(9, 10, 11)
                residual(b, 0, ca)
                if ahead:
                    split_lo(b + 1, (0, 1))
                gated(b, 3)
                ternary2(12, 13)
                residual(b, 1, ca)
                if ahead:
                    split_lo(b + 1, (2, 3))
                ternary2(14, 15)
                residual(b, 2, ca)
                done(3)
                residual(b, 3, ca)
                assert ca.n == DVE_A, ca.n

            norm_stats(0)
            norm_apply(0)
            largest(W_QK)
            split_lo(0, range(KD))
            largest(W_V)
            largest(W_O)
            largest(W_OUT)
            scales()
            weights_lo()
            sequence(0, None, True)
            with dve.Fori(1, B - 1) as b:
                sequence(b, b - 1, True)
            sequence(B - 1, B - 2, False)
            norm2_apply(B - 1, range(T))
            split2_lo(B - 1, range(KD))
            for f in range(NF):
                gelu_lo(B - 1, f)
            for t in range(T):
                result(B - 1, t)

        @block.tensor
        def _(pe):
            PARTS = ((HI, HI), (HI, LO), (LO, HI))

            def weights():
                pe.wait_ge(s_ident, 1)
                pe.wait_ge(s_amax, 1)
                for n in range(2):
                    pe.wait_ge(pa_free[n], pa_done(*x_use(0, 2 + n)))
                for n in range(W_BANKS):
                    g, k = divmod(n, KD)
                    bank = wbank[n % 4]
                    if n >= 4:
                        pe.wait_ge(s_wfree[n % 4], n // 4)
                    for i in range(4):
                        if g < 4:
                            last = nc.tensor.transpose(bank[:, tok(i)], rows[:, 4 * g + i, tok(k)], ident[:, :])
                        else:
                            last = nc.tensor.transpose(bank[:, i * GROWS:(i + 1) * GROWS], th[:, tok(i)],
                                                       ident[0:GROWS, 0:GROWS])
                    last.then_inc(s_wfill, 1)
                for n in range(4):
                    pe.wait_ge(s_wfree[n], W_READ[n])

            def ternary_transpose(w, pairs):
                for q in pairs:
                    n = UNITS // 2 * w + q
                    pe.wait_ge(s_tern, 2 * n + 2)
                    if n >= 2:
                        pe.wait_ge(pf_free[q % 2], n // 2)
                    for i in range(2):
                        for k in range(KD):
                            last = nc.tensor.transpose(pair_bank(q)[:, i, k, :], tern(2 * q + i)[:, tok(k)], ident16[:, :])
                    last.then_inc(s_ufill, 1)

            def take_pa(b, use):
                count = pa_taken(b, use)
                if not (isinstance(count, int) and count == 0):
                    pe.wait_ge(pa_free[use % 2], count)
                return pa[:, use % 2, :]

            def take_pf(fb, use):
                pe.wait_ge(pf_free[use % 2], at(fb, PF, PF_SETUP + use // 2))
                return pf[:, use % 2, :]

            def take_ph(b, use):
                if not (isinstance(b, int) and b == 0 and use == 0):
                    pe.wait_ge(ph_free, at(b, PH_USES, use))

            def transposes(b, ks):
                for k in ks:
                    bank = take_pa(*x_use(b, k))
                    for t in range(T):
                        if k == 0:
                            pe.wait_ge(xn_ok, at(b, T, t + 1))
                        last = nc.tensor.transpose(bank[:, tok(t)], xin[:, t, tok(k)], ident[:, :])
                    last.then_inc(pa_fill, 1)

            def gates(b):
                bank = take_pa(b, U_GATE)
                for k in range(KD):
                    when, use = x_use(b, k)
                    pe.wait_ge(pa_free[use % 2], pa_done(when, use))
                    for n, (ws, xs) in enumerate(PARTS):
                        last = nc.tensor.matmul(bank[0:GROWS, :], wgT[:, ws, k, :], xT[:, xs, k, :],
                                                start=(k == 0 and n == 0), stop=(k == KD - 1 and n == 2))
                last.then_inc(pa_fill, 1)

            def features(b, use, col):
                bank = take_pa(b, use)
                for k in range(KD):
                    for n, (ws, xs) in enumerate(PARTS):
                        last = nc.tensor.matmul(bank, wT[:, ws, k, col:col + P], xT[:, xs, k, :],
                                                start=(k == 0 and n == 0), stop=(k == KD - 1 and n == 2))
                last.then_inc(pa_fill, 1)

            def tokens(b, use, src, t, col):
                bank = take_pa(b, use)
                for k in range(KD):
                    for n, (xs, ws) in enumerate(PARTS):
                        last = nc.tensor.matmul(bank, src[:, xs, k, tok(t)], wT[:, ws, k, col:col + D],
                                                start=(k == 0 and n == 0), stop=(k == KD - 1 and n == 2))
                last.then_inc(pa_fill, 1)

            def gate_columns(b):
                take_ph(b, U_GT)
                pe.wait_ge(gate_act, at(b, 5, 5))
                for t in range(T):
                    last = nc.tensor.transpose(ph[:, 0, t * P:t * P + STACK], stack[:, tok(t)],
                                               ident[0:STACK, 0:STACK])
                last.then_inc(ph_fill, 1)

            def key_tokens(chunk, bank):
                for g in range(HG):
                    last = nc.tensor.transpose(bank[:, tok(g)], kT[:, g, tok(chunk)], ident[:, :])
                return last

            def key_tokens_first(b):
                for n in range(HG):
                    pe.wait_ge(pa_free[(U_K + n) % 2], pa_done(b, U_K + n))
                if not (isinstance(b, int) and b == 0):
                    pe.wait_ge(ps_free[0], at(b, PS_USES[0], 0))
                key_tokens(0, ps[:, 0, 0:QK])
                key_tokens(1, ps[:, 0, QK:2 * QK]).then_inc(ps_fill, 1)

            def key_tokens_last(b):
                key_tokens(2, take_pa(b, U_KLAST)).then_inc(pa_fill, 1)

            def outer(b, j):
                take_ph(b, U_U + j)
                if j == 2:
                    pe.wait_ge(pa_free[U_KLAST % 2], pa_done(b, U_KLAST))
                if j == 0:
                    pe.wait_ge(ps_free[0], at(b, PS_USES[0], 1))
                    for t in (T - 2, T - 1):
                        pe.wait_ge(pa_free[(U_V + t) % 2], pa_done(b, U_V + t))
                for g in range(HG):
                    last = nc.tensor.matmul(ph[:, g, 0:H4 * VA], ktok[:, j, tok(g)],
                                            vaug[:, j, g * H4:(g + 1) * H4, :], start=True, stop=True)
                last.then_inc(ph_fill, 1)

            def scores(b, n):
                if not (isinstance(b, int) and b == 0 and n == 1):
                    pe.wait_ge(ps_free[n % 2], ps_done(b, n) - 1)
                if n % HG == 0:
                    pe.wait_ge(kq_ok, at(b, H4, n // HG + 1))
                for j in range(T):
                    last = nc.tensor.matmul(ps[:, n % 2, tok(j)], kst[:, HEADS[n], tok(j)], qst(b)[:, HEADS[n], tok(j)],
                                            start=True, stop=True)
                last.then_inc(ps_fill, 1)

            def chunk(b, j):
                take_ph(b, U_H + j)
                if j == 0:
                    for n in range(2):
                        pe.wait_ge(ps_free[n], at(b, PS_USES[n], PS_USES[n]))
                if j == 1:
                    pe.wait_ge(qw_ok, at(b, 1, 1))
                    pe.wait_ge(ph_free, at(b, PH_USES, U_U + 1))
                if j >= 2:
                    pe.wait_ge(c_ok, at(b, T - 2, j - 1))
                for g in range(HG):
                    if j > 0:
                        nc.tensor.matmul(ph[:, g, 0:H4 * VA], qw[:, g, tok(j - 1)], cst[:, j - 1, g, :],
                                         start=True, stop=False, skip_group_check=True)
                    for i in range(H4):
                        h = g * H4 + i
                        last = nc.tensor.matmul(ph[:, g, i * VA:(i + 1) * VA], dec[:, h, tok(j)], vaug[:, j, h, :],
                                                start=(j == 0 and i == 0), stop=(i == H4 - 1), skip_group_check=True)
                last.then_inc(ph_fill, 1)

            def head_transposes(b, j):
                bank = take_pa(b, U_HT[j])
                pe.wait_ge(hn_ok, at(b, T, j + 1))
                for k in range(KD):
                    last = nc.tensor.transpose(bank[:, tok(k)], cent[j % 2][:, tok(k)], ident[:, :])
                last.then_inc(pa_fill, 1)

            def project(b, t):
                pe.wait_ge(ho_lo, at(b, T, t + 1))
                tokens(b, U_Y[t], hoT, t, C_OUT)

            def transposes2(fb, ks):
                for k in ks:
                    bank = take_pf(fb, U_T2 + k)
                    for t in range(T):
                        if k == 0:
                            pe.wait_ge(xn2_ok, at(fb, T, t + 1))
                        last = nc.tensor.transpose(bank[:, tok(t)], xres[:, t, tok(k)], ident[:, :])
                    last.then_inc(pf_fill, 1)

            def up(fb, f):
                bank = take_pf(fb, U_F1 + f)
                for k in range(KD):
                    if f == 0:
                        pe.wait_ge(pf_free[(U_T2 + k) % 2], pf_done(fb, U_T2 + k))
                    for part in (HI, LO):
                        last = nc.tensor.matmul(bank, w1T[:, k, tok(f)], x2T[:, part, k, :],
                                                start=(k == 0 and part == HI), stop=(k == KD - 1 and part == LO))
                last.then_inc(pf_fill, 1)

            def down(fb, t, fs):
                bank = take_pf(fb, U_F2 + t) if fs[0] == 0 else pf[:, (U_F2 + t) % 2, :]
                for f in fs:
                    if t == 0 and (f % 4 == 0 or f >= NF - 4):
                        pe.wait_ge(gs_ok, at(fb, NF, max(f + 1, min(f + 4, NF - 4))))
                    for part in (HI, LO):
                        last = nc.tensor.matmul(bank, gT[:, part, f, tok(t)], w2T[:, f, :],
                                                start=(f == 0 and part == HI), stop=(f == NF - 1 and part == LO))
                if fs[-1] == NF - 1:
                    last.then_inc(pf_fill, 1)

            FIRST, SECOND, ALL = range(NF // 2), range(NF // 2, NF), range(NF)
            QUARTER = [range(NF // 4 * i, NF // 4 * (i + 1)) for i in range(4)]

            def sequence(b, fb, ahead):
                def hidden(*fs):
                    if fb is not None:
                        for f in fs:
                            up(fb, f)

                def model(t, fs):
                    if fb is not None:
                        down(fb, t, fs)

                gates(b)
                for t in range(T):
                    tokens(b, U_V + t, xT, t, C_V)
                for n in range(HG):
                    features(b, U_K + n, C_QK + QK + n * P)
                gate_columns(b)
                for n in range(HG):
                    features(b, U_Q + n, C_QK + n * P)
                key_tokens_first(b)
                for n in range(KD):
                    features(b, U_O + n, C_O + n * P)
                    if fb is not None and n in (1, 2):
                        transposes2(fb, (2 * n - 2, 2 * n - 1))
                key_tokens_last(b)
                outer(b, 0)
                hidden(0, 1)
                scores(b, 0)
                for n in range(NH):
                    if n != 1:
                        scores(b, max(n, 1))
                    if fb is None:
                        ternary_transpose(0, (n,))
                    hidden(2 + n)
                outer(b, 1)
                hidden(10, 11, 12)
                outer(b, 2)
                hidden(13, 14, 15)
                def ternary2(*pairs):
                    if fb is None:
                        ternary_transpose(1, pairs)

                model(0, ALL)
                chunk(b, 0)
                model(1, FIRST)
                chunk(b, 1)
                ternary2(0)
                model(1, SECOND)
                head_transposes(b, 0)
                chunk(b, 2)
                ternary2(1, 2)
                model(2, FIRST)
                head_transposes(b, 1)
                chunk(b, 3)
                ternary2(3)
                model(2, SECOND)
                head_transposes(b, 2)
                project(b, 0)
                ternary2(4, 5)
                if ahead:
                    transposes(b + 1, (0,))
                model(3, QUARTER[0])
                if ahead:
                    transposes(b + 1, (1,))
                model(3, QUARTER[1])
                head_transposes(b, 3)
                project(b, 1)
                ternary2(6)
                if ahead:
                    transposes(b + 1, (2,))
                model(3, QUARTER[2])
                if ahead:
                    transposes(b + 1, (3,))
                model(3, QUARTER[3])
                project(b, 2)
                ternary2(7)
                project(b, 3)

            transposes(0, range(KD))
            weights()
            sequence(0, None, True)
            with pe.Fori(1, B - 1) as b:
                sequence(b, b - 1, True)
            sequence(B - 1, B - 2, False)
            transposes2(B - 1, range(KD))
            for f in range(NF):
                up(B - 1, f)
            for t in range(T):
                down(B - 1, t, ALL)


_INS = ["x", "Wq", "Wk", "Wv", "Wog", "Wig", "big", "Wfg", "bfg", "gamma", "Wout"]
_FFN = ["w1", "b1", "w2", "b2"]


def kernel(**inputs):
    import numpy as np
    import concourse.bacc as bacc
    from concourse.bass_utils import run_bass_kernel_spmd

    nc = bacc.Bacc("TRN2", target_bir_lowering=False, num_devices=1)
    arrays, args = {}, []
    for name in [f"L0_attn_{n}" for n in _INS] + [f"L0_ffn_{n}" for n in _FFN]:
        a = np.ascontiguousarray(inputs[name])
        arrays[name] = a
        args.append(nc.dram_tensor(name, a.shape, mybir.dt.from_np(a.dtype), kind="ExternalInput").ap())
    shape = inputs["L0_attn_x"].shape
    out = nc.dram_tensor("out", shape, F32, kind="ExternalOutput").ap()
    block_program(nc, *args, out)
    return run_bass_kernel_spmd(nc, [arrays], core_ids=[0]).results[0]["out"]
```

```python
from contextlib import ExitStack

import concourse.bass as bass
from concourse import mybir

F32 = mybir.dt.float32
F16 = mybir.dt.float16
I32 = mybir.dt.int32
ALU = mybir.AluOpType
ACT = mybir.ActivationFunctionType
AX = mybir.AxisListType
RMAX = bass.bass_isa.ReduceOp.max
RADD = bass.bass_isa.ReduceOp.add

P = 128
CAP = 15.0
MLSTM_EPS = 1e-6
LN_EPS = 1e-5
MASKED = -30000.0
X_SCALE = 2.0 ** 11
H_SCALE = 2.0 ** 12
TOP = 2.0 ** 15
TINY = 2.0 ** -100
HI, LO = 0, 1


def at(b, per, k):
    return b * per + k


class Chain:

    def __init__(self, b, per):
        self.b, self.per, self.n = b, per, 0

    def next(self):
        self.n += 1
        assert self.n <= self.per, self.n
        return at(self.b, self.per, self.n)


DVE_L, DVE_A = 3, 6 + 4 + 4 * 5 + 4 + 2
POOL_A = 4


def block_program(nc, x, Wq, Wk, Wv, Wog, Wig, big, Wfg, bfg, gamma, Wout, w1, b1, w2, b2, out):
    B, S, D = x.shape
    QK, DV_ALL = Wq.shape[0], Wv.shape[0]
    NH, DHV = gamma.shape
    DQ = QK // NH
    FF = w1.shape[0]
    T = S // P
    KD = D // P
    NF = FF // P
    HG = NH * DQ // P
    H4 = NH // HG
    VA = DHV + 1
    GATE_F = 32
    GROWS = GATE_F + NH
    ROW_C, ROW_EM, ROW_G = range(3)
    STACK = 2 * 32 + NH
    UNITS = FF * D // (P * D)
    LATE = S - P
    G_V, G_QK, G_O, G_OUT = range(4)
    C_V, C_QK, C_O, C_OUT = (g * D for g in range(4))
    W_GATE, W_V, W_QK, W_O, W_OUT, W_GELU, GAMMA = range(7)
    EARLY, LATER = slice(W_GATE, W_QK), slice(W_QK, GAMMA)
    assert (T, KD, HG, QK, DV_ALL) == (4, 4, 2, 256, D)

    HEADS = [g * H4 + h for h in range(H4) for g in range(HG)]
    U_GATE, U_V, U_K, U_Q, U_O, U_KLAST = 0, 1, 5, 7, 9, 13
    U_Y = 14
    X_PAIRS = (U_Y, U_Y)
    PA_USES = U_Y + T
    PS_USES = (1 + NH // 2, NH // 2)
    U_F1, U_F2 = 0, NF
    U_T2 = -KD
    PF_USES = NF + T
    U_GT, U_U, U_H = 0, 1, T
    PH_USES = 2 * T

    gate_r = nc.dram_tensor("gate_r", (B, NH, S), F32, kind="Internal").ap()
    gate_w = nc.dram_tensor("gate_w", (B, NH, LATE), F32, kind="Internal").ap()

    with ExitStack() as ctx:
        def sb(name, shape, dt=F32):
            return ctx.enter_context(nc.sbuf_tensor(name, shape, dt))

        def pb(name):
            return ctx.enter_context(nc.psum_tensor(name, [P, 2, 512], F32))

        def sem(name):
            return ctx.enter_context(nc.semaphore(name))

        wT = sb("wT", [P, 2, KD, 4 * D], F16)
        wgT = sb("wgT", [P, KD, 2, P // 2], F16)
        w1T = sb("w1T", [P, KD, FF], F16)
        w2T = sb("w2T", [P, NF, D], F16)
        b1c = sb("b1c", [P, NF])
        b2r = sb("b2r", [P, D])
        gate_bias = sb("gate_bias", [GROWS, 1])
        ident = sb("ident", [P, P])
        ident16 = sb("ident16", [P, P], F16)
        causal = sb("causal", [P, P])
        own_head = sb("own_head", [P, H4])
        one = sb("one", [P, 1])
        half = sb("half", [P, NH])
        peak = sb("peak", [P, 7])
        bound = sb("bound", [P, 7])
        floor2 = sb("floor2", [P, 6])
        wscale = sb("wscale", [P, 6])
        winv = sb("winv", [P, 6])
        gcol = sb("gcol", [P, KD])
        split_scale = sb("split_scale", [P, 2])
        evac = sb("evac", [P, 6])
        asum1, asum2 = sb("asum1", [P, UNITS // 2]), sb("asum2", [P, KD])
        w12 = sb("w12", [P, 4, 2])
        xin = sb("xin", [P, T, D])
        xres = sb("xres", [P, T, D])
        x1b = sb("x1b", [P, T, D])
        xT = sb("xT", [P, 2, T, KD, P], F16)
        hoT = sb("hoT", [P, T, 2, KD, P], F16)
        x2T = sb("x2T", [P, 2, T, KD, P], F16)
        qT = sb("qT", [P, HG, S])
        kT = sb("kT", [P, HG, S])
        qw = sb("qw", [P, HG, LATE])
        fcol = sb("fcol", [P, HG, T - 1])
        vaug = sb("vaug", [P, T, NH, VA])
        sig = sb("sig", [P, T, D])
        dec = sb("dec", [P, NH, S])
        ktok = sb("ktok", [P, T - 1, QK])
        cst = sb("cst", [P, T - 1, HG, H4 * VA])
        g32 = sb("g32", [P, 2, S])
        gT = sb("gT", [P, 2, NF, S], F16)
        stack = sb("stack", [STACK, S])
        gtok = sb("gtok", [P, T, 3, NH])
        stats = sb("stats", [P, T, 6])
        mean, dif, dev, ve, rstd = (sb(n, [P, T]) for n in ("mean", "dif", "dev", "ve", "rstd"))
        den, hsum, hvar, hinv = (sb(n, [P, NH]) for n in ("den", "hsum", "hvar", "hinv"))
        asums, totals, thr, nthr = (w12[:, i, :] for i in range(4))
        gu, gl = g32[0:NH, 0, :], g32[0:NH, 1, :]
        gi, gf = kT[0:NH, 0, :], kT[0:NH, 1, :]
        th, ge = qT[0:GROWS, 0, :], qT[0:NH, 1, :]
        cent = [kT[:, i, :] for i in range(2)]
        head_parts = [qT[:, i, :].bitcast(F16).rearrange("p (a d) -> p a d", a=2) for i in range(2)]
        square = ktok[:, 0:2, :]
        kq_parts = (cst[:, :, :, :].rearrange("p a g n -> p (a g n)")[:, 0:HG * S].bitcast(F16)
                    .rearrange("p (a g s) -> p a g s", a=2, g=HG))
        kst = hoT[:, :, :, :, :].rearrange("p t a k c -> p (t a) (k c)")

        def qst(b):
            return xres[:, :, :].bitcast(F16).rearrange("p t (a s) -> p (t a) s", s=S) if isinstance(b, int) and b == 0 \
                else gT[:, HI, NF - NH:NF, :]

        parts1, parts2 = (gT[:, LO, n * NF // 2:(n + 1) * NF // 2, :].rearrange("p (a t) d -> p a t d", a=2) for n in (1, 0))
        rows = gT[:, :, :, :].bitcast(F32).rearrange("p a n s -> p (a n s)").rearrange("p (n s) -> p n s", s=D)

        pa, pf, ps, ph = pb("pa"), pb("pf"), pb("ps"), pb("ph")

        s_wload = [sem(f"s_wload{g}") for g in range(5)]
        s_bias, s_small = sem("s_bias"), sem("s_small")
        s_w12 = [[sem(f"s_w{w}load{n}") for n in range(4)] for w in (1, 2)]
        s_w2early = [sem(f"s_w2early{n}") for n in range(4)]
        s_const = sem("s_const")
        s_ident = sem("s_ident")
        s_pchain = sem("s_pchain")
        s_dchain = sem("s_dchain")
        s_sums = sem("s_sums")
        s_peak = sem("s_peak")
        s_allmax = sem("s_allmax")
        s_bound = sem("s_bound")
        s_rbound = sem("s_rbound")
        s_scales = sem("s_scales")
        s_whi = sem("s_whi")
        s_wfill = sem("s_wfill")
        s_wfree = [sem(f"s_wfree{n}") for n in range(4)]
        s_abs = sem("s_abs")
        s_asum = sem("s_asum")
        s_allsum = sem("s_allsum")
        s_thr = sem("s_thr")
        s_low = [sem("s_low_pool"), sem("s_low_dve")]
        s_tern = sem("s_tern")
        s_ufill = sem("s_ufill")
        s_sign = sem("s_sign")
        s_low2, s_tern2 = sem("s_low2"), sem("s_tern2")
        s_ufill2 = sem("s_ufill2")
        xT_loaded, x2T_loaded = sem("xT_loaded"), sem("x2T_loaded")
        hoT_loaded = [sem(f"hoT_loaded{t}") for t in range(T)]
        x_loaded = sem("x_loaded")
        res_loaded, res_last = sem("res_loaded"), sem("res_last")
        r_stored, w_stored = sem("r_stored"), sem("w_stored")
        r_loaded = [sem(f"r_loaded{g}") for g in range(HG)]
        w_loaded = sem("w_loaded")
        out_stored = [sem(f"out_stored{t}") for t in range(T)]
        pa_fill, pf_fill, ps_fill, ph_fill = sem("pa_fill"), sem("pf_fill"), sem("ps_fill"), sem("ph_fill")
        pa_free = [sem("pa_free0"), sem("pa_free1")]
        pf_free = [sem("pf_free0"), sem("pf_free1")]
        ps_free = [sem("ps_free0"), sem("ps_free1")]
        ph_free = sem("ph_free")
        dve_l, dve_a = sem("dve_l"), sem("dve_a")
        pool_a = sem("pool_a")
        var1, var2 = sem("var1"), sem("var2")
        rstd1_ok, rstd2_ok = sem("rstd1_ok"), sem("rstd2_ok")
        xn_ok, xn2_ok = sem("xn_ok"), sem("xn2_ok")
        x_hi, x2t_hi = sem("x_hi"), sem("x2t_hi")
        part1_hi, part2_hi = sem("part1_hi"), sem("part2_hi")
        part1_ok, part2_ok = sem("part1_ok"), sem("part2_ok")
        gate_lo, tanh_ok = sem("gate_lo"), sem("tanh_ok")
        gate_dve, gate_act = sem("gate_dve"), sem("gate_act")
        r_ok = sem("r_ok")
        masked = sem("masked")
        d_ok = sem("d_ok")
        qw_ok, fcol_ok = sem("qw_ok"), sem("fcol_ok")
        k_ok, kq_ok = sem("k_ok"), sem("kq_ok")
        c_ok = sem("c_ok")
        sq_ok = sem("sq_ok")
        hvar_ok = sem("hvar_ok")
        hn_ok = sem("hn_ok")
        gated_ok = sem("gated_ok")
        ho_hi = sem("ho_hi")
        ho_lo = [sem(f"ho_lo{t}") for t in range(T)]
        x1b_ok = sem("x1b_ok")
        g_hi, gs_ok = sem("g_hi"), sem("gs_ok")
        sig_ok = sem("sig_ok")

        def pa_index(b, use):
            if isinstance(b, int) and b == 0:
                return KD + use + 2 * sum(use >= pair for pair in X_PAIRS)
            return at(b, PA_USES, 2 * KD + use)

        def pa_filled(b, use):
            return pa_index(b, use) + 1

        def pa_taken(b, use):
            if isinstance(b, int) and b == 0:
                return pa_index(b, use) // 2
            return at(b, PA_USES // 2, KD + use // 2)

        def pa_done(b, use):
            return pa_taken(b, use) + 1

        def x_index(b, k):
            return k if b == 0 else KD + X_PAIRS[k // 2] + k

        def ps_done(b, n):
            return at(b, PS_USES[n % 2], PS_USES[n % 2] - NH // 2 + n // 2 + 1)

        PF = PF_USES // 2
        PF_W1, PF_W2 = UNITS // 4, UNITS // 2
        PF_SETUP = PF_W1 + PF_W2

        def pf_index(fb, use):
            return use + (KD if isinstance(fb, int) and fb == B - 1 else 0)

        def pf_filled(fb, use):
            return at(fb, PF_USES, pf_index(fb, use) + 1)

        def pf_taken(fb, use):
            return at(fb, PF, PF_SETUP + pf_index(fb, use) // 2)

        def pf_done(fb, use):
            return at(fb, PF, PF_SETUP + pf_index(fb, use) // 2 + 1)

        def tok(t):
            return slice(t * P, (t + 1) * P)

        HALVES = (slice(0, T // 2), slice(T // 2, T))
        RES_TILES = (slice(0, T // 2), slice(T // 2, T - 1), slice(T - 1, T))

        def by_tile(bank):
            return bank.rearrange("p (t c) -> p t c", c=P)

        def per_head(ap, n):
            return ap.rearrange("p (a h) -> p a h", h=H4).unsqueeze(3).to_broadcast([P, HG, H4, n])

        def heads(j):
            return ph[:, :, 0:H4 * VA].rearrange("p a (h v) -> p a h v", v=VA)[:, :, :, 0:DHV]

        def by_head(ap):
            return ap.rearrange("p (a h v) -> p a h v", a=HG, h=H4)

        wbank = [ps[:, 0, :], ps[:, 1, :], pf[:, 0, :], pf[:, 1, :]]
        USES_V, USE_GATE, USES_QK, USES_O, USES_OUT = range(4), 4, range(5, 9), range(9, 13), range(13, 17)

        def group_rows(g):
            return x1b[:, :, :] if g == G_OUT else rows[:, 4 * g:4 * g + 4, :]

        def weight_use(n):
            return (None, None) if n == USE_GATE else divmod(n - (n > USE_GATE), KD)

        def w_bank(n):
            return n % 2 if n in USES_OUT else n % 4

        def w_taken(n):
            return sum(w_bank(m) == w_bank(n) for m in range(n))

        def early_w2(n):
            return (dec[:, 0:T, :], dec[:, T:2 * T, :], xres[:, :, :],
                    x2T[:, :, :, :, :].bitcast(F32).rearrange("p a t k c -> p (a t k c)").rearrange("p (t d) -> p t d", d=D))[n]

        def tern(u):
            return x2T[:, HI, u % 4, :, :].rearrange("p k c -> p (k c)")

        def low(u):
            return x2T[:, LO, u % 4, :, :].rearrange("p k c -> p (k c)")

        def pair_bank(q):
            return pf[:, q % 2, :].bitcast(F16).rearrange("p (u k c) -> p u k c", u=2, c=P)

        def load_w1(engine, n):
            engine.dma_start(rows[:, 4 * n:4 * n + 4, :],
                             w1.rearrange("(n p) d -> p n d", p=P)[:, 4 * n:4 * n + 4, :]).then_inc(s_w12[0][n], 16)

        block = ctx.enter_context(nc.Block())

        @block.sync
        def _(sp):
            sp.dma_start(xin[:, :, :], x[0].rearrange("(t p) d -> p t d", p=P)).then_inc(x_loaded, 16)
            for g, parts in enumerate(((Wv,), (Wq, Wk), (Wog,), (Wout,))):
                n = 0
                for w in parts:
                    k = w.shape[0] // P
                    sp.dma_start(group_rows(g)[:, n:n + k, :], w.rearrange("(n p) d -> p n d", p=P)).then_inc(s_wload[g], 16)
                    n += k
                if g == G_V:
                    sp.wait_ge(s_const, 1)
                    sp.dma_start(th[0:NH, :], Wig).then_inc(s_wload[4], 16)
                    sp.dma_start(th[GATE_F:GROWS, :], Wfg).then_inc(s_wload[4], 16)
                    sp.dma_start(gate_bias[0:NH, :], big.unsqueeze(1)).then_inc(s_bias, 16)
                    sp.dma_start(gate_bias[GATE_F:GROWS, :], bfg.unsqueeze(1)).then_inc(s_bias, 16)
            sp.dma_start(gcol[:, :], gamma.rearrange("h v -> (h v)").rearrange("(k p) -> p k", p=P),
                         allow_slow_non_contiguous=True).then_inc(s_small, 16)
            sp.dma_start(b1c[:, :], b1.rearrange("(n p) -> p n", p=P),
                         allow_slow_non_contiguous=True).then_inc(s_small, 16)
            sp.dma_start(b2r[:, :], b2.partition_broadcast(P)).then_inc(s_small, 16)
            for n in range(4):
                if n == 3:
                    load_w1(sp, G_OUT)
                sp.dma_start(early_w2(n), w2.rearrange("(n p) (c d) -> p n c d", p=P, d=D)[:, n, :, :]).then_inc(s_w2early[n], 16)

            def residual(b, tiles):
                if isinstance(b, int) and b == 0:
                    sp.wait_ge(ps_fill, sum(PS_USES))
                else:
                    sp.wait_ge(part2_ok, at(b - 1, 2, 2))
                sp.dma_start(xres[:, tiles, :], x[b].rearrange("(t p) d -> p t d", p=P)[:, tiles, :]
                             ).then_inc(res_last if tiles == RES_TILES[2] else res_loaded, 16)

            def gate_rows(b):
                sp.wait_ge(r_ok, at(b, 1, 1))
                sp.dma_start(gate_r[b], th[0:NH, :]).then_inc(r_stored, 16)
                sp.wait_ge(gate_act, at(b, 5, 4))
                sp.dma_start(gate_w[b], ge[:, 0:LATE]).then_inc(w_stored, 16)
                if not (isinstance(b, int) and b == 0):
                    sp.wait_ge(ph_fill, at(b, PH_USES, 0))
                sp.wait_ge(r_stored, at(b, 16, 16))
                for g in range(HG):
                    sp.dma_start(dec[:, g * H4:(g + 1) * H4, :],
                                 gate_r[b, g * H4:(g + 1) * H4, :].rearrange("h s -> (h s)").partition_broadcast(P)
                                 .rearrange("p (h s) -> p h s", s=S)).then_inc(r_loaded[g], 16)
                sp.wait_ge(w_stored, at(b, 16, 16))
                for h in range(H4):
                    for g in range(HG):
                        sp.dma_start(qw[h * DQ:(h + 1) * DQ, g, :],
                                     gate_w[b, g * H4 + h, :].partition_broadcast(DQ)).then_inc(w_loaded, 16)

            def next_x(b):
                sp.dma_start(xin[:, :, :], x[b + 1].rearrange("(t p) d -> p t d", p=P)).then_inc(x_loaded, 16)

            def transpose_x2(fb):
                residual(fb + 1, RES_TILES[0])
                sp.dma_start(x2T[:, :, :, :, :].rearrange("p a t k c -> p (a t k) c"),
                             parts2.rearrange("p a t d -> p (a t d)"), transpose=True).then_inc(x2T_loaded, 16)

            def transpose_x(b):
                sp.wait_ge(part1_ok, at(b, 1, -1))
                sp.wait_ge(pa_fill, pa_filled(b - 1, U_O + KD - 1))
                residual(b - 1, RES_TILES[1])
                sp.dma_start(xT[:, :, :, :, :].rearrange("p a t k c -> p (a t k) c"),
                             parts1.rearrange("p a t d -> p (a t d)"), transpose=True).then_inc(xT_loaded, 16)

            def store(fb, t, wait=True):
                if wait:
                    result_ready(fb, t)
                sp.dma_start(out[fb, tok(t), :], x1b[:, t, :]).then_inc(out_stored[t], 16)

            def result_ready(fb, t):
                use = U_F2 + t
                sp.wait_ge(pf_free[use % 2], pf_done(fb, use))

            def heads_out(b, fb):
                for j in range(T):
                    if fb is not None and j < T - 1:
                        result_ready(fb, j)
                    sp.wait_ge(ho_lo[j], at(b, 1, 1))
                    if j == T - 1:
                        residual(b, RES_TILES[2])
                    elif fb is not None:
                        store(fb, j, wait=False)
                    sp.dma_start(hoT[:, j, :, :, :].rearrange("p a k c -> p (a k) c"),
                                 head_parts[j % 2].rearrange("p a d -> p (a d)"),
                                 transpose=True).then_inc(hoT_loaded[j], 16)
                if fb is not None:
                    store(fb, T - 1)

            sp.wait_ge(pa_fill, x_index(0, KD - 1) + 1)
            next_x(0)
            gate_rows(0)
            for n in range(4):
                sp.wait_ge(s_tern, 4 * (n + 1))
                sp.dma_start(rows[:, 4 * n:4 * n + 4, :],
                             w2.rearrange("(n p) (c d) -> p n c d", p=P, d=D)[:, n, :, :]).then_inc(s_w12[1][n], 16)
            residual(0, RES_TILES[0])
            residual(0, RES_TILES[1])
            heads_out(0, None)
            sp.wait_ge(pa_fill, x_index(1, KD - 1) + 1)
            with sp.Fori(1, B - 1) as b:
                next_x(b)
                gate_rows(b)
                transpose_x2(b - 1)
                transpose_x(b + 1)
                heads_out(b, b - 1)
            gate_rows(B - 1)
            transpose_x2(B - 2)
            residual(B - 1, RES_TILES[1])
            heads_out(B - 1, B - 2)
            for t in range(T):
                store(B - 1, t)
            for t in range(T):
                sp.wait_ge(out_stored[t], 16 * B)

        @block.gpsimd
        def _(pool):
            nc.gpsimd.memset(gate_bias[:, :], 0.0)
            nc.gpsimd.memset(peak[:, :], 0.0)
            nc.gpsimd.memset(th, 0.0).then_inc(s_const, 1)
            nc.gpsimd.memset(wgT[:, :, :, :], 0.0)
            nc.gpsimd.memset(ident[:, :], 0.0)
            nc.gpsimd.memset(causal[:, :], 0.0)
            nc.gpsimd.memset(own_head[:, :], 1.0)
            nc.gpsimd.memset(one[:, :], 1.0)
            nc.gpsimd.memset(stack[:, :], 0.0)
            nc.gpsimd.memset(half[:, :], -0.5)
            nc.gpsimd.memset(vaug[:, :, :, DHV:VA], 1.0).then_inc(s_pchain, 1)
            pool.wait_ge(s_pchain, 1)
            nc.gpsimd.affine_select(out=ident[:, :], in_=ident[:, :], compare_op=ALU.not_equal, fill=1.0,
                                    base=0, pattern=[[-1, P]], channel_multiplier=1)
            nc.gpsimd.affine_select(out=causal[:, :], in_=causal[:, :], compare_op=ALU.is_ge, fill=MASKED,
                                    base=0, pattern=[[1, P]], channel_multiplier=-1)
            nc.gpsimd.affine_select(out=own_head[:, :], in_=own_head[:, :], compare_op=ALU.is_ge, fill=0.0,
                                    base=0, pattern=[[-DQ, H4]], channel_multiplier=1).then_inc(s_pchain, 1)
            pool.wait_ge(s_pchain, 2)
            nc.gpsimd.affine_select(out=own_head[:, :], in_=own_head[:, :], compare_op=ALU.is_ge, fill=0.0,
                                    base=DQ - 1, pattern=[[DQ, H4]], channel_multiplier=-1)
            nc.gpsimd.tensor_copy(ident16[:, :], ident[:, :]).then_inc(s_ident, 1)

            def w_sums():
                pool.wait_ge(s_asum, 1)
                nc.gpsimd.partition_all_reduce(totals, asums, P, RADD).then_inc(s_allsum, 1)

            def layer_norm(b):
                pool.wait_ge(var1, at(b, 1, 1))
                nc.gpsimd.tensor_tensor(rstd[:, :], ve[:, :], half[:, 0:T], ALU.pow).then_inc(rstd1_ok, 1)

            def ternary_low():
                for u in range(0, UNITS, 2):
                    if u == 0:
                        pool.wait_ge(s_thr, 1)
                    if u >= 4:
                        pool.wait_ge(s_tern, u - 3)
                    nc.gpsimd.tensor_scalar(low(u), rows[:, u, :], nthr[:, 0:1], None, ALU.is_le).then_inc(s_low[0], 1)

            def decay(b):
                for n in range(NH // 2):
                    if n % 2 == 0:
                        pool.wait_ge(r_loaded[n // 2], at(b, 16, 16))
                    rows_of = dec[:, 2 * n:2 * n + 2, :].rearrange("p h (t s) -> p (h t) s", s=P)
                    nc.gpsimd.tensor_tensor(rows_of, rows_of,
                                            causal[:, :].unsqueeze(1).to_broadcast([P, 2 * T, P]),
                                            ALU.add).then_inc(masked, 1)

            def weigh_queries(b):
                pool.wait_ge(fcol_ok, at(b, 1, 1))
                pool.wait_ge(pa_free[(U_Q + 1) % 2], pa_done(b, U_Q + 1))
                pool.wait_ge(pa_free[U_Q % 2], pa_done(b, U_Q))
                nc.gpsimd.tensor_tensor(qw[:, :, :], qw[:, :, :], qT[:, :, P:S], ALU.mult).then_inc(qw_ok, 1)

            def head_norm(b, j):
                pool.wait_ge(hvar_ok, at(b, T, j + 1))
                nc.gpsimd.tensor_tensor(hinv[:, :], hvar[:, :], half[:, :], ALU.pow).then_inc(pool_a, 1)
                pool.wait_ge(pool_a, at(b, POOL_A, j + 1))
                hc = by_head(cent[j % 2])
                nc.gpsimd.tensor_tensor(hc, hc, per_head(hinv[:, :], DHV), ALU.mult).then_inc(hn_ok, 1)

            def gated_lo(b, j):
                pool.wait_ge(ho_hi, at(b, T, j + 1))
                nc.gpsimd.tensor_tensor(head_parts[j % 2][:, LO, :], cent[j % 2], head_parts[j % 2][:, HI, :],
                                        ALU.subtract).then_inc(ho_lo[j], 1)

            def residual_bias(b, t):
                use = U_Y + t
                pool.wait_ge(pa_free[use % 2], pa_done(b, use))
                if not (isinstance(b, int) and b == 0):
                    pool.wait_ge(out_stored[t], at(b, 16, 0))
                nc.gpsimd.tensor_tensor(x1b[:, t, :], xres[:, t, :], b2r[:, :], ALU.add).then_inc(x1b_ok, 1)

            def layer_norm2(b):
                pool.wait_ge(var2, at(b, 1, 1))
                nc.gpsimd.tensor_tensor(rstd[:, :], ve[:, :], half[:, 0:T], ALU.pow).then_inc(rstd2_ok, 1)

            layer_norm(0)

            def bounds(cols, sums, peaks, step):
                pool.wait_ge(s_sums, sums)
                if peaks:
                    pool.wait_ge(s_peak, peaks)
                n = cols.stop - cols.start
                last = cols.stop + (cols == LATER)
                nc.gpsimd.partition_all_reduce(bound[:, cols.start:last], peak[:, cols.start:last], P,
                                               RMAX).then_inc(s_allmax, 1)
                pool.wait_ge(s_bound, step)
                nc.gpsimd.tensor_tensor(floor2[:, cols], bound[:, cols], half[:, 0:n], ALU.pow).then_inc(s_rbound, 1)

            bounds(EARLY, 2, 0, 1)
            bounds(LATER, 3, 1, 2)

            def sequence(b, ahead):
                if ahead:
                    layer_norm(b + 1)
                first = isinstance(b, int) and b == 0
                decay(b)
                if first:
                    w_sums()
                    ternary_low()
                weigh_queries(b)
                head_norm(b, 0)
                for j in range(1, T):
                    gated_lo(b, j - 1)
                    head_norm(b, j)
                gated_lo(b, T - 1)
                for t in range(T):
                    residual_bias(b, t)
                layer_norm2(b)

            sequence(0, True)
            with pool.Fori(1, B - 1) as b:
                sequence(b, True)
            sequence(B - 1, False)

        @block.scalar
        def _(act):
            def sum_squares(g):
                if g == G_V:
                    act.wait_ge(s_const, 1)
                elif g is None:
                    act.wait_ge(s_sums, 1)
                else:
                    act.wait_ge(s_sums, 2)
                if g is None:
                    act.wait_ge(s_wload[4], 32)
                    nc.scalar.activation(sig[0:GROWS, 0, :], th, ACT.Square,
                                         accum_out=peak[0:GROWS, W_GATE:W_GATE + 1]).then_inc(s_sums, 1)
                else:
                    act.wait_ge(s_wload[g], 32 if g == G_QK else 16)
                    nc.scalar.activation(sig[:, :, :], group_rows(g), ACT.Square,
                                         accum_out=peak[:, W_V + g:W_V + g + 1]).then_inc(s_sums, 1)

            def weights_hi(*uses):
                for n in uses:
                    g, k = weight_use(n)
                    act.wait_ge(s_wfill, n + 1)
                    if n in (USES_V[0], USES_QK[0]):
                        act.wait_ge(s_scales, 1 if n == USES_V[0] else 2)
                    if g is None:
                        nc.scalar.activation(wgT[:, :, HI, 0:GROWS], wbank[w_bank(n)][:, 0:KD * GROWS].rearrange("p (k r) -> p k r", r=GROWS),
                                             ACT.Copy, scale=wscale[:, W_GATE:W_GATE + 1]).then_inc(s_whi, 1)
                    else:
                        scale = gcol[:, k:k + 1] if g == G_OUT else wscale[:, W_V + g:W_V + g + 1]
                        nc.scalar.activation(wT[:, HI, k, g * D:(g + 1) * D], wbank[w_bank(n)], ACT.Copy,
                                             scale=scale).then_inc(s_whi, 1)

            def replace_rows(g):
                act.wait_ge(s_wfill, (USES_V, USES_QK, USES_O)[g][-1] + 1)
                if g == G_O:
                    act.wait_ge(s_peak, 1)
                load_w1(act, g)

            sums = Chain(0, 4 + UNITS // 2)

            def absolute_sums2(*quarters):
                for n in quarters:
                    act.wait_ge(s_w2early[n], 16)
                    nc.scalar.activation(early_w2(n), early_w2(n), ACT.Abs, accum_out=asum2[:, n:n + 1]).then_inc(s_abs, 1)
                    sums.next()

            def absolute_sums1(*pairs):
                for n in pairs:
                    act.wait_ge(s_w12[0][n // 2], 16)
                    act.wait_ge(s_abs, sums.n)
                    act.wait_ge(gate_act, 5)
                    nc.scalar.activation(g32[:, :, :], rows[:, 2 * n:2 * n + 2, :], ACT.Abs,
                                         accum_out=asum1[:, n:n + 1]).then_inc(s_abs, 1)
                    sums.next()

            def ternary_out(*pairs):
                for q in pairs:
                    act.wait_ge(s_ufill, q + 1)
                    nc.scalar.activation(w1T[:, :, 2 * q * P:(2 * q + 2) * P].rearrange("p k (u c) -> p u k c", c=P),
                                         pair_bank(q), ACT.Copy).then_inc(pf_free[q % 2], 1)

            def signs(*pairs):
                for q in pairs:
                    act.wait_ge(s_w12[1][q // 2], 16)
                    if q < 2:
                        act.wait_ge(s_ufill, UNITS // 2)
                    else:
                        act.wait_ge(s_ufill2, q - 1)
                    nc.scalar.activation(tern(2 * q), rows[:, 2 * q, :], ACT.Sign, bias=nthr[:, 1:2])
                    nc.scalar.activation(low(2 * q), rows[:, 2 * q, :], ACT.Sign, bias=thr[:, 1:2]).then_inc(s_sign, 1)

            def ternary2_out(*pairs):
                for q in pairs:
                    act.wait_ge(s_ufill2, q + 1)
                    for u in (2 * q, 2 * q + 1):
                        nc.scalar.activation(w2T[:, 4 * (u % 4):4 * (u % 4) + 4, tok(u // 4)],
                                             pf[:, u % 2, :].rearrange("p (k c) -> p k c", c=P),
                                             ACT.Sign).then_inc(pf_free[u % 2], 1)

            def split_hi(b, ks):
                for k in ks:
                    n = x_index(b, k)
                    act.wait_ge(pa_fill, n + 1)
                    nc.scalar.activation(xT[:, HI, :, k, :], by_tile(pa[:, n % 2, :]), ACT.Copy, scale=X_SCALE).then_inc(x_hi, 1)

            def tokens_hi(b):
                act.wait_ge(xn_ok, at(b, T, T))
                nc.scalar.activation(parts1[:, HI, :, :], xin[:, :, :], ACT.Copy, scale=X_SCALE).then_inc(part1_hi, 1)

            def tokens2_hi(fb, half):
                act.wait_ge(xn2_ok, at(fb, T, half.stop))
                nc.scalar.activation(parts2[:, HI, half, :], xres[:, half, :], ACT.Copy, scale=X_SCALE).then_inc(part2_hi, 1)

            def gates(b, fb):
                def weights_between(*uses):
                    if isinstance(b, int) and b == 0:
                        weights_hi(*uses)

                def sums_between(n):
                    if isinstance(b, int) and b == 0:
                        absolute_sums2(n)

                act.wait_ge(pa_fill, pa_filled(b, U_GATE))
                nc.scalar.activation(th, pa[P // 2:P // 2 + GROWS, U_GATE % 2, :], ACT.Copy).then_inc(gate_lo, 1)
                sums_between(1)
                act.wait_ge(pa_free[U_GATE % 2], pa_done(b, U_GATE))
                nc.scalar.activation(th, th, ACT.Tanh, bias=gate_bias[:, 0:1],
                                     scale=evac[0:GROWS, W_GATE:W_GATE + 1]).then_inc(tanh_ok, 1)
                sums_between(2)
                value(b, 0)
                act.wait_ge(gate_dve, at(b, 4, 1))
                nc.scalar.activation(ge, ge, ACT.Exp).then_inc(gate_act, 1)
                act.wait_ge(gate_dve, at(b, 4, 2))
                nc.scalar.activation(gl, gu, ACT.Ln).then_inc(gate_act, 1)
                weights_between(*USES_QK[0:2])
                value(b, 1)
                weights_between(USES_QK[2])
                value(b, 2)
                act.wait_ge(gate_dve, at(b, 4, 3))
                nc.scalar.activation(stack[32:32 + NH, :], gu, ACT.Exp, scale=-1.0).then_inc(gate_act, 1)
                weights_between(USES_QK[3])
                value(b, 3)
                if fb is not None:
                    tokens2_hi(fb, HALVES[0])
                act.wait_ge(gate_dve, at(b, 4, 4))
                nc.scalar.activation(ge[:, 0:LATE], ge[:, 0:LATE], ACT.Exp).then_inc(gate_act, 1)
                nc.scalar.activation(stack[64:64 + NH, 0:LATE], gf[:, 0:LATE], ACT.Exp).then_inc(gate_act, 1)
                if fb is not None:
                    tokens2_hi(fb, HALVES[1])

            def value(b, t):
                use = U_V + t
                act.wait_ge(pa_fill, pa_filled(b, use))
                nc.scalar.activation(vaug[:, t, :, 0:DHV], pa[:, use % 2, :].rearrange("p (h v) -> p h v", v=DHV),
                                     ACT.Copy, scale=evac[:, W_V:W_V + 1]).then_inc(pa_free[use % 2], 1)

            def output_gate(b, *ns):
                for n in ns:
                    use = U_O + n
                    act.wait_ge(pa_fill, pa_filled(b, use))
                    nc.scalar.activation(sig[:, n, :], pa[:, use % 2, :], ACT.Copy,
                                         scale=evac[:, W_O:W_O + 1]).then_inc(pa_free[use % 2], 1)

            def sigmoids(b):
                for n in (U_O + 2, U_O + 3):
                    act.wait_ge(pa_free[n % 2], pa_done(b, n))
                nc.scalar.activation(sig[:, :, :], sig[:, :, :], ACT.Sigmoid).then_inc(sig_ok, 1)

            def gate_columns(b):
                act.wait_ge(ph_fill, at(b, PH_USES, U_GT + 1))
                nc.scalar.activation(gtok[:, :, :, :], ph[:, 0, :].rearrange("p (t a h) -> p t a h", t=T, h=32)[:, :, 0:3, 0:NH],
                                     ACT.Copy).then_inc(ph_free, 1)

            def keys(b, *ns):
                act.wait_ge(gate_act, at(b, 5, 5))
                for n in ns:
                    use = U_K + n
                    act.wait_ge(pa_fill, pa_filled(b, use))
                    nc.scalar.activation(kT[:, n, :], pa[:, use % 2, :], ACT.Copy,
                                         scale=evac[:, W_QK:W_QK + 1]).then_inc(pa_free[use % 2], 1)

            def queries(b, *ns):
                if 0 in ns:
                    act.wait_ge(r_stored, at(b, 16, 16))
                    act.wait_ge(w_stored, at(b, 16, 16))
                for n in ns:
                    use = U_Q + n
                    act.wait_ge(pa_fill, pa_filled(b, use))
                    nc.scalar.activation(qT[:, n, :], pa[:, use % 2, :], ACT.Copy,
                                         scale=evac[:, W_GELU:W_GELU + 1]).then_inc(pa_free[use % 2], 1)

            def decay(b, first):
                act.wait_ge(masked, at(b, NH // 2, first // 2 + 1))
                if first == 0:
                    act.wait_ge(ph_free, at(b, PH_USES, U_GT + 1))
                for h in (first, first + 1):
                    for j in range(T):
                        last = nc.scalar.activation(dec[:, h, tok(j)], dec[:, h, tok(j)], ACT.Exp,
                                                    bias=gtok[:, j, ROW_C, h:h + 1])
                    last.then_inc(d_ok, 1)

            def split2_hi(fb, ks):
                for k in ks:
                    act.wait_ge(pf_fill, pf_filled(fb, U_T2 + k))
                    nc.scalar.activation(x2T[:, HI, :, k, :], by_tile(pf[:, (U_T2 + k) % 2, :]), ACT.Copy,
                                         scale=X_SCALE).then_inc(x2t_hi, 1)

            def gelu(fb, f):
                use = U_F1 + f
                act.wait_ge(pf_fill, pf_filled(fb, use))
                if f >= 2:
                    act.wait_ge(gs_ok, at(fb, NF, f - 1))
                if f == 0:
                    act.wait_ge(gate_act, at(fb, 5, 5))
                nc.scalar.activation(g32[:, f % 2, :], pf[:, use % 2, :], ACT.Gelu, bias=b1c[:, f:f + 1],
                                     scale=1.0 / X_SCALE).then_inc(pf_free[use % 2], 1)
                act.wait_ge(pf_free[use % 2], pf_done(fb, use))
                nc.scalar.activation(gT[:, HI, f, :], g32[:, f % 2, :], ACT.Copy,
                                     scale=wscale[:, W_GELU:W_GELU + 1]).then_inc(g_hi, 1)

            def squares(b, j):
                act.wait_ge(ph_free, at(b, PH_USES, U_H + j + 1))
                nc.scalar.activation(square, cent[j % 2].rearrange("p (a s) -> p a s", a=2), ACT.Square).then_inc(sq_ok, 1)

            def gated_hi(b, j):
                act.wait_ge(gated_ok, at(b, T, j + 1))
                if j >= 2:
                    act.wait_ge(hoT_loaded[j - 2], at(b, 16, 16))
                nc.scalar.activation(head_parts[j % 2][:, HI, :], cent[j % 2], ACT.Copy).then_inc(ho_hi, 1)

            def sequence(b, fb, ahead):
                gates(b, fb)
                run_f = fb is not None
                if run_f:
                    keys(b, 0, 1)
                    gate_columns(b)
                    queries(b, 0)
                    if ahead:
                        tokens_hi(b + 1)
                    queries(b, 1)
                else:
                    weights_hi(*USES_O[0:2])
                    absolute_sums1(6, 7)
                    absolute_sums2(3)
                    keys(b, 0)
                    replace_rows(G_QK)
                    weights_hi(USES_O[2])
                    absolute_sums1(0)
                    weights_hi(USES_O[3])
                    keys(b, 1)
                    replace_rows(G_O)
                    gate_columns(b)
                    absolute_sums1(1)
                    queries(b, 0)
                    absolute_sums1(2)
                    queries(b, 1)
                    absolute_sums1(3, 4, 5)
                decay(b, 0)
                output_gate(b, 0)
                decay(b, 2)
                output_gate(b, 1)
                decay(b, 4)
                output_gate(b, 2)
                decay(b, 6)
                output_gate(b, 3)
                if run_f:
                    for f in range(NF):
                        gelu(fb, f)
                else:
                    ternary_out(*range(UNITS // 2))

                def between(make=(), use=(), out=()):
                    if not run_f:
                        ternary2_out(*use)
                        signs(*make)
                        weights_hi(*out)

                def split_next(*ks):
                    if not run_f:
                        split_hi(b + 1, ks)

                between((0, 1))
                between((2,), (0,))
                between((), (1,))
                if not run_f:
                    sigmoids(b)
                squares(b, 0)
                if run_f:
                    sigmoids(b)
                between(out=USES_OUT[0:2])
                split_next(0, 1)
                between((3,))
                squares(b, 1)
                gated_hi(b, 0)
                between((), (2,), USES_OUT[2:4])
                squares(b, 2)
                gated_hi(b, 1)
                split_next(2, 3)
                between((4,))
                squares(b, 3)
                gated_hi(b, 2)
                between((5,), (3,))
                gated_hi(b, 3)
                between((6,), (4,))
                between((7,), (5,))
                between((), (6, 7))

            sum_squares(G_V)
            sum_squares(None)
            sum_squares(G_QK)
            split_hi(0, range(KD))
            weights_hi(*USES_V)
            weights_hi(USE_GATE)
            replace_rows(G_V)
            absolute_sums2(0)
            sequence(0, None, True)
            with act.Fori(1, B - 1) as b:
                sequence(b, b - 1, True)
            sequence(B - 1, B - 2, False)
            split2_hi(B - 1, range(KD))
            act.wait_ge(gs_ok, at(B - 1, NF, 0))
            for f in range(NF):
                gelu(B - 1, f)

        @block.vector
        def _(dve):
            ch_setup = Chain(0, 99)

            def setup_step(ins):
                ins.then_inc(s_dchain, 1)
                dve.wait_ge(s_dchain, ch_setup.next())

            def largest():
                dve.wait_ge(s_ident, 1)
                for g in (G_O, G_OUT):
                    dve.wait_ge(s_wload[g], 16)
                    nc.vector.tensor_reduce(peak[:, W_V + g:W_V + g + 1], group_rows(g), AX.XY, ALU.max,
                                            apply_absolute_value=True)
                dve.wait_ge(s_small, 48)
                nc.vector.tensor_reduce(peak[:, GAMMA:GAMMA + 1], gcol[:, :], AX.X, ALU.max, apply_absolute_value=True)
                nc.vector.tensor_reduce(peak[:, W_GELU:W_GELU + 1], b1c[:, :], AX.X, ALU.max,
                                        apply_absolute_value=True).then_inc(s_peak, 1)

            def bounds(cols, step):
                dve.wait_ge(s_allmax, step)
                if step == 2:
                    gelu, wout, gmax = (bound[:, c:c + 1] for c in (W_GELU, W_OUT, GAMMA))
                    setup_step(nc.vector.tensor_scalar(gelu, gelu, float(D), None, ALU.add))
                    magnitudes = bound[:, W_O:GAMMA]
                    setup_step(nc.vector.scalar_tensor_tensor(magnitudes, magnitudes, 1.0, magnitudes, ALU.mult, ALU.mult))
                    setup_step(nc.vector.tensor_scalar(wout, wout, gmax, gmax, ALU.mult, ALU.mult))
                nc.vector.tensor_scalar(bound[:, cols], bound[:, cols], TINY, None, ALU.max).then_inc(s_bound, 1)

            def scales(cols, step):
                dve.wait_ge(s_rbound, step)
                bits = floor2[:, cols].bitcast(I32)
                setup_step(nc.vector.tensor_scalar(bits, bits, 0x7F800000, None, ALU.bitwise_and))
                setup_step(nc.vector.tensor_scalar(wscale[:, cols], floor2[:, cols], TOP, None, ALU.mult))
                setup_step(nc.vector.reciprocal(winv[:, cols], wscale[:, cols]))
                if step == 1:
                    dve.wait_ge(s_bias, 32)
                    nc.vector.tensor_scalar(gate_bias[:, :], gate_bias[:, :], 1.0 / CAP, None, ALU.mult)
                    nc.vector.tensor_scalar(evac[:, W_V:W_V + 1], winv[:, W_V:W_V + 1], 1.0 / X_SCALE, None, ALU.mult)
                    nc.vector.tensor_scalar(evac[:, W_GATE:W_GATE + 1], winv[:, W_GATE:W_GATE + 1], 1.0 / (X_SCALE * CAP), None,
                                            ALU.mult).then_inc(s_scales, 1)
                else:
                    qk = winv[:, W_QK:W_QK + 1]
                    nc.vector.tensor_scalar(evac[:, W_QK:W_QK + 1], qk, 1.0 / X_SCALE, None, ALU.mult)
                    nc.vector.tensor_scalar(evac[:, W_GELU:W_GELU + 1], qk, DQ ** -0.5 / X_SCALE, None, ALU.mult)
                    nc.vector.tensor_scalar(evac[:, W_O:W_O + 1], winv[:, W_O:W_O + 1], 1.0 / X_SCALE, None, ALU.mult)
                    nc.vector.tensor_scalar(evac[:, W_OUT:W_OUT + 1], winv[:, W_OUT:W_OUT + 1], 1.0 / H_SCALE, None, ALU.mult)
                    nc.vector.tensor_scalar(split_scale[:, 0:1], wscale[:, W_QK:W_QK + 1], 2.0 ** -5, None, ALU.mult)
                    nc.vector.tensor_scalar(split_scale[:, 1:2], qk, 2.0 ** 10, qk, ALU.mult, ALU.mult)
                    nc.vector.tensor_scalar(gcol[:, :], gcol[:, :], wscale[:, W_OUT:W_OUT + 1], None, ALU.mult).then_inc(s_scales, 1)
                dve.wait_ge(s_scales, step)

            def weights_lo(*uses):
                for n in uses:
                    g, k = weight_use(n)
                    dve.wait_ge(s_whi, n + 1)
                    if g is None:
                        hi, lo = (wgT[:, :, part, 0:GROWS] for part in (HI, LO))
                        src = wbank[w_bank(n)][:, 0:KD * GROWS].rearrange("p (k r) -> p k r", r=GROWS)
                        scale = wscale[:, W_GATE:W_GATE + 1]
                    else:
                        hi, lo = (wT[:, part, k, g * D:(g + 1) * D] for part in (HI, LO))
                        src = wbank[w_bank(n)]
                        scale = gcol[:, k:k + 1] if g == G_OUT else wscale[:, W_V + g:W_V + g + 1]
                    nc.vector.scalar_tensor_tensor(lo, src, scale, hi, ALU.mult, ALU.subtract).then_inc(s_wfree[w_bank(n)], 1)

            def thresholds():
                dve.wait_ge(s_abs, 4 + UNITS // 2)
                nc.vector.tensor_reduce(asums[:, 0:1], asum1[:, :], AX.X, ALU.add)
                nc.vector.tensor_reduce(asums[:, 1:2], asum2[:, :], AX.X, ALU.add).then_inc(s_asum, 1)
                dve.wait_ge(s_allsum, 1)
                setup_step(nc.vector.tensor_scalar(thr, totals, 1.0 / (FF * D), 0.7, ALU.mult, ALU.mult))
                nc.vector.tensor_scalar(nthr, thr, -1.0, None, ALU.mult).then_inc(s_thr, 1)
                dve.wait_ge(s_thr, 1)

            def ternary(*units):
                for u in units:
                    by_pool = u % 2 == 0
                    if not by_pool:
                        if u >= 4:
                            dve.wait_ge(s_tern, u - 3)
                        nc.vector.tensor_scalar(low(u), rows[:, u, :], nthr[:, 0:1], None, ALU.is_le).then_inc(s_low[1], 1)
                    dve.wait_ge(s_low[u % 2], u // 2 + 1)
                    if u >= 4:
                        dve.wait_ge(s_ufill, u // 2 - 1)
                    nc.vector.scalar_tensor_tensor(tern(u), rows[:, u, :], thr[:, 0:1], low(u), ALU.is_ge,
                                                   ALU.subtract).then_inc(s_tern, 1)

            def ternary2(q):
                u = 2 * q + 1
                dve.wait_ge(s_w12[1][q // 2], 16)
                if q >= 2:
                    dve.wait_ge(s_ufill2, q - 1)
                else:
                    dve.wait_ge(s_ufill, UNITS // 2)
                nc.vector.tensor_scalar(low(u), rows[:, u, :], nthr[:, 1:2], None, ALU.is_le).then_inc(s_low2, 1)
                dve.wait_ge(s_low2, q + 1)
                nc.vector.scalar_tensor_tensor(tern(u), rows[:, u, :], thr[:, 1:2], low(u), ALU.is_ge,
                                               ALU.subtract).then_inc(s_tern2, 1)

            def mean_var(order, ch):
                nc.vector.tensor_tensor(mean[:, :], stats[:, :, 1], stats[:, :, 4], ALU.add)
                nc.vector.tensor_tensor(dif[:, :], stats[:, :, 1], stats[:, :, 4], ALU.subtract)
                nc.vector.tensor_tensor(dev[:, :], stats[:, :, 2], stats[:, :, 5], ALU.add).then_inc(order, 1)
                dve.wait_ge(order, ch.next())
                nc.vector.tensor_scalar(mean[:, :], mean[:, :], 0.5, None, ALU.mult)
                nc.vector.scalar_tensor_tensor(dif[:, :], dif[:, :], 0.25, dif[:, :], ALU.mult, ALU.mult)
                nc.vector.tensor_scalar(dev[:, :], dev[:, :], 1.0 / D, LN_EPS, ALU.mult, ALU.add).then_inc(order, 1)
                dve.wait_ge(order, ch.next())

            def norm_stats(b):
                ch = Chain(b, DVE_L)
                dve.wait_ge(x_loaded, at(b, 16, 16))
                for t in range(T):
                    last = nc.vector.bn_stats(stats[:, t, :], xin[:, t, :])
                last.then_inc(dve_l, 1)
                dve.wait_ge(dve_l, ch.next())
                mean_var(dve_l, ch)
                nc.vector.tensor_tensor(ve[:, :], dif[:, :], dev[:, :], ALU.add).then_inc(var1, 1)

            def norm_apply(b):
                dve.wait_ge(rstd1_ok, at(b, 1, 1))
                for t in range(T):
                    nc.vector.tensor_scalar(xin[:, t, :], xin[:, t, :], mean[:, t:t + 1], rstd[:, t:t + 1],
                                            ALU.subtract, ALU.mult).then_inc(xn_ok, 1)

            def split_lo(b, ks):
                for k in ks:
                    n = x_index(b, k)
                    dve.wait_ge(x_hi, b * KD + k + 1)
                    nc.vector.scalar_tensor_tensor(xT[:, LO, :, k, :], by_tile(pa[:, n % 2, :]), X_SCALE, xT[:, HI, :, k, :],
                                                   ALU.mult, ALU.subtract).then_inc(pa_free[n % 2], 1)

            def tokens_lo(b):
                dve.wait_ge(part1_hi, at(b, 1, -1))
                nc.vector.scalar_tensor_tensor(parts1[:, LO, :, :], xin[:, :, :], X_SCALE, parts1[:, HI, :, :],
                                               ALU.mult, ALU.subtract).then_inc(part1_ok, 1)

            def tokens2_lo(fb, half, n):
                dve.wait_ge(part2_hi, at(fb, 2, n + 1))
                nc.vector.scalar_tensor_tensor(parts2[:, LO, half, :], xres[:, half, :], X_SCALE, parts2[:, HI, half, :],
                                               ALU.mult, ALU.subtract).then_inc(part2_ok, 1)

            def gate_decay(b, ch, between):
                dve.wait_ge(gate_lo, at(b, 1, 1))
                nc.vector.tensor_tensor(th, pa[0:GROWS, U_GATE % 2, :], th, ALU.add).then_inc(pa_free[U_GATE % 2], 1)
                dve.wait_ge(tanh_ok, at(b, 1, 1))
                nc.vector.tensor_scalar(ge, th[GATE_F:GROWS, :], CAP, None, ALU.mult).then_inc(dve_a, 1)
                dve.wait_ge(dve_a, ch.next())
                nc.vector.scalar_tensor_tensor(ge, ge, -1.0, ge, ALU.mult, ALU.min).then_inc(gate_dve, 1)
                nc.vector.tensor_scalar(gi, th[0:NH, :], CAP, None, ALU.mult)
                nc.vector.tensor_scalar(gf, th[GATE_F:GROWS, :], CAP, 0.0, ALU.mult, ALU.min)
                between[0]()
                dve.wait_ge(gate_act, at(b, 5, 1))
                nc.vector.tensor_scalar(gu, ge, 1.0, None, ALU.add).then_inc(gate_dve, 1)
                dve.wait_ge(gate_dve, at(b, 4, 2))
                nc.vector.scalar_tensor_tensor(ge, gu, 1.0, ge, ALU.subtract, ALU.subtract).then_inc(dve_a, 1)
                dve.wait_ge(dve_a, ch.next())
                nc.vector.tensor_tensor(gf, gf, ge, ALU.add).then_inc(dve_a, 1)
                dve.wait_ge(dve_a, ch.next())
                dve.wait_ge(gate_act, at(b, 5, 2))
                nc.vector.tensor_tensor(gf, gf, gl, ALU.subtract).then_inc(dve_a, 1)
                dve.wait_ge(dve_a, ch.next())
                nc.vector.tensor_tensor_scan(gu, gf, gi, 0.0, ALU.add, ALU.max).then_inc(gate_dve, 1)
                for j in range(T):
                    last = nc.vector.tensor_tensor_scan(gl[:, tok(j)], one[0:NH, :].to_broadcast([NH, P]), gf[:, tok(j)], 0.0,
                                                        ALU.mult, ALU.add)
                last.then_inc(dve_a, 1)
                dve.wait_ge(dve_a, ch.next())
                nc.vector.tensor_tensor(th[0:NH, :], gl, gu, ALU.subtract).then_inc(r_ok, 1)
                nc.vector.tensor_tensor(stack[0:NH, :], gi, gl, ALU.subtract).then_inc(dve_a, 1)
                dve.wait_ge(dve_a, ch.next())
                dve.wait_ge(r_ok, at(b, 1, 1))
                chunks = (NH, T - 1, P)
                nc.vector.tensor_tensor(ge[:, 0:LATE].rearrange("h (c s) -> h c s", s=P),
                                        th[0:NH, P:S].rearrange("h (c s) -> h c s", s=P),
                                        gu[:, P - 1:LATE:P].unsqueeze(2).to_broadcast(list(chunks)), ALU.add)
                nc.vector.tensor_tensor(gf[:, 0:LATE].rearrange("h (c s) -> h c s", s=P),
                                        stack[0:NH, 0:LATE].rearrange("h (c s) -> h c s", s=P),
                                        th[0:NH, P - 1:LATE:P].unsqueeze(2).to_broadcast(list(chunks)),
                                        ALU.add).then_inc(gate_dve, 1)
                between[1]()

            def split_parts(b, ch, use, whole):
                for n in range(HG):
                    dve.wait_ge(pa_free[(use + n) % 2], pa_done(b, use + n))
                nc.vector.tensor_scalar(kq_parts[:, HI, :, :], whole, split_scale[:, 0:1], None, ALU.mult).then_inc(dve_a, 1)
                dve.wait_ge(dve_a, ch.next())
                nc.vector.scalar_tensor_tensor(kq_parts[:, LO, :, :], whole, split_scale[:, 0:1], kq_parts[:, HI, :, :],
                                               ALU.mult, ALU.subtract).then_inc(dve_a, 1)
                dve.wait_ge(dve_a, ch.next())

            def stack_heads(stacked, order, h, done):
                for r, part in enumerate(order):
                    last = nc.vector.tensor_copy(stacked[r * DQ:(r + 1) * DQ, h::H4, :],
                                                 kq_parts[h * DQ:(h + 1) * DQ, part, :, :])
                last.then_inc(done, 1)

            def weigh_keys(b, chunks, src, free):
                n = len(chunks)
                nc.vector.tensor_tensor(ktok[:, chunks[0]:chunks[0] + n, :].rearrange("p c (h d) -> p c h d", d=DQ),
                                        src.rearrange("p (c h d) -> p c h d", c=n, d=DQ),
                                        gtok[:, chunks[0]:chunks[0] + n, ROW_G, :].unsqueeze(3).to_broadcast([P, n, NH, DQ]),
                                        ALU.mult).then_inc(free, 1)

            def keys_first(b):
                dve.wait_ge(ph_free, at(b, PH_USES, U_GT + 1))
                dve.wait_ge(ps_fill, at(b, sum(PS_USES), 1))
                weigh_keys(b, (0, 1), ps[:, 0, :], ps_free[0])

            def keys_last(b):
                dve.wait_ge(pa_fill, pa_filled(b, U_KLAST))
                weigh_keys(b, (2,), pa[:, U_KLAST % 2, 0:QK], pa_free[U_KLAST % 2])

            def chunk_decay(b):
                dve.wait_ge(w_loaded, at(b, 16 * NH, 16 * NH))
                nc.vector.tensor_copy(fcol[:, :, :], qw[:, :, P - 1::P]).then_inc(fcol_ok, 1)

            def state(b, j):
                dve.wait_ge(ph_fill, at(b, PH_USES, U_U + j + 1))
                nc.vector.tensor_tensor(cst[:, j, :, :].rearrange("p a (h v) -> p a h v", v=VA),
                                        ph[:, :, 0:H4 * VA].rearrange("p a (h v) -> p a h v", v=VA),
                                        own_head[:, :].unsqueeze(1).unsqueeze(3).to_broadcast([P, HG, H4, VA]),
                                        ALU.mult).then_inc(ph_free, 1)
                dve.wait_ge(ph_free, at(b, PH_USES, U_U + j + 1))
                if j == 1:
                    dve.wait_ge(fcol_ok, at(b, 1, 1))
                if j == 2:
                    dve.wait_ge(c_ok, at(b, T - 2, 1))
                if j >= 1:
                    for g in range(HG):
                        last = nc.vector.scalar_tensor_tensor(cst[:, j, g, :], cst[:, j - 1, g, :], fcol[:, g, j - 1:j],
                                                              cst[:, j, g, :], ALU.mult, ALU.add)
                    last.then_inc(c_ok, 1)

            def weigh(b, n):
                h = HEADS[n]
                dve.wait_ge(ps_fill, at(b, sum(PS_USES), n + 2))
                dve.wait_ge(d_ok, at(b, NH, h + 1))
                nc.vector.scalar_tensor_tensor(dec[:, h, :], ps[:, n % 2, :], split_scale[:, 1:2], dec[:, h, :],
                                               ALU.mult, ALU.mult).then_inc(ps_free[n % 2], 1)

            def head_stats(b, j, ch):
                if not (isinstance(b, int) and b == 0 and j == 0):
                    dve.wait_ge(hvar_ok, at(b, T, j))
                if j >= 2:
                    dve.wait_ge(ho_lo[j - 2], at(b, 1, 1))
                dve.wait_ge(ph_fill, at(b, PH_USES, U_H + j + 1))
                norm = ph[:, :, 0:H4 * VA].rearrange("p a (h v) -> p a h v", v=VA)[:, :, :, DHV]
                den_of = den[:, :].rearrange("p (a h) -> p a h", h=H4)
                nc.vector.tensor_tensor(den_of, norm, gtok[:, j, ROW_EM, :].rearrange("p (a h) -> p a h", h=H4), ALU.max)
                nc.vector.tensor_reduce(hsum[:, :].rearrange("p (a h) -> p a h", h=H4), heads(j), AX.X,
                                        ALU.add).then_inc(dve_a, 1)
                dve.wait_ge(dve_a, ch.next())
                nc.vector.scalar_tensor_tensor(den_of, norm, -1.0, den_of, ALU.mult, ALU.max)
                nc.vector.tensor_scalar(hsum[:, :], hsum[:, :], 1.0 / DHV, None, ALU.mult).then_inc(dve_a, 1)
                dve.wait_ge(dve_a, ch.next())
                nc.vector.tensor_scalar(den[:, :], den[:, :], MLSTM_EPS, None, ALU.add).then_inc(dve_a, 1)
                dve.wait_ge(dve_a, ch.next())
                nc.vector.tensor_tensor(by_head(cent[j % 2]), heads(j), per_head(hsum[:, :], DHV),
                                        ALU.subtract).then_inc(ph_free, 1)
                nc.vector.scalar_tensor_tensor(den[:, :], den[:, :], MLSTM_EPS, den[:, :], ALU.mult, ALU.mult).then_inc(dve_a, 1)
                dve.wait_ge(dve_a, ch.next())
                if j > 0:
                    gated(b, j - 1)
                dve.wait_ge(sq_ok, at(b, T, j + 1))
                nc.vector.tensor_reduce(hsum[:, :], square.rearrange("p a (h v) -> p (a h) v", v=DHV), AX.X,
                                        ALU.add).then_inc(dve_a, 1)
                dve.wait_ge(dve_a, ch.next())
                if not (isinstance(b, int) and b == 0 and j == 0):
                    dve.wait_ge(hn_ok, at(b, T, j))
                nc.vector.scalar_tensor_tensor(hvar[:, :], hsum[:, :], 1.0 / DHV, den[:, :], ALU.mult,
                                               ALU.add).then_inc(hvar_ok, 1)

            def gated(b, j):
                dve.wait_ge(hn_ok, at(b, T, j + 1))
                if j == 0:
                    dve.wait_ge(sig_ok, at(b, 1, 1))
                    dve.wait_ge(qw_ok, at(b, 1, 1))
                nc.vector.scalar_tensor_tensor(cent[j % 2], cent[j % 2], H_SCALE, sig[:, j, :],
                                               ALU.mult, ALU.mult).then_inc(gated_ok, 1)

            def residual(b, t, ch):
                use = U_Y + t
                dve.wait_ge(pa_fill, pa_filled(b, use))
                if t == 0:
                    dve.wait_ge(res_loaded, at(b, 32, 32))
                if t == T - 1:
                    dve.wait_ge(res_last, at(b, 16, 16))
                nc.vector.scalar_tensor_tensor(xres[:, t, :], pa[:, use % 2, :], evac[:, W_OUT:W_OUT + 1], xres[:, t, :],
                                               ALU.mult, ALU.add).then_inc(pa_free[use % 2], 1)
                dve.wait_ge(pa_free[use % 2], pa_done(b, use))
                nc.vector.bn_stats(stats[:, t, :], xres[:, t, :]).then_inc(dve_a, 1)
                dve.wait_ge(dve_a, ch.next())
                if t == T - 1:
                    mean_var(dve_a, ch)
                    nc.vector.tensor_tensor(ve[:, :], dif[:, :], dev[:, :], ALU.add).then_inc(var2, 1)

            def norm2_apply(fb, tiles):
                dve.wait_ge(rstd2_ok, at(fb, 1, 1))
                for t in tiles:
                    dve.wait_ge(x1b_ok, at(fb, T, t + 1))
                    nc.vector.tensor_scalar(xres[:, t, :], xres[:, t, :], mean[:, t:t + 1], rstd[:, t:t + 1],
                                            ALU.subtract, ALU.mult).then_inc(xn2_ok, 1)

            def split2_lo(fb, ks):
                for k in ks:
                    use = U_T2 + k
                    dve.wait_ge(x2t_hi, k + 1)
                    nc.vector.scalar_tensor_tensor(x2T[:, LO, :, k, :], by_tile(pf[:, use % 2, :]), X_SCALE, x2T[:, HI, :, k, :],
                                                   ALU.mult, ALU.subtract).then_inc(pf_free[use % 2], 1)

            def gelu_lo(fb, f, after_parts=None):
                dve.wait_ge(g_hi, at(fb, NF, f + 1))
                if after_parts is not None and f == NF // 2:
                    dve.wait_ge(xT_loaded, at(after_parts, 16, 0))
                nc.vector.scalar_tensor_tensor(gT[:, LO, f, :], g32[:, f % 2, :], wscale[:, W_GELU:W_GELU + 1],
                                               gT[:, HI, f, :], ALU.mult, ALU.subtract).then_inc(gs_ok, 1)

            def result(fb, t):
                use = U_F2 + t
                dve.wait_ge(pf_fill, pf_filled(fb, use))
                dve.wait_ge(x1b_ok, at(fb, T, t + 1))
                nc.vector.scalar_tensor_tensor(x1b[:, t, :], pf[:, use % 2, :], winv[:, W_GELU:W_GELU + 1], x1b[:, t, :],
                                               ALU.mult, ALU.add).then_inc(pf_free[use % 2], 1)

            def sequence(b, fb, ahead):
                ca = Chain(b, DVE_A)
                run_f = fb is not None
                gate_decay(b, ca, [lambda: norm2_apply(fb, (0, 1)) if run_f else scales(LATER, 2),
                                   lambda: norm2_apply(fb, (2, 3)) if run_f else weights_lo(*USES_QK)])
                if ahead:
                    norm_stats(b + 1)
                if run_f:
                    for n, half in enumerate(HALVES):
                        tokens2_lo(fb, half, n)
                else:
                    weights_lo(*USES_O[0:2])
                if ahead:
                    norm_apply(b + 1)
                if not run_f:
                    weights_lo(*USES_O[2:4])
                split_parts(b, ca, U_K, kT[:, :, :])
                for h in range(H4):
                    stack_heads(kst, (HI, HI, LO, LO), h, k_ok)
                    if h == 1:
                        keys_first(b)
                        chunk_decay(b)
                dve.wait_ge(k_ok, at(b, H4, H4))
                split_parts(b, ca, U_Q, qT[:, :, :])
                for h in range(H4):
                    stack_heads(qst(b), (HI, LO, HI, LO), h, kq_ok)
                    if not run_f and h == 1:
                        thresholds()
                dve.wait_ge(kq_ok, at(b, H4, H4))
                if run_f and ahead:
                    tokens_lo(b + 1)

                def hidden(*fs):
                    if run_f:
                        for f in fs:
                            gelu_lo(fb, f, b if ahead else None)

                hidden(0, 1)
                for n in range(NH):
                    if not run_f:
                        ternary(2 * n, 2 * n + 1)
                    weigh(b, n)
                    hidden(2 + n)
                    if n == 3:
                        keys_last(b)
                    if n == 5:
                        state(b, 0)
                def between(q, *uses):
                    if not run_f:
                        ternary2(q)
                        weights_lo(*uses)

                def split_next(*ks):
                    if not run_f:
                        split_lo(b + 1, ks)

                between(0)
                state(b, 1)
                hidden(10, 11, 12)
                between(1)
                state(b, 2)
                hidden(13, 14, 15)

                def done(t):
                    if run_f:
                        result(fb, t)

                head_stats(b, 0, ca)
                done(0)
                between(2, *USES_OUT[0:2])
                head_stats(b, 1, ca)
                split_next(0, 1)
                between(3, *USES_OUT[2:4])
                head_stats(b, 2, ca)
                done(1)
                split_next(2, 3)
                head_stats(b, 3, ca)
                done(2)
                between(4)
                gated(b, 3)
                between(5)
                residual(b, 0, ca)
                between(6)
                residual(b, 1, ca)
                between(7)
                residual(b, 2, ca)
                done(3)
                residual(b, 3, ca)
                assert ca.n == DVE_A, ca.n

            norm_stats(0)
            norm_apply(0)
            bounds(EARLY, 1)
            split_lo(0, (0, 1))
            scales(EARLY, 1)
            split_lo(0, (2, 3))
            weights_lo(*USES_V)
            weights_lo(USE_GATE)
            largest()
            bounds(LATER, 2)
            sequence(0, None, True)
            with dve.Fori(1, B - 1) as b:
                sequence(b, b - 1, True)
            sequence(B - 1, B - 2, False)
            norm2_apply(B - 1, range(T))
            split2_lo(B - 1, range(KD))
            for f in range(NF):
                gelu_lo(B - 1, f)
            for t in range(T):
                result(B - 1, t)

        @block.tensor
        def _(pe):
            PARTS = ((HI, HI), (HI, LO), (LO, HI))

            def weights(*uses):
                for n in uses:
                    g, k = weight_use(n)
                    bank = wbank[w_bank(n)]
                    if n == 0:
                        pe.wait_ge(s_ident, 1)
                    if g is None:
                        pe.wait_ge(s_wload[4], 32)
                    elif k == 0:
                        pe.wait_ge(s_wload[g], 32 if g == G_QK else 16)
                    if n >= 4:
                        pe.wait_ge(s_wfree[w_bank(n)], w_taken(n))
                    for i in range(4):
                        if g is not None:
                            last = nc.tensor.transpose(bank[:, tok(i)], group_rows(g)[:, i, tok(k)], ident[:, :])
                        else:
                            last = nc.tensor.transpose(bank[:, i * GROWS:(i + 1) * GROWS], th[:, tok(i)],
                                                       ident[0:GROWS, 0:GROWS])
                    last.then_inc(s_wfill, 1)

            def weights_ready(*uses):
                for n in uses:
                    pe.wait_ge(s_wfree[w_bank(n)], w_taken(n) + 1)

            def ternary_transpose(q):
                pe.wait_ge(s_tern, 2 * q + 2)
                if q >= 2:
                    pe.wait_ge(pf_free[q % 2], q // 2)
                for i in range(2):
                    for k in range(KD):
                        last = nc.tensor.transpose(pair_bank(q)[:, i, k, :], tern(2 * q + i)[:, tok(k)], ident16[:, :])
                last.then_inc(s_ufill, 1)

            def ternary2_transpose(q):
                pe.wait_ge(s_sign, q + 1)
                pe.wait_ge(s_tern2, q + 1)
                for n in range(2):
                    pe.wait_ge(pf_free[n], PF_W1 + q)
                for k in range(KD):
                    nc.tensor.matmul(pf[:, 0, tok(k)], tern(2 * q)[:, tok(k)], ident16[:, :], start=True, stop=False)
                    nc.tensor.matmul(pf[:, 0, tok(k)], low(2 * q)[:, tok(k)], ident16[:, :], start=False, stop=True)
                    last = nc.tensor.matmul(pf[:, 1, tok(k)], tern(2 * q + 1)[:, tok(k)], ident16[:, :], start=True, stop=True)
                last.then_inc(s_ufill2, 1)

            def take_pa(b, use):
                count = pa_taken(b, use)
                if not (isinstance(count, int) and count == 0):
                    pe.wait_ge(pa_free[use % 2], count)
                return pa[:, use % 2, :]

            def take_pf(fb, use):
                pe.wait_ge(pf_free[use % 2], pf_taken(fb, use))
                return pf[:, use % 2, :]

            def take_ph(b, use):
                if not (isinstance(b, int) and b == 0 and use == 0):
                    pe.wait_ge(ph_free, at(b, PH_USES, use))

            def transposes(b, ks):
                for k in ks:
                    n = x_index(b, k)
                    bank = pa[:, n % 2, :]
                    if n >= 2:
                        pe.wait_ge(pa_free[n % 2], n // 2)
                    for t in range(T):
                        if k == 0:
                            pe.wait_ge(xn_ok, at(b, T, t + 1))
                        last = nc.tensor.transpose(bank[:, tok(t)], xin[:, t, tok(k)], ident[:, :])
                    last.then_inc(pa_fill, 1)

            def x_ready(b):
                if isinstance(b, int) and b <= 1:
                    for n in (x_index(b, KD - 2), x_index(b, KD - 1)):
                        pe.wait_ge(pa_free[n % 2], n // 2 + 1)
                else:
                    pe.wait_ge(xT_loaded, at(b, 16, -16))

            def gates(b):
                bank = take_pa(b, U_GATE)
                for k in range(KD):
                    nc.tensor.matmul(bank, wgT[:, k, :, :].rearrange("p a r -> p (a r)"), xT[:, HI, :, k, :],
                                     start=(k == 0), stop=False, skip_group_check=True)
                    last = nc.tensor.matmul(bank[0:P // 2, :], wgT[:, k, HI, :], xT[:, LO, :, k, :],
                                            start=False, stop=(k == KD - 1), skip_group_check=True)
                last.then_inc(pa_fill, 1)

            def features(b, use, col):
                bank = take_pa(b, use)
                for k in range(KD):
                    for n, (ws, xs) in enumerate(PARTS):
                        last = nc.tensor.matmul(bank, wT[:, ws, k, col:col + P], xT[:, xs, :, k, :],
                                                start=(k == 0 and n == 0), stop=(k == KD - 1 and n == 2))
                last.then_inc(pa_fill, 1)

            def tokens(b, use, src, col):
                bank = take_pa(b, use)
                for k in range(KD):
                    for n, (xs, ws) in enumerate(PARTS):
                        last = nc.tensor.matmul(bank, src[:, xs, k, :], wT[:, ws, k, col:col + D],
                                                start=(k == 0 and n == 0), stop=(k == KD - 1 and n == 2))
                last.then_inc(pa_fill, 1)

            def gate_columns(b):
                take_ph(b, U_GT)
                pe.wait_ge(gate_act, at(b, 5, 5))
                for t in range(T):
                    last = nc.tensor.transpose(ph[:, 0, t * P:t * P + STACK], stack[:, tok(t)],
                                               ident[0:STACK, 0:STACK])
                last.then_inc(ph_fill, 1)

            def key_tokens(chunk, bank):
                for g in range(HG):
                    last = nc.tensor.transpose(bank[:, tok(g)], kT[:, g, tok(chunk)], ident[:, :])
                return last

            def key_tokens_first(b):
                for n in range(HG):
                    pe.wait_ge(pa_free[(U_K + n) % 2], pa_done(b, U_K + n))
                if not (isinstance(b, int) and b == 0):
                    pe.wait_ge(ps_free[0], at(b, PS_USES[0], 0))
                key_tokens(0, ps[:, 0, 0:QK])
                key_tokens(1, ps[:, 0, QK:2 * QK]).then_inc(ps_fill, 1)

            def key_tokens_last(b):
                key_tokens(2, take_pa(b, U_KLAST)).then_inc(pa_fill, 1)

            def outer(b, j):
                take_ph(b, U_U + j)
                if j == 2:
                    pe.wait_ge(pa_free[U_KLAST % 2], pa_done(b, U_KLAST))
                if j == 0:
                    pe.wait_ge(ps_free[0], at(b, PS_USES[0], 1))
                    for t in (T - 2, T - 1):
                        pe.wait_ge(pa_free[(U_V + t) % 2], pa_done(b, U_V + t))
                for g in range(HG):
                    last = nc.tensor.matmul(ph[:, g, 0:H4 * VA], ktok[:, j, tok(g)],
                                            vaug[:, j, g * H4:(g + 1) * H4, :], start=True, stop=True)
                last.then_inc(ph_fill, 1)

            def scores(b, n):
                if not (isinstance(b, int) and b == 0 and n == 1):
                    pe.wait_ge(ps_free[n % 2], ps_done(b, n) - 1)
                if n % HG == 0:
                    pe.wait_ge(kq_ok, at(b, H4, n // HG + 1))
                for j in range(T):
                    last = nc.tensor.matmul(ps[:, n % 2, tok(j)], kst[:, HEADS[n], tok(j)], qst(b)[:, HEADS[n], tok(j)],
                                            start=True, stop=True)
                last.then_inc(ps_fill, 1)

            def chunk_state(b, j):
                take_ph(b, U_H + j)
                if j == 0:
                    for n in range(2):
                        pe.wait_ge(ps_free[n], at(b, PS_USES[n], PS_USES[n]))
                if j == 1:
                    pe.wait_ge(qw_ok, at(b, 1, 1))
                    pe.wait_ge(ph_free, at(b, PH_USES, U_U + 1))
                if j >= 2:
                    pe.wait_ge(c_ok, at(b, T - 2, j - 1))
                if j > 0:
                    for g in range(HG):
                        nc.tensor.matmul(ph[:, g, 0:H4 * VA], qw[:, g, tok(j - 1)], cst[:, j - 1, g, :],
                                         start=True, stop=False, skip_group_check=True)

            def chunk_head(b, j, h):
                g, i = divmod(h, H4)
                last = nc.tensor.matmul(ph[:, g, i * VA:(i + 1) * VA], dec[:, h, tok(j)], vaug[:, j, h, :],
                                        start=(j == 0 and i == 0), stop=(i == H4 - 1), skip_group_check=True)
                if h == NH - 1:
                    last.then_inc(ph_fill, 1)

            def project(b, t):
                pe.wait_ge(hoT_loaded[t], at(b, 16, 16))
                tokens(b, U_Y + t, hoT[:, t, :, :, :], C_OUT)

            def transposes2(fb, ks):
                for k in ks:
                    bank = take_pf(fb, U_T2 + k)
                    for t in range(T):
                        if k == 0:
                            pe.wait_ge(xn2_ok, at(fb, T, t + 1))
                        last = nc.tensor.transpose(bank[:, tok(t)], xres[:, t, tok(k)], ident[:, :])
                    last.then_inc(pf_fill, 1)

            def up(fb, f):
                bank = take_pf(fb, U_F1 + f)
                for k in range(KD):
                    if f == 0 and isinstance(fb, int) and fb == B - 1:
                        pe.wait_ge(pf_free[(U_T2 + k) % 2], pf_done(fb, U_T2 + k))
                    elif f == 0 and k == 0:
                        pe.wait_ge(x2T_loaded, at(fb, 16, 16))
                    for part in (HI, LO):
                        last = nc.tensor.matmul(bank, w1T[:, k, tok(f)], x2T[:, part, :, k, :],
                                                start=(k == 0 and part == HI), stop=(k == KD - 1 and part == LO))
                last.then_inc(pf_fill, 1)

            def down(fb, t, fs, b=None, j=None):
                bank = take_pf(fb, U_F2 + t) if fs[0] == 0 else pf[:, (U_F2 + t) % 2, :]
                if j is not None:
                    chunk_state(b, j)
                for f in fs:
                    if t == 0 and (f % 4 == 0 or f >= NF - 4):
                        pe.wait_ge(gs_ok, at(fb, NF, max(f + 1, min(f + 4, NF - 4))))
                    for part in (HI, LO):
                        last = nc.tensor.matmul(bank, gT[:, part, f, tok(t)], w2T[:, f, :],
                                                start=(f == 0 and part == HI), stop=(f == NF - 1 and part == LO),
                                                skip_group_check=True)
                        if f == NF - 1 and part == LO:
                            last.then_inc(pf_fill, 1)
                        if j is not None:
                            chunk_head(b, j, 2 * (f - fs[0]) + part)

            QUARTERS = [range(NF // 4 * i, NF // 4 * (i + 1)) for i in range(4)]

            def sequence(b, fb, ahead):
                def hidden(*fs):
                    if fb is not None:
                        for f in fs:
                            up(fb, f)

                def model(t, *quarters):
                    if fb is not None:
                        for q in quarters:
                            down(fb, t, QUARTERS[q])

                def chunk(j, t, q):
                    if fb is not None:
                        down(fb, t, QUARTERS[q], b, j)
                    else:
                        chunk_state(b, j)
                        for h in range(NH):
                            chunk_head(b, j, h)

                first = fb is None

                def prepare(*uses):
                    if first:
                        weights(*uses)

                if first:
                    weights_ready(USE_GATE)
                gates(b)
                prepare(*USES_QK[0:2])
                if first:
                    weights_ready(*USES_V)
                for t in range(T):
                    tokens(b, U_V + t, xT[:, :, t, :, :], C_V)
                    prepare(*USES_QK[t + 2:t + 3])
                prepare(*USES_O[0:2])
                if first:
                    weights_ready(*USES_QK)
                for n in range(HG):
                    features(b, U_K + n, C_QK + QK + n * P)
                    prepare(USES_O[n + 2])
                gate_columns(b)
                for n in range(HG):
                    features(b, U_Q + n, C_QK + n * P)
                if first:
                    weights_ready(*USES_O)
                key_tokens_first(b)
                for n in range(T):
                    tokens(b, U_O + n, xT[:, :, n, :, :], C_O)
                key_tokens_last(b)
                outer(b, 0)
                hidden(0, 1)
                scores(b, 0)
                for n in range(NH):
                    if n != 1:
                        scores(b, max(n, 1))
                    if first:
                        ternary_transpose(n)
                    hidden(2 + n)
                def between(q, *uses):
                    if first:
                        ternary2_transpose(q)
                        weights(*uses)

                def transpose_next(*ks):
                    if first:
                        transposes(b + 1, ks)

                outer(b, 1)
                hidden(10, 11, 12)
                between(0)
                outer(b, 2)
                hidden(13, 14, 15)
                between(1)
                model(0, 0)
                chunk(0, 0, 1)
                prepare(*USES_OUT[0:2])
                transpose_next(0, 1)
                model(0, 2, 3)
                chunk(1, 1, 0)
                model(1, 1, 2)
                between(2, *USES_OUT[2:4])
                chunk(2, 1, 3)
                transpose_next(2, 3)
                model(2, 0, 1)
                chunk(3, 2, 2)
                model(2, 3)
                between(3)
                if first:
                    weights_ready(*USES_OUT)
                project(b, 0)
                model(3, 0, 1)
                between(4)
                project(b, 1)
                model(3, 2, 3)
                between(5)
                project(b, 2)
                between(6)
                between(7)
                project(b, 3)
                if ahead:
                    x_ready(b + 1)

            weights(*USES_V)
            transposes(0, range(KD))
            weights(USE_GATE)
            x_ready(0)
            sequence(0, None, True)
            with pe.Fori(1, B - 1) as b:
                sequence(b, b - 1, True)
            sequence(B - 1, B - 2, False)
            transposes2(B - 1, range(KD))
            for f in range(NF):
                up(B - 1, f)
            for t in range(T):
                down(B - 1, t, range(NF))


_INS = ["x", "Wq", "Wk", "Wv", "Wog", "Wig", "big", "Wfg", "bfg", "gamma", "Wout"]
_FFN = ["w1", "b1", "w2", "b2"]


def kernel(**inputs):
    import numpy as np
    import concourse.bacc as bacc
    from concourse.bass_utils import run_bass_kernel_spmd

    nc = bacc.Bacc("TRN2", target_bir_lowering=False, num_devices=1)
    arrays, args = {}, []
    for name in [f"L0_attn_{n}" for n in _INS] + [f"L0_ffn_{n}" for n in _FFN]:
        a = np.ascontiguousarray(inputs[name])
        arrays[name] = a
        args.append(nc.dram_tensor(name, a.shape, mybir.dt.from_np(a.dtype), kind="ExternalInput").ap())
    shape = inputs["L0_attn_x"].shape
    out = nc.dram_tensor("out", shape, F32, kind="ExternalOutput").ap()
    block_program(nc, *args, out)
    return run_bass_kernel_spmd(nc, [arrays], core_ids=[0]).results[0]["out"]
```
